# Optimizing a Trainium2 kernel written in Bass

```python
import numpy as np
import jax
import jax.numpy as jnp

def _softmax(x, axis=-1):
    return jax.nn.softmax(x, axis=axis)

def _gelu(x):
    return jax.nn.gelu(x, approximate=True)

def _silu(x):
    return jax.nn.silu(x)

def _sigmoid(x):
    return jax.nn.sigmoid(x)

def _layernorm(x, axis=-1, eps=1e-05):
    m = jnp.mean(x, axis=axis, keepdims=True)
    v = jnp.var(x, axis=axis, keepdims=True)
    return (x - m) / jnp.sqrt(v + eps)

def _scatter_add(tgt, idx, src, axis=0):
    return tgt.at[idx].add(src)

def _segment_sum(src, seg, n):
    return jax.ops.segment_sum(src, seg, n)
kernel_name = 'mk_gnn_ffn_d2_gnn_r8_702994'

def setup_inputs(seed: int=0):
    np.random.seed(seed)
    _w = jnp.asarray

    def _rec_inputs():
        import jax
        import jax.numpy as jnp
        _gk = jax.random.key(seed)
        x = -0.0003019 + 1 * jax.random.normal(jax.random.fold_in(_gk, 1), (1250, 1024), jnp.float32)
        src = jax.random.randint(jax.random.fold_in(_gk, 2), (20000,), 0, 1250, jnp.int32)
        dst = jax.random.randint(jax.random.fold_in(_gk, 3), (20000,), 0, 1250, jnp.int32)
        _o = jnp.argsort(dst, stable=True)
        src = src[_o]
        dst = dst[_o]
        return (x, src, dst)
    x, src, dst = _rec_inputs()

    def _L0_gnn_setup():
        import jax, jax.numpy as jnp
        import numpy as np
        N = 2500
        E = 40000
        D_IN = 1024
        D_OUT = 1024
        key = jax.random.key(seed)
        k1, k2, k3, k4 = jax.random.split(key, 4)
        x = jax.random.normal(k1, (N, D_IN), dtype=jnp.float32)
        edge_index = jax.random.randint(k2, (2, E), 0, N, dtype=jnp.int64)
        W = jax.random.normal(k3, (D_OUT, D_IN), dtype=jnp.float32) * (1.0 / np.sqrt(D_IN))
        b = jax.random.normal(k4, (D_OUT,), dtype=jnp.float32) * 0.01
        return {'x': x, 'edge_index': edge_index, 'W': W, 'b': b}
    _L0_gnn_all = _L0_gnn_setup()
    _L0_gnn_in = {k: v for k, v in _L0_gnn_all.items() if k in ('W', 'b')}
    del _L0_gnn_all

    def _L0_ffn_setup():
        import jax, jax.numpy as jnp
        import numpy as np
        NUM_EXPERTS = 8
        TOP_K = 2
        key = jax.random.key(seed)
        ks = jax.random.split(key, 6)
        B, S, D, F = (2, 256, 1024, 512)
        E = NUM_EXPERTS
        sd = 1.0 / np.sqrt(D)
        sf = 1.0 / np.sqrt(F)
        return {'x': jax.random.normal(ks[0], (B, S, D), dtype=jnp.float32), 'gate_w': jax.random.normal(ks[1], (E, D), dtype=jnp.float32) * sd, 'w1': jax.random.uniform(ks[2], (F, E, D), dtype=jnp.float32, minval=-sd, maxval=sd), 'b1': jax.random.uniform(ks[3], (E, F), dtype=jnp.float32, minval=-sd, maxval=sd), 'w2': jax.random.uniform(ks[4], (D, E, F), dtype=jnp.float32, minval=-sf, maxval=sf), 'b2': jax.random.uniform(ks[5], (E, D), dtype=jnp.float32, minval=-sf, maxval=sf)}
    _L0_ffn_all = _L0_ffn_setup()
    _L0_ffn_in = {k: v for k, v in _L0_ffn_all.items() if k in ('gate_w', 'w1', 'b1', 'w2', 'b2')}
    del _L0_ffn_all

    def _L1_gnn_setup():
        import jax, jax.numpy as jnp
        import numpy as np
        N_NODES = 3125
        N_EDGES = 50000
        D = 1024

        def _sage_layer(h, edge_src, edge_dst, deg_inv, W_self, W_neigh, b):
            msg = h[edge_src]
            agg = jax.ops.segment_sum(msg, edge_dst, num_segments=h.shape[0])
            mean = agg * deg_inv[:, None]
            return h @ W_self + mean @ W_neigh + b
        key = jax.random.key(seed)
        ks = jax.random.split(key, 8)
        s = 1.0 / np.sqrt(D)
        return {'x': jax.random.normal(ks[0], (N_NODES, D), dtype=jnp.float32), 'edge_src': jax.random.randint(ks[1], (N_EDGES,), 0, N_NODES, dtype=jnp.int32), 'edge_dst': jax.random.randint(ks[2], (N_EDGES,), 0, N_NODES, dtype=jnp.int32), 'W_self0': jax.random.normal(ks[3], (D, D), dtype=jnp.float32) * s, 'W_neigh0': jax.random.normal(ks[4], (D, D), dtype=jnp.float32) * s, 'b0': jnp.zeros((D,), dtype=jnp.float32), 'W_self1': jax.random.normal(ks[5], (D, D), dtype=jnp.float32) * s, 'W_neigh1': jax.random.normal(ks[6], (D, D), dtype=jnp.float32) * s, 'b1': jnp.zeros((D,), dtype=jnp.float32)}
    _L1_gnn_all = _L1_gnn_setup()
    _L1_gnn_in = {k: v for k, v in _L1_gnn_all.items() if k in ('W_self0', 'W_neigh0', 'b0', 'W_self1', 'W_neigh1', 'b1')}
    del _L1_gnn_all

    def _L1_ffn_setup():
        import jax, jax.numpy as jnp
        import numpy as np
        HIDDEN = 1024
        INNER = 512

        def _weight_quant(w):
            scale = 1.0 / jnp.clip(jnp.mean(jnp.abs(w)), 1e-05)
            wq = jnp.clip(jnp.round(w * scale), -1.0, 1.0) / scale
            return w + jax.lax.stop_gradient(wq - w)

        def _act_quant(x):
            scale = 127.0 / jnp.clip(jnp.max(jnp.abs(x), axis=-1, keepdims=True), 1e-05)
            xq = jnp.clip(jnp.round(x * scale), -128.0, 127.0) / scale
            return x + jax.lax.stop_gradient(xq - x)

        def _bitlinear(x, w):
            return jnp.einsum('bsi,oi->bso', _act_quant(x), _weight_quant(w))
        key = jax.random.key(seed)
        k0, k1, k2, k3 = jax.random.split(key, 4)
        x = jax.random.normal(k0, (4, 256, HIDDEN), dtype=jnp.float32)
        w_gate = jax.random.normal(k1, (INNER, HIDDEN), dtype=jnp.float32) / np.sqrt(HIDDEN)
        w_up = jax.random.normal(k2, (INNER, HIDDEN), dtype=jnp.float32) / np.sqrt(HIDDEN)
        w_down = jax.random.normal(k3, (HIDDEN, INNER), dtype=jnp.float32) / np.sqrt(INNER)
        return {'x': x, 'w_gate': w_gate, 'w_up': w_up, 'w_down': w_down}
    _L1_ffn_all = _L1_ffn_setup()
    _L1_ffn_in = {k: v for k, v in _L1_ffn_all.items() if k in ('w_gate', 'w_up', 'w_down')}
    del _L1_ffn_all
    return {'x': x, 'src': src, 'dst': dst, 'L0_gnn_W': _L0_gnn_in['W'], 'L0_gnn_b': _L0_gnn_in['b'], 'L0_ffn_gate_w': _L0_ffn_in['gate_w'], 'L0_ffn_w1': _L0_ffn_in['w1'], 'L0_ffn_b1': _L0_ffn_in['b1'], 'L0_ffn_w2': _L0_ffn_in['w2'], 'L0_ffn_b2': _L0_ffn_in['b2'], 'L1_gnn_W_self0': _L1_gnn_in['W_self0'], 'L1_gnn_W_neigh0': _L1_gnn_in['W_neigh0'], 'L1_gnn_b0': _L1_gnn_in['b0'], 'L1_gnn_W_self1': _L1_gnn_in['W_self1'], 'L1_gnn_W_neigh1': _L1_gnn_in['W_neigh1'], 'L1_gnn_b1': _L1_gnn_in['b1'], 'L1_ffn_w_gate': _L1_ffn_in['w_gate'], 'L1_ffn_w_up': _L1_ffn_in['w_up'], 'L1_ffn_w_down': _L1_ffn_in['w_down']}

def reference(x, src, dst, L0_gnn_W, L0_gnn_b, L0_ffn_gate_w, L0_ffn_w1, L0_ffn_b1, L0_ffn_w2, L0_ffn_b2, L1_gnn_W_self0, L1_gnn_W_neigh0, L1_gnn_b0, L1_gnn_W_self1, L1_gnn_W_neigh1, L1_gnn_b1, L1_ffn_w_gate, L1_ffn_w_up, L1_ffn_w_down):
    import jax
    import jax.numpy as jnp

    def _L0_gnn_ref(x, edge_index, W, b):
        import jax, jax.numpy as jnp
        import numpy as np
        N = 2500
        E = 40000
        D_IN = 1024
        D_OUT = 1024
        num_nodes = x.shape[0]
        self_idx = jnp.arange(num_nodes, dtype=edge_index.dtype)
        ei = jnp.concatenate([edge_index, jnp.stack([self_idx, self_idx], axis=0)], axis=1)
        row, col = (ei[0], ei[1])
        h = jnp.einsum('nd,od->no', x, W) + b
        deg = jnp.zeros((num_nodes,), dtype=h.dtype).at[row].add(1.0)
        deg_inv_sqrt = deg ** (-0.5)
        norm = deg_inv_sqrt[row] * deg_inv_sqrt[col]
        msg = norm[:, None] * h[col]
        out = jax.ops.segment_sum(msg, row, num_segments=num_nodes)
        return out

    def _L0_ffn_ref(x, gate_w, w1, b1, w2, b2):
        import jax, jax.numpy as jnp
        import numpy as np
        NUM_EXPERTS = 8
        TOP_K = 2
        logits = jnp.einsum('bsd,ed->bse', x, gate_w)
        probs = jax.nn.softmax(logits, axis=-1)
        topk_probs, topk_idx = jax.lax.top_k(probs, TOP_K)
        oh = jax.nn.one_hot(topk_idx, NUM_EXPERTS, dtype=x.dtype)
        h = jnp.einsum('bsd,fed,bske->bskf', x, w1, oh)
        h = h + jnp.take(b1, topk_idx, axis=0)
        h = jax.nn.gelu(h)
        y = jnp.einsum('bskf,def,bske->bskd', h, w2, oh)
        y = y + jnp.take(b2, topk_idx, axis=0)
        out = jnp.sum(y * topk_probs[..., None], axis=-2)
        return out

    def _L1_gnn_ref(x, edge_src, edge_dst, W_self0, W_neigh0, b0, W_self1, W_neigh1, b1):
        import jax, jax.numpy as jnp
        import numpy as np
        N_NODES = 3125
        N_EDGES = 50000
        D = 1024

        def _sage_layer(h, edge_src, edge_dst, deg_inv, W_self, W_neigh, b):
            msg = h[edge_src]
            agg = jax.ops.segment_sum(msg, edge_dst, num_segments=h.shape[0])
            mean = agg * deg_inv[:, None]
            return h @ W_self + mean @ W_neigh + b
        N = x.shape[0]
        deg = jax.ops.segment_sum(jnp.ones_like(edge_dst, dtype=x.dtype), edge_dst, num_segments=N)
        deg_inv = 1.0 / jnp.maximum(deg, 1.0)
        h = jax.nn.relu(_sage_layer(x, edge_src, edge_dst, deg_inv, W_self0, W_neigh0, b0))
        out = _sage_layer(h, edge_src, edge_dst, deg_inv, W_self1, W_neigh1, b1)
        return out

    def _L1_ffn_ref(x, w_gate, w_up, w_down):
        import jax, jax.numpy as jnp
        import numpy as np
        HIDDEN = 1024
        INNER = 512

        def _weight_quant(w):
            scale = 1.0 / jnp.clip(jnp.mean(jnp.abs(w)), 1e-05)
            wq = jnp.clip(jnp.round(w * scale), -1.0, 1.0) / scale
            return w + jax.lax.stop_gradient(wq - w)

        def _act_quant(x):
            scale = 127.0 / jnp.clip(jnp.max(jnp.abs(x), axis=-1, keepdims=True), 1e-05)
            xq = jnp.clip(jnp.round(x * scale), -128.0, 127.0) / scale
            return x + jax.lax.stop_gradient(xq - x)

        def _bitlinear(x, w):
            return jnp.einsum('bsi,oi->bso', _act_quant(x), _weight_quant(w))
        gate = jax.nn.silu(_bitlinear(x, w_gate))
        up = _bitlinear(x, w_up)
        return _bitlinear(gate * up, w_down)
    edge_index = jnp.stack([src, dst])
    x = x + _L0_gnn_ref(_layernorm(x, axis=-1), edge_index, L0_gnn_W, L0_gnn_b)
    x = x + _L0_ffn_ref(_layernorm(x, axis=-1)[None], L0_ffn_gate_w, L0_ffn_w1, L0_ffn_b1, L0_ffn_w2, L0_ffn_b2)[0]
    x = x + _L1_gnn_ref(_layernorm(x, axis=-1), src, dst, L1_gnn_W_self0, L1_gnn_W_neigh0, L1_gnn_b0, L1_gnn_W_self1, L1_gnn_W_neigh1, L1_gnn_b1)
    x = x + _L1_ffn_ref(_layernorm(x, axis=-1)[None], L1_ffn_w_gate, L1_ffn_w_up, L1_ffn_w_down)[0]
    return x

_drawn_inputs = setup_inputs


def setup_inputs(seed=0):
    import zlib

    import numpy as np

    out = dict(_drawn_inputs(seed))
    spreads = {'L1_gnn_b0': (0.0, 0.1), 'L1_gnn_b1': (0.0, 0.1)}
    factors = {'L0_gnn_b': 4.563, 'L0_ffn_b1': 8.0, 'L0_ffn_b2': 4.831}
    for name, (base, spread) in spreads.items():
        noise = np.random.default_rng([zlib.crc32(name.encode()), seed]).standard_normal(out[name].shape)
        drawn = base * np.exp(spread * noise) if base else spread * noise
        out[name] = jnp.asarray(drawn.astype(out[name].dtype))
    for name, factor in factors.items():
        out[name] = (out[name] * factor).astype(out[name].dtype)
    return out
```

```python
from contextlib import ExitStack

import concourse.bass as bass
from concourse import mybir

P = 128
F32 = mybir.dt.float32
F16 = mybir.dt.float16
I32 = mybir.dt.int32
ALU = mybir.AluOpType
ACT = mybir.ActivationFunctionType
AX_X = mybir.AxisListType.X

NODES, D = 1250, 1024
EDGES = 20000
NT = -(-NODES // P)
NP = NT * P
LAST = NODES - (NT - 1) * P
CH = -(-EDGES // P)
KD = D // P
STEP = 4
CHP = CH + STEP - 1
TURNS = -(-CH // STEP)
NOWHERE = 2047
HALF = 512
COLS = [(0, 512), (512, 512), (1024, 256)]
EPS = 1e-5
MAGIC = 12582912.0
AS = 8.0
WS = 64.0


def gnn_ffn_kernel(nc, x, src, dst, l0_w, l0_b, gate, w1, b1, w2, b2, s0, n0, c0, s1, n1, c1, wg, wu, wd, out, stop):
    ctx = ExitStack()
    with ctx:
        def sb(name, shape, dt, c=ctx):
            return c.enter_context(nc.sbuf_tensor(name, shape, dt))

        held = []

        def sem(name):
            held.append(nc.alloc_semaphore(name))
            return held[-1]

        def end_phase():
            nc.clear_and_free_semaphores(held)
            nc.all_engine_barrier()
            held.clear()

        X = sb("X", [P, NT, D], F32)
        BIG = sb("BIG", [P, 61440], F16)
        FEAT = BIG[:, 0:40960].rearrange("p (k h n) -> p k h n", k=16, h=2)
        N = BIG[:, 40960:61440].rearrange("p (j h d) -> p j h d", j=NT, h=2)
        B0 = BIG[:, 0:NT * NP].rearrange("p (t n) -> p t n", t=NT)
        B1 = sb("B1", [P, NT, NP], F16)
        ident = sb("ident", [P, P], F16)
        ident32 = sb("ident32", [P, P], F32)
        ones32 = sb("ones32", [P, P], F32)
        bn = sb("bn", [P, NT, 2, 6], F32)
        mv = sb("mv", [P, NT, 2], F32)
        rstd = sb("rstd", [P, NT], F32)
        shift = sb("shift", [P, NT], F32)
        pw = sb("pw", [P, NT], F32)
        indeg = sb("indeg", [P, NT], F32)
        outdeg = sb("outdeg", [P, NT], F32)
        dinv = sb("dinv", [P, NT], F32)
        dinv8 = sb("dinv8", [P, NT], F32)
        degi = sb("degi", [P, NT], F32)
        bsum = sb("bsum", [P, NT], F32)
        chosen = sb("chosen", [P, NT, 8], F32)

        qmax = sb("qmax", [P, NT], F32)
        qscale = sb("qscale", [P, NT], F32)
        early = ctx.enter_context(ExitStack())
        rowscale = sb("rowscale", [P, NP], F32, early)

        with ExitStack() as pctx:
            n32 = BIG[:, 20480:40960].bitcast(F32).rearrange("p (j d) -> p j d", j=NT)
            tmp = BIG[:, 12800:20480]
            iota = tmp[:, 0:1280]
            hot_src = tmp[:, 1280:6400].rearrange("p (s n) -> p s n", s=STEP)
            hot_dst = tmp[:, 6400:6912].rearrange("p (s n) -> p s n", s=STEP)
            edges_i = tmp[:, 6912:6912 + 4 * CHP].bitcast(I32).rearrange("p (a c) -> p a c", a=2)
            zero = N[:, 1, 0, 0:HALF]
            edges = sb("edges", [P, 2, CHP], F32, pctx)
            above = N[:, 0:1, :, :].rearrange("p j h d -> p (j h d)")[:, 0:11 * CH].rearrange("p (t c) -> p t c", t=11)
            band = sb("band", [P, 24], F16, pctx)
            chunk_lo = sb("chunk_lo", [P, CH], F32, pctx)
            chunk_hi = sb("chunk_hi", [P, CH], F32, pctx)
            pick = sb("pick", [NT, 2, CH], F32, pctx)
            span = sb("span", [NT, 2], F32, pctx)
            span_i = sb("span_i", [NT, 2], I32, pctx)
            cnt = pctx.enter_context(nc.psum_tensor("cnt", [P, 2, 3 * HALF], F32))
            there = pctx.enter_context(nc.psum_tensor("there", [P, 2, HALF], F32))

            flip = cnt[:, :, 0:640].bitcast(F16)
            diag = tmp[:, 0:2560].bitcast(F32).rearrange("p (j n) -> p j n", j=NT)

            e_in = sem("e_in")
            x_in = sem("x_in")
            x_pad = sem("x_pad")
            consts = sem("consts")
            edges_f = sem("edges_f")
            above_ok = sem("above_ok")
            there_ok = sem("there_ok")
            picked = sem("picked")
            span_ok = sem("span_ok")
            flipped = sem("flipped")
            flip_free = sem("flip_free")
            deg_ok = sem("deg_ok")
            dinv_ok = sem("dinv_ok")
            scaled = sem("scaled")
            diag_ok = sem("diag_ok")
            spread = sem("spread")
            hi_ok = sem("hi_ok")
            lo_ok = sem("lo_ok")
            looped = sem("looped")
            row_ok = sem("row_ok")
            hot = sem("hot")
            hot_used = sem("hot_used")
            cnt_full = sem("cnt_full")
            cnt_free = sem("cnt_free")
            stats = sem("stats")
            moments = sem("moments")
            root = sem("root")
            n32_ok = sem("n32_ok")

            with nc.Block() as block:
                @block.sync
                def _(sp):
                    sp.dma_start(edges_i[:, 0, :], src).then_inc(e_in, 16)
                    sp.dma_start(edges_i[:, 1, :], dst).then_inc(e_in, 16)
                    sp.dma_start(X[:, 0:NT - 1, :], x[0:(NT - 1) * P, :].rearrange("(j p) d -> p j d", p=P)).then_inc(x_in, 16)
                    sp.wait_ge(x_pad, 1)
                    sp.dma_start(X[0:LAST, NT - 1, :], x[(NT - 1) * P:NODES, :]).then_inc(x_in, 16)

                @block.gpsimd
                def _(pool):
                    pool.iota(iota, [[1, NP]], base=0, channel_multiplier=0, allow_small_or_imprecise_dtypes=True).then_inc(hot_used, STEP)
                    pool.memset(band[:, :], 0.0).then_inc(consts, 1)
                    pool.memset(zero, 0.0).then_inc(consts, 1)
                    pool.iota(chunk_lo[:, :], [[1, CH]], base=-CH, channel_multiplier=0, allow_small_or_imprecise_dtypes=True).then_inc(consts, 1)
                    pool.iota(chunk_hi[:, :], [[1, CH]], base=1, channel_multiplier=0, allow_small_or_imprecise_dtypes=True).then_inc(consts, 1)
                    pool.wait_ge(consts, 1)
                    pool.memset(band[:, 10:11], -1.0).then_inc(consts, 1)
                    pool.memset(band[:, 11:12], 1.0).then_inc(consts, 1)
                    pool.memset(pw[:, :], -0.5).then_inc(consts, 1)
                    pool.memset(ident[:, :], 0.0).then_inc(consts, 1)
                    pool.memset(ident32[:, :], 0.0).then_inc(consts, 1)
                    pool.memset(ones32[:, :], 1.0).then_inc(consts, 1)
                    pool.wait_ge(consts, 10)
                    for m in (ident, ident32):
                        pool.affine_select(out=m[:, :], in_=m[:, :], compare_op=ALU.not_equal, fill=1.0,
                                           base=0, pattern=[[-1, P]], channel_multiplier=1).then_inc(consts, 1)
                    for j in range(NT):
                        pool.wait_ge(moments, j + 1)
                        pool.tensor_scalar(rstd[:, j:j + 1], mv[:, j, 1:2], 1.0, EPS, ALU.mult, ALU.add).then_inc(root, 1)
                        pool.tensor_scalar(shift[:, j:j + 1], mv[:, j, 0:1], -1.0, 0.0, ALU.mult, ALU.add).then_inc(root, 1)
                        pool.wait_ge(root, 4 * j + 2)
                        pool.tensor_tensor(rstd[:, j:j + 1], rstd[:, j:j + 1], pw[:, j:j + 1], ALU.pow).then_inc(root, 1)
                        pool.wait_ge(root, 4 * j + 3)
                        pool.tensor_tensor(shift[:, j:j + 1], shift[:, j:j + 1], rstd[:, j:j + 1], ALU.mult).then_inc(root, 1)
                    pool.wait_ge(deg_ok, 1)
                    pool.tensor_tensor(dinv[:, :], dinv[:, :], pw[:, :], ALU.pow).then_inc(dinv_ok, 1)

                @block.scalar
                def _(act):
                    for t in range(NT):
                        act.wait_ge(cnt_full, t + 1)
                        act.activation(B0[:, t, :], cnt[:, t % 2, 0:NP], ACT.Copy, accum_out=indeg[:, t:t + 1]).then_inc(cnt_free, 1)
                        act.wait_ge(root, 4 * t + 4)
                        act.activation(n32[:, t, :], X[:, t, :], ACT.Identity, bias=shift[:, t:t + 1],
                                       scale=rstd[:, t:t + 1]).then_inc(n32_ok, 1)
                    for j in range(NT):
                        act.wait_ge(flipped, j + 1)
                        act.activation(B1[:, j, :], flip[:, j % 2, 0:NP], ACT.Copy, accum_out=outdeg[:, j:j + 1]).then_inc(flip_free, 1)
                    act.wait_ge(scaled, 1)
                    act.wait_ge(n32_ok, NT)
                    for j in range(NT):
                        act.activation(N[:, j, 0, :], n32[:, j, :], ACT.Copy, scale=dinv8[:, j:j + 1]).then_inc(hi_ok, 1)
                    act.wait_ge(spread, 1)
                    act.activation(rowscale[:, :], cnt[:, 0, 0:NP], ACT.Copy).then_inc(row_ok, 1)

                @block.tensor
                def _(pe):
                    pe.wait_ge(consts, 6)
                    for t in range(NT + 1):
                        pe.wait_ge(above_ok, t + 1)
                        mm = pe.matmul(there[0:NT, 0, 0:CH], band[:, 11 - t:11 - t + NT], above[:, t, :],
                                       start=(t == 0), stop=(t == NT))
                    mm.then_inc(there_ok, 1)
                    pe.wait_ge(span_ok, 1)
                    done = 0
                    for t in range(NT):
                        n = pe.value_load(span_i[t:t + 1, 1:2], min_val=1, max_val=TURNS)
                        if t >= 2:
                            pe.wait_ge(cnt_free, t - 1)
                        for c, w in COLS:
                            pe.matmul(cnt[:, t % 2, c:c + w], zero[:, 0:P], zero[:, 0:w], start=True, stop=False)
                        with pe.Fori(done, done + n) as turn:
                            for u in range(STEP):
                                pe.wait_ge(hot, STEP * turn + u + 1)
                                for c, w in COLS:
                                    mm = pe.matmul(cnt[:, t % 2, c:c + w], hot_dst[:, u, :], hot_src[:, u, c:c + w], start=False, stop=False)
                                mm.then_inc(hot_used, 1)
                        for c, w in COLS:
                            mm = pe.matmul(cnt[:, t % 2, c:c + w], zero[:, 0:P], zero[:, 0:w], start=False, stop=True)
                        mm.then_inc(cnt_full, 1)
                        done = pe.snap(done + n)

                    pe.wait_ge(cnt_free, NT)
                    pe.wait_ge(consts, 12)
                    for j in range(NT):
                        if j >= 2:
                            pe.wait_ge(flip_free, j - 1)
                        for t in range(NT):
                            mm = pe.transpose(flip[:, j % 2, t * P:(t + 1) * P], B0[:, t, j * P:(j + 1) * P], ident[:, :])
                        mm.then_inc(flipped, 1)
                    pe.wait_ge(diag_ok, NT)
                    pe.wait_ge(flip_free, NT)
                    dg = diag.rearrange("p j n -> p (j n)")
                    for c, w in COLS:
                        mm = pe.matmul(cnt[:, 0, c:c + w], ones32[:, :], dg[:, c:c + w], start=True, stop=True)
                    mm.then_inc(spread, 1)

                @block.vector
                def _(dve):
                    dve.memset(X[96:P, NT - 1, :], 0.0).then_inc(x_pad, 1)
                    dve.wait_ge(e_in, 32)
                    dve.tensor_copy(edges[:, :, :], edges_i).then_inc(edges_f, 1)
                    dve.wait_ge(edges_f, 1)
                    for t in range(NT + 1):
                        dve.tensor_scalar(above[:, t, :], edges[:, 1, 0:CH], float(P * t), None, ALU.is_ge).then_inc(above_ok, 1)
                    dve.wait_ge(there_ok, 1)
                    dve.wait_ge(consts, 4)
                    dve.scalar_tensor_tensor(pick[:, 0, :], there[0:NT, 0, 0:CH], 0.0, chunk_lo[0:NT, :], ALU.is_gt, ALU.mult).then_inc(picked, 1)
                    dve.scalar_tensor_tensor(pick[:, 1, :], there[0:NT, 0, 0:CH], 0.0, chunk_hi[0:NT, :], ALU.is_gt, ALU.mult).then_inc(picked, 1)
                    dve.wait_ge(picked, 2)
                    dve.tensor_reduce(span[:, 0:1], pick[:, 0, :], AX_X, ALU.min).then_inc(picked, 1)
                    dve.tensor_reduce(span[:, 1:2], pick[:, 1, :], AX_X, ALU.max).then_inc(picked, 1)
                    dve.wait_ge(picked, 4)
                    dve.tensor_scalar(span[:, 0:1], span[:, 0:1], float(CH), float(CH - 1), ALU.add, ALU.min).then_inc(picked, 1)
                    dve.wait_ge(picked, 5)
                    dve.scalar_tensor_tensor(span[:, 1:2], span[:, 0:1], -1.0, span[:, 1:2], ALU.mult, ALU.add).then_inc(picked, 1)
                    dve.wait_ge(picked, 6)
                    dve.tensor_scalar(span[:, 1:2], span[:, 1:2], 1.0, 1 / STEP, ALU.max, ALU.mult).then_inc(picked, 1)
                    dve.wait_ge(picked, 7)
                    dve.tensor_scalar(span[:, 1:2], span[:, 1:2], 0.375, MAGIC, ALU.add, ALU.add).then_inc(picked, 1)
                    dve.wait_ge(picked, 8)
                    dve.tensor_scalar(span[:, 1:2], span[:, 1:2], MAGIC, None, ALU.subtract).then_inc(picked, 1)
                    dve.wait_ge(picked, 9)
                    dve.tensor_copy(span_i[:, :], span[:, :]).then_inc(span_ok, 1)
                    dve.wait_ge(span_ok, 1)
                    dve.wait_ge(x_in, 32)
                    done = 0
                    for t in range(NT):
                        lo = dve.value_load(span_i[t:t + 1, 0:1], min_val=0, max_val=CH - 1)
                        n = dve.value_load(span_i[t:t + 1, 1:2], min_val=1, max_val=TURNS)
                        back = dve.snap(lo - STEP * done)
                        with dve.Fori(done, done + n) as turn:
                            first = nc.s_assert_within(dve.snap(STEP * turn + back), 0, CH - 1, skip_runtime_bounds_check_because="the turns of a tile start in its span of chunks")
                            for u in range(STEP):
                                dve.wait_ge(hot_used, STEP * turn + u + 1)
                                dve.tensor_scalar(hot_dst[:, u, :], iota[:, t * P:(t + 1) * P], edges[:, 1, bass.ds(first + u, 1)], None, ALU.is_equal)
                                dve.tensor_scalar(hot_src[:, u, :], iota, edges[:, 0, bass.ds(first + u, 1)], None, ALU.is_equal).then_inc(hot, 1)
                        for h in range(2):
                            dve.bn_stats(bn[:, t, h, :], X[:, t, h * HALF:(h + 1) * HALF]).then_inc(stats, 1)
                        dve.wait_ge(stats, 2 * t + 2)
                        dve.bn_aggr(mv[:, t, :], bn[:, t, :, :]).then_inc(moments, 1)
                        done = dve.snap(done + n)
                    dve.wait_ge(flip_free, NT)
                    dve.tensor_scalar(dinv[:, :], outdeg[:, :], 1.0, None, ALU.add).then_inc(deg_ok, 1)
                    dve.wait_ge(dinv_ok, 1)
                    dve.tensor_scalar(dinv8[:, :], dinv[:, :], AS, None, ALU.mult).then_inc(scaled, 1)
                    for j in range(NT):
                        dve.tensor_scalar(diag[:, j, :], ident32[:, :], dinv[:, j:j + 1], None, ALU.mult).then_inc(diag_ok, 1)
                    dve.wait_ge(scaled, 1)
                    for j in range(NT):
                        own = B0[:, j, j * P:(j + 1) * P]
                        dve.tensor_tensor(own, own, ident[:, :], ALU.add).then_inc(looped, 1)
                        dve.wait_ge(hi_ok, j + 1)
                        dve.scalar_tensor_tensor(N[:, j, 1, :], n32[:, j, :], dinv8[:, j:j + 1], N[:, j, 0, :], ALU.mult, ALU.subtract).then_inc(lo_ok, 1)


        end_phase()

        def gather(tag, last_scale):
            with ExitStack() as c:
                counts = B0 if tag == "l0" else B1
                acc = c.enter_context(nc.psum_tensor(f"acc_{tag}", [P, 2, 3 * HALF], F32))
                if tag == "l0":
                    t32 = BIG[:, 12800:17920].bitcast(F32).rearrange("p (s n) -> p s n", s=2)
                else:
                    t32 = sb(f"t32_{tag}", [P, 2, NP], F32, c)
                summed = sem(f"summed_{tag}")
                scaled_ok, hi_w, lo_w = sem(f"scaled_{tag}"), sem(f"hi_w_{tag}"), sem(f"lo_w_{tag}")
                if tag == "l0":
                    bias_in, bsum_ok, bias_ok = sem("bias_in"), sem("bsum_ok"), sem("bias_ok")
                brow = BIG[:, 17920:19968].bitcast(F32)
                rs = rowscale if tag == "l0" else sb(f"rowscale_{tag}", [P, NP], F32, c)
                diag = None if tag == "l0" else t32[:, 0, :].rearrange("p (j n) -> p j n", j=NT)
                if tag != "l0":
                    deg_ok, diag_ok, spread, row_ok = (sem(f"{n}_{tag}") for n in ("degree_ok", "diag_ok", "spread", "row_ok"))
                junk = sb(f"junk_{tag}", [P, NP], F32, c) if tag == "l0" else None
                with nc.Block() as block:
                    @block.tensor
                    def _(pe):
                        if tag != "l0":
                            pe.wait_ge(diag_ok, NT)
                            for c_, w in COLS:
                                mm = pe.matmul(acc[:, 0, c_:c_ + w], ones32[:, :], t32[:, 0, c_:c_ + w], start=True, stop=True)
                            mm.then_inc(spread, 1)
                            pe.wait_ge(row_ok, 1)
                        with pe.Fori(0, KD // 2) as g:
                            for s in range(2):
                                pe.wait_ge(scaled_ok, 2 * g + s + 1)
                                f = (2 * g + s) * P
                                for j in range(NT):
                                    for h in range(2):
                                        for c_, w in COLS:
                                            mm = pe.matmul(acc[:, s, c_:c_ + w], N[:, j, h, bass.ds(f, P)], counts[:, j, c_:c_ + w],
                                                           start=(j == 0 and h == 0), stop=(j == NT - 1 and h == 1))
                                mm.then_inc(summed, 1)

                    @block.scalar
                    def _(act):
                        if tag != "l0":
                            act.wait_ge(spread, 1)
                            act.activation(rs[:, :], acc[:, 0, 0:NP], ACT.Copy).then_inc(row_ok, 1)
                        with act.Fori(0, KD // 2) as g:
                            for s in range(2):
                                act.wait_ge(scaled_ok, 2 * g + s + 3)
                                act.activation(FEAT[:, bass.ds(8 + 2 * g + s, 1), 0, :], t32[:, s:s + 1, :], ACT.Copy).then_inc(hi_w, 1)

                    @block.vector
                    def _(dve):
                        dve.sem_inc(scaled_ok, 2)
                        if tag == "l0":
                            for j in range(NT):
                                if j:
                                    dve.wait_ge(bsum_ok, j)
                                dve.tensor_tensor_reduce(junk[:, :], B1[:, j, :], rowscale[:, :], 1.0, 0.0, ALU.mult, ALU.add,
                                                         bsum[:, j:j + 1]).then_inc(bsum_ok, 1)
                            dve.wait_ge(bsum_ok, NT)
                            dve.tensor_tensor(bsum[:, :], bsum[:, :], dinv[:, :], ALU.add).then_inc(bsum_ok, 1)
                            dve.wait_ge(bsum_ok, NT + 1)
                            dve.tensor_tensor(bsum[:, :], bsum[:, :], dinv[:, :], ALU.mult).then_inc(bsum_ok, 1)
                            dve.wait_ge(bsum_ok, NT + 2)
                            dve.wait_ge(bias_in, 16)
                            for j in range(NT):
                                dve.scalar_tensor_tensor(X[:, j, :], brow, bsum[:, j:j + 1], X[:, j, :], ALU.mult, ALU.add).then_inc(bias_ok, 1)
                        else:
                            dve.tensor_scalar(degi[:, :], indeg[:, :], 1.0, None, ALU.max).then_inc(deg_ok, 1)
                            dve.wait_ge(deg_ok, 1)
                            dve.reciprocal(degi[:, :], degi[:, :]).then_inc(deg_ok, 1)
                            dve.wait_ge(deg_ok, 2)
                            for j in range(NT):
                                dve.tensor_scalar(diag[:, j, :], ident32[:, :], degi[:, j:j + 1], None, ALU.mult).then_inc(diag_ok, 1)
                            dve.wait_ge(row_ok, 1)
                        with dve.Fori(0, KD // 2) as g:
                            for s in range(2):
                                dve.wait_ge(summed, 2 * g + s + 1)
                                dve.wait_ge(lo_w, 2 * g + s)
                                dve.tensor_tensor(t32[:, s, :], acc[:, s, 0:NP], rs[:, :], ALU.mult).then_inc(scaled_ok, 1)
                                dve.wait_ge(hi_w, 2 * g + s + 1)
                                dve.tensor_tensor(FEAT[:, bass.ds(8 + 2 * g + s, 1), 1, :], t32[:, s:s + 1, :],
                                                  FEAT[:, bass.ds(8 + 2 * g + s, 1), 0, :], ALU.subtract).then_inc(lo_w, 1)

                    if tag == "l0":
                        @block.sync
                        def _(sp):
                            sp.dma_start(brow, l0_b.partition_broadcast(P)).then_inc(bias_in, 16)

        def project(tag, mats, k0, bias, hidden):
            K = KD * len(mats)
            Q = K // 4
            with ExitStack() as c:
                stage = sb(f"stage_{tag}", [P, 4, HALF], F32, c)
                wr = sb(f"wr_{tag}", [P, 4, 2, HALF], F16, c)
                if bias is not None:
                    bst = sb(f"bst_{tag}", [64, D], F16, c)
                    one = sb(f"one_{tag}", [64, P], F16, c)
                    b32 = stage[0:1, 0:2, :].rearrange("p a n -> p (a n)")
                ps = c.enter_context(nc.psum_tensor(f"ps_{tag}", [P, 8, HALF], F32))
                w_in = [sem(f"w_in{r}_{tag}") for r in range(4)]
                w_hi, w_lo, w_used = sem(f"w_hi_{tag}"), sem(f"w_lo_{tag}"), sem(f"w_used_{tag}")
                out_ok, out_free = sem(f"out_ok_{tag}"), sem(f"out_free_{tag}")
                if hidden:
                    h_ok, l_ok = sem(f"h_ok_{tag}"), sem(f"l_ok_{tag}")
                if bias is not None:
                    b_in, b_ok = sem(f"b_in_{tag}"), sem(f"b_ok_{tag}")
                bank = [[0, 1, 2, 3, 4], [5, 6, 7, 0, 1]]
                with nc.Block() as block:
                    @block.sync
                    def _(sp):
                        if bias is not None:
                            sp.dma_start(b32, bias.rearrange("(a d) -> a d", a=1)).then_inc(b_in, 16)
                            sp.wait_ge(b_ok, 3)
                        for s in range(4):
                            for m, w in enumerate(mats):
                                with sp.Fori(0, 2) as q:
                                    for r in range(4):
                                        n = (s * len(mats) + m) * 8 + q * 4 + r
                                        sp.wait_ge(w_lo, n + 1)
                                        sp.dma_start(stage[:, r, :], w[bass.ds((q * 4 + r) * P, P), (s % 2) * HALF:(s % 2 + 1) * HALF]).then_inc(w_in[r], 16)

                    @block.scalar
                    def _(act):
                        if bias is not None:
                            act.wait_ge(b_in, 16)
                            act.wait_ge(b_ok, 1)
                            act.activation(bst[0:1, :], b32, ACT.Copy, scale=AS * WS).then_inc(b_ok, 1)

                        def hi(s, q, r):
                            n = s * K + q * 4 + r
                            act.wait_ge(w_in[r], 16 * (s * Q + q + 1))
                            if not isinstance(q, int) or q:
                                act.wait_ge(w_used, n - 3 - s)
                            elif s and r < 3:
                                act.wait_ge(w_used, n - 2 - s)
                            elif s:
                                act.wait_ge(out_ok, 5 * s)
                            act.activation(wr[:, r, 0, :], stage[:, r, :], ACT.Copy, scale=WS).then_inc(w_hi, 1)

                        def evac(s):
                            if hidden:
                                for i in range(5):
                                    j, h = 5 * (s // 2) + i, s % 2
                                    act.wait_ge(l_ok, 5 * s + i + 1)
                                    act.activation(N[:, j, 0, h * HALF:(h + 1) * HALF], ps[:, bank[h][i], :], ACT.Copy).then_inc(h_ok, 1)

                        for s in range(4):
                            for r in range(4):
                                hi(s, 0, r)
                            if s:
                                evac(s - 1)
                            with act.Fori(1, Q) as q:
                                for r in range(4):
                                    hi(s, q, r)
                        evac(3)

                    @block.vector
                    def _(dve):
                        dve.sem_inc(w_lo, 4)
                        dve.sem_inc(out_free, 10)
                        if bias is not None:
                            dve.memset(bst[:, :], 0.0).then_inc(b_ok, 1)
                            dve.wait_ge(b_ok, 2)
                            dve.scalar_tensor_tensor(bst[32:33, :], b32, AS * WS, bst[0:1, :], ALU.mult, ALU.subtract).then_inc(b_ok, 1)
                            dve.memset(one[:, :], 1.0).then_inc(b_ok, 1)

                        def lo(s, q, r):
                            n = s * K + q * 4 + r
                            dve.wait_ge(w_hi, n + 1)
                            dve.scalar_tensor_tensor(wr[:, r, 1, :], stage[:, r, :], WS, wr[:, r, 0, :], ALU.mult, ALU.subtract).then_inc(w_lo, 1)

                        def evac(s):
                            for i in range(5):
                                j, h, u = 5 * (s // 2) + i, s % 2, 5 * s + i
                                cols = slice(h * HALF, (h + 1) * HALF)
                                dve.wait_ge(out_ok, u + 1)
                                if hidden:
                                    o = ps[:, bank[h][i], :]
                                    dve.tensor_scalar(o, o, 1 / WS, 0.0, ALU.mult, ALU.max).then_inc(l_ok, 1)
                                    dve.wait_ge(h_ok, u + 1)
                                    dve.tensor_tensor(N[:, j, 1, cols], o, N[:, j, 0, cols], ALU.subtract).then_inc(out_free, 1)
                                else:
                                    dve.scalar_tensor_tensor(X[:, j, cols], ps[:, bank[h][i], :], 1 / (AS * WS), X[:, j, cols],
                                                             ALU.mult, ALU.add).then_inc(out_free, 1)

                        for s in range(4):
                            for r in range(4):
                                lo(s, 0, r)
                            if s:
                                evac(s - 1)
                            with dve.Fori(1, Q) as q:
                                for r in range(4):
                                    lo(s, q, r)
                        evac(3)

                    @block.tensor
                    def _(pe):
                        if bias is not None:
                            pe.wait_ge(b_ok, 4)
                        for s in range(4):
                            g, h = s // 2, s % 2
                            for k in range(K):
                                n = s * K + k
                                pe.wait_ge(w_lo, n + 1 + 4)
                                for i in range(5):
                                    o = ps[:, bank[h][i], :]
                                    if k == 0:
                                        ahead = (i + 9 if i < 2 else i + 1) if h == 0 else (i + 6 if i < 3 else i + 8)
                                        pe.wait_ge(out_free, 10 * g + ahead)
                                        if bias is not None:
                                            pe.matmul(o, one[:, :], bst[:, h * HALF:(h + 1) * HALF], start=True, stop=False)
                                    at = slice((5 * g + i) * P, (5 * g + i + 1) * P)
                                    for a, b in ((0, 0), (0, 1), (1, 0)):
                                        mm = pe.matmul(o, FEAT[:, k0 + k, a, at], wr[:, k % 4, b, :],
                                                       start=(k == 0 and bias is None and (a, b) == (0, 0)),
                                                       stop=(k == K - 1 and (a, b) == (1, 0)))
                                    if k == K - 1:
                                        mm.then_inc(out_ok, 1)
                                if k < K - 1:
                                    mm.then_inc(w_used, 1)

        def normalise(tag, quant):
            with ExitStack() as c:
                n32 = FEAT[:, 8:12, :, :].rearrange("p k h n -> p (k h n)")[:, 0:4096].bitcast(F32).rearrange("p (s d) -> p s d", s=2)
                ps = c.enter_context(nc.psum_tensor(f"tp_{tag}", [P, 4, 2 * HALF], F16))
                stats, moments, root, n32_ok, lo_ok, turned, out_hi = (
                    sem(f"{n}_{tag}") for n in "stats moments root n32_ok lo_ok turned out_hi".split())
                if quant:
                    quant_chain = sem(f"quant_chain_{tag}")
                else:
                    hi_ok, out_lo = sem(f"hi_ok_{tag}"), sem(f"out_lo_{tag}")
                with nc.Block() as block:
                    @block.gpsimd
                    def _(pool):
                        pool.sem_inc(out_hi, 2)
                        if not quant:
                            pool.sem_inc(out_lo, 2)
                        for j in range(NT):
                            pool.wait_ge(moments, j + 1)
                            pool.tensor_scalar(rstd[:, j:j + 1], mv[:, j, 1:2], 1.0, EPS, ALU.mult, ALU.add).then_inc(root, 1)
                            pool.tensor_scalar(shift[:, j:j + 1], mv[:, j, 0:1], -1.0, 0.0, ALU.mult, ALU.add).then_inc(root, 1)
                            pool.wait_ge(root, 5 * j + 2)
                            pool.tensor_tensor(rstd[:, j:j + 1], rstd[:, j:j + 1], pw[:, j:j + 1], ALU.pow).then_inc(root, 1)
                            pool.wait_ge(root, 5 * j + 3)
                            pool.tensor_scalar(rstd[:, j:j + 1], rstd[:, j:j + 1], 1.0 if quant else AS, 0.0, ALU.mult, ALU.add).then_inc(root, 1)
                            pool.wait_ge(root, 5 * j + 4)
                            pool.tensor_tensor(shift[:, j:j + 1], shift[:, j:j + 1], rstd[:, j:j + 1], ALU.mult).then_inc(root, 1)

                    @block.scalar
                    def _(act):
                        def step(j, before):
                            act.wait_ge(root, 5 * j + 5)
                            if j >= 2:
                                act.wait_ge(lo_ok, j - 1)
                            act.activation(n32[:, j % 2, :], X[:, j, :], ACT.Identity, bias=shift[:, j:j + 1],
                                           scale=rstd[:, j:j + 1]).then_inc(n32_ok, 1)
                            if not quant:
                                act.wait_ge(n32_ok, j + 1)
                                act.activation(N[:, j, 0, :], n32[:, j % 2, :], ACT.Copy).then_inc(hi_ok, 1)
                            if before:
                                put(j - 1)

                        def put(j):
                            at = FEAT[:, 0:8, 0, j * P:(j + 1) * P]
                            act.wait_ge(turned, (1 if quant else 2) * j + 1)
                            act.activation(at, ps[:, (2 * j) % 4, :].rearrange("p (k n) -> p k n", k=8), ACT.Copy).then_inc(out_hi, 1)

                        for j in range(NT):
                            step(j, j > 0)
                        put(NT - 1)

                    @block.tensor
                    def _(pe):
                        for j in range(NT):
                            pe.wait_ge(lo_ok, j + 1)
                            for h in range(1 if quant else 2):
                                pe.wait_ge(out_lo if h else out_hi, j + 1)
                                for k in range(KD):
                                    mm = pe.transpose(ps[:, (2 * j + h) % 4, k * P:(k + 1) * P], N[:, j, h, k * P:(k + 1) * P], ident[:, :])
                                mm.then_inc(turned, 1)

                    @block.vector
                    def _(dve):
                        def moment(j):
                            for h in range(2):
                                dve.bn_stats(bn[:, j, h, :], X[:, j, h * HALF:(h + 1) * HALF]).then_inc(stats, 1)
                            dve.wait_ge(stats, 2 * j + 2)
                            dve.bn_aggr(mv[:, j, :], bn[:, j, :, :]).then_inc(moments, 1)

                        def put(j):
                            at = FEAT[:, 0:8, 1, j * P:(j + 1) * P]
                            dve.wait_ge(turned, 2 * j + 2)
                            dve.tensor_copy(at, ps[:, (2 * j + 1) % 4, :].rearrange("p (k n) -> p k n", k=8)).then_inc(out_lo, 1)

                        moment(0)
                        for j in range(NT):
                            if j < NT - 1:
                                moment(j + 1)
                            if quant:
                                quantise(dve, n32[:, j % 2, :], n32_ok, j + 1, qmax[:, j:j + 1], qscale[:, j:j + 1], N[:, j, 0, :], quant_chain, 4 * j, lo_ok)
                            else:
                                dve.wait_ge(hi_ok, j + 1)
                                dve.tensor_tensor(N[:, j, 1, :], n32[:, j % 2, :], N[:, j, 0, :], ALU.subtract).then_inc(lo_ok, 1)
                                if j:
                                    put(j - 1)
                        if not quant:
                            put(NT - 1)

        def quantise(dve, v, v_ok, count, vmax, vscale, whole, chain, n, done):
            dve.wait_ge(v_ok, count)
            dve.tensor_reduce(vmax, v, AX_X, ALU.max, apply_absolute_value=True).then_inc(chain, 1)
            dve.wait_ge(chain, n + 1)
            dve.tensor_scalar(vmax, vmax, 1e-5, 1 / 127.0, ALU.max, ALU.mult).then_inc(chain, 1)
            dve.wait_ge(chain, n + 2)
            dve.reciprocal(vscale, vmax).then_inc(chain, 1)
            dve.wait_ge(chain, n + 3)
            dve.tensor_scalar(v, v, vscale, MAGIC, ALU.mult, ALU.add).then_inc(chain, 1)
            dve.wait_ge(chain, n + 4)
            dve.tensor_scalar(whole, v, MAGIC, 127.0, ALU.subtract, ALU.min).then_inc(done, 1)

        def turn_hidden(tag):
            with ExitStack() as c:
                ps = c.enter_context(nc.psum_tensor(f"tp_{tag}", [P, 4, 2 * HALF], F16))
                turned, out_hi, out_lo = sem(f"turned_{tag}"), sem(f"out_hi_{tag}"), sem(f"out_lo_{tag}")
                with nc.Block() as block:
                    @block.tensor
                    def _(pe):
                        pe.sem_inc(out_hi, 2)
                        pe.sem_inc(out_lo, 2)
                        with pe.Fori(0, NT // 2) as g:
                            for s in range(2):
                                for h in range(2):
                                    pe.wait_ge(out_lo if h else out_hi, 2 * g + s + 1)
                                    for k in range(KD):
                                        mm = pe.transpose(ps[:, 2 * s + h, k * P:(k + 1) * P],
                                                          N[:, bass.ds(2 * g + s, 1), h, k * P:(k + 1) * P], ident[:, :])
                                    mm.then_inc(turned, 1)

                    @block.scalar
                    def _(act):
                        with act.Fori(0, NT // 2) as g:
                            for s in range(2):
                                act.wait_ge(turned, 4 * g + 2 * s + 1)
                                act.activation(FEAT[:, 0:8, 0, bass.ds((2 * g + s) * P, P)],
                                               ps[:, 2 * s, :].rearrange("p (k n) -> p k n", k=8), ACT.Copy).then_inc(out_hi, 1)

                    @block.vector
                    def _(dve):
                        with dve.Fori(0, NT // 2) as g:
                            for s in range(2):
                                dve.wait_ge(turned, 4 * g + 2 * s + 2)
                                dve.tensor_copy(FEAT[:, 0:8, 1, bass.ds((2 * g + s) * P, P)],
                                                ps[:, 2 * s + 1, :].rearrange("p (k n) -> p k n", k=8)).then_inc(out_lo, 1)

        def route():
            with ExitStack() as c:
                g32 = sb("g32", [P, KD, 8], F32, c)
                g2 = sb("g2", [P, KD, 2, 8], F16, c)
                both = sb("both", [P, NT, 2, 8], F32, c)
                logit = sb("logit", [P, NT, 8], F32, c)
                best = sb("best", [P, NT, 8], F32, c)
                where = sb("where", [P, NT, 8], mybir.dt.uint32, c)
                where_f = sb("where_f", [P, NT, 8], F32, c)
                mask = sb("mask", [P, NT, 8], F32, c)
                which = sb("which", [P, 8], F32, c)
                total = sb("total", [P, NT], F32, c)
                neg = sb("neg", [P, NT], F32, c)
                b2s = sb("b2s", [8, D], F32, c)
                byx = sb("byx", [8, NP], F32, c)
                pl = c.enter_context(nc.psum_tensor("pl", [P, 4, HALF], F32))
                pt = c.enter_context(nc.psum_tensor("pt", [P, 2, HALF], F32))
                py = c.enter_context(nc.psum_tensor("py", [P, 2, HALF], F32))
                r_in, r2_in, g_ok, w_ok, l_ok, c1, c2, c3, p_ok, x_ok, e_ok = (sem(f"route_{n}") for n in range(11))
                t_ok, b_ok, y_ok, y_free = (sem(f"routeb_{n}") for n in range(4))
                with nc.Block() as block:
                    @block.sync
                    def _(sp):
                        sp.dma_start(g32[:, :, :], gate.rearrange("(k p) e -> p k e", p=P)).then_inc(r_in, 16)
                        sp.dma_start(b2s[:, :], b2).then_inc(r2_in, 16)

                    @block.gpsimd
                    def _(pool):
                        pool.iota(which[:, :], [[1, 8]], base=0, channel_multiplier=0, allow_small_or_imprecise_dtypes=True).then_inc(w_ok, 1)

                    @block.scalar
                    def _(act):
                        act.wait_ge(r_in, 16)
                        act.activation(g2[:, :, 0, :], g32[:, :, :], ACT.Copy, scale=WS).then_inc(g_ok, 1)
                        act.wait_ge(c2, NT)
                        for j in range(NT):
                            act.activation(mask[:, j, :], logit[:, j, :], ACT.Exp, bias=neg[:, j:j + 1], accum_out=total[:, j:j + 1]).then_inc(e_ok, 1)
                        act.wait_ge(t_ok, NT)
                        act.activation(byx[:, 0:512], pt[0:8, 0, :], ACT.Copy).then_inc(b_ok, 1)
                        act.activation(byx[:, 512:1024], pt[0:8, 1, :], ACT.Copy).then_inc(b_ok, 1)
                        act.activation(byx[:, 1024:1280], pl[0:8, 3, 0:256], ACT.Copy).then_inc(b_ok, 1)

                    @block.tensor
                    def _(pe):
                        pe.wait_ge(g_ok, 2)
                        for j in range(NT):
                            o = pl[:, 0, 16 * j:16 * j + 16]
                            for k in range(KD):
                                pe.matmul(o, FEAT[:, k, 0, j * P:(j + 1) * P], g2[:, k, :, :].rearrange("p a e -> p (a e)"),
                                          start=(k == 0), stop=False)
                                mm = pe.matmul(o[:, 0:8], FEAT[:, k, 1, j * P:(j + 1) * P], g2[:, k, 0, :], start=False, stop=(k == KD - 1))
                            mm.then_inc(l_ok, 1)
                        pe.wait_ge(p_ok, 1)
                        for j in range(NT):
                            o = pt[0:8, j // 4, (j % 4) * P:(j % 4 + 1) * P] if j < 8 else pl[0:8, 3, (j - 8) * P:(j - 7) * P]
                            pe.transpose(o, chosen[:, j, :], ident32[:, :]).then_inc(t_ok, 1)
                        pe.wait_ge(r2_in, 16)
                        pe.wait_ge(b_ok, 3)
                        for j in range(NT):
                            for h in range(2):
                                pe.wait_ge(y_free, 2 * j + h + 1)
                                pe.matmul(py[:, h, :], byx[:, j * P:(j + 1) * P], b2s[:, h * HALF:(h + 1) * HALF], start=True, stop=True).then_inc(y_ok, 1)

                    @block.vector
                    def _(dve):
                        dve.sem_inc(y_free, 2)
                        dve.wait_ge(g_ok, 1)
                        dve.scalar_tensor_tensor(g2[:, :, 1, :], g32[:, :, :], WS, g2[:, :, 0, :], ALU.mult, ALU.subtract).then_inc(g_ok, 1)
                        dve.wait_ge(l_ok, NT)
                        dve.tensor_scalar(both[:, :, :, :].rearrange("p j a e -> p (j a e)"), pl[:, 0, 0:16 * NT], 1 / (AS * WS), None, ALU.mult).then_inc(c1, 1)
                        dve.wait_ge(c1, 1)
                        dve.tensor_tensor(logit[:, :, :], both[:, :, 0, :], both[:, :, 1, :], ALU.add).then_inc(c1, 1)
                        dve.wait_ge(c1, 2)
                        for j in range(NT):
                            dve.max(best[:, j, :], logit[:, j, :]).then_inc(c1, 1)
                        dve.wait_ge(c1, NT + 2)
                        for j in range(NT):
                            dve.tensor_scalar(neg[:, j:j + 1], best[:, j, 0:1], -1.0, None, ALU.mult).then_inc(c2, 1)
                            dve.max_index(where[:, j, :], best[:, j, :], logit[:, j, :]).then_inc(c3, 1)
                        dve.wait_ge(c3, NT)
                        dve.tensor_copy(where_f[:, :, :], where[:, :, :]).then_inc(c3, 1)
                        dve.wait_ge(c3, NT + 1)
                        dve.wait_ge(w_ok, 1)
                        dve.wait_ge(e_ok, NT)
                        for j in range(NT):
                            dve.tensor_scalar(both[:, j, 0, :], which[:, :], where_f[:, j, 0:1], None, ALU.is_equal).then_inc(x_ok, 1)
                            dve.tensor_scalar(both[:, j, 1, :], which[:, :], where_f[:, j, 1:2], None, ALU.is_equal).then_inc(x_ok, 1)
                        dve.reciprocal(total[:, :], total[:, :]).then_inc(x_ok, 1)
                        dve.wait_ge(x_ok, 2 * NT + 1)
                        dve.tensor_tensor(logit[:, :, :], both[:, :, 0, :], both[:, :, 1, :], ALU.add).then_inc(x_ok, 1)
                        dve.wait_ge(x_ok, 2 * NT + 2)
                        for j in range(NT):
                            last = dve.scalar_tensor_tensor(chosen[:, j, :], mask[:, j, :], total[:, j:j + 1], logit[:, j, :], ALU.mult, ALU.mult)
                        last.then_inc(p_ok, 1)
                        for j in range(NT):
                            for h in range(2):
                                cols = slice(h * HALF, (h + 1) * HALF)
                                dve.wait_ge(y_ok, 2 * j + h + 1)
                                dve.tensor_tensor(X[:, j, cols], py[:, h, :], X[:, j, cols], ALU.add).then_inc(y_free, 1)
                        dve.wait_ge(p_ok, 1)
                        dve.tensor_scalar(chosen[:, :, :], chosen[:, :, :], 1 / (AS * WS), None, ALU.mult).then_inc(p_ok, 1)

        def experts():
            with ExitStack() as c:
                WM = FEAT[:, 8:16, :, :].rearrange("p k h n -> p (k h n)")
                w1s = WM[:, 0:8192].rearrange("p (k h f) -> p k h f", k=8, h=2)
                w2s = WM[:, 8192:16384].rearrange("p (k h d) -> p k h d", k=8, h=2)
                NM = N.rearrange("p j h d -> p (j h d)")
                HT = NM[:, 0:4 * 2 * NP].rearrange("p (f h n) -> p f h n", f=4, h=2)
                stage = NM[:, 10240:10240 + 8192].bitcast(F32).rearrange("p (r n) -> p r n", r=8)
                g32 = sb("ge32", [P, 2, NP], F32, c)
                b1s = sb("b1s", [P, 8, 4], F32, c)
                pa = c.enter_context(nc.psum_tensor("pa", [P, 8, HALF], F32))
                SET = [4, 0]
                w_in = [sem(f"moe_in{r}") for r in range(8)]
                b_in = sem("moe_b_in")
                hi, lo, a_ok, a_free, hh, hl, y_ok, y_free = (sem(f"moe_{n}") for n in range(8))
                flat = pa[:, :, :].rearrange("p b n -> p (b n)")
                with nc.Block() as block:
                    @block.sync
                    def _(sp):
                        sp.dma_start(b1s[:, :, :], b1).then_inc(b_in, 16)

                        def first(e):
                            for k in range(8):
                                sp.wait_ge(lo, 16 * e + k + 1)
                                sp.dma_start(stage[:, k, :], w1[bass.ds(e * D + k * P, P), :]).then_inc(w_in[k], 16)

                        def second(e):
                            for k in range(8):
                                sp.wait_ge(lo, 16 * e + 8 + k + 1)
                                sp.dma_start(stage[:, k, :], w2[bass.ds(e * HALF + (k // 2) * P, P), (k % 2) * HALF:(k % 2 + 1) * HALF]).then_inc(w_in[k], 16)

                        with sp.Fori(0, 8) as e:
                            first(e)
                            second(e)

                    def hi_part(act, e, i):
                        k = i % 8
                        act.wait_ge(w_in[k], 32 * e + (16 if i < 8 else 32))
                        if i < 8:
                            act.wait_ge(a_ok, 4 * e)
                        else:
                            act.wait_ge(y_ok, NT * e)
                        dst = w1s if i < 8 else w2s
                        act.activation(dst[:, k, 0, :], stage[:, k, :], ACT.Copy, scale=WS).then_inc(hi, 1)

                    def lo_part(dve, e, i):
                        k = i % 8
                        dst = w1s if i < 8 else w2s
                        dve.wait_ge(hi, 16 * e + i + 1)
                        dve.scalar_tensor_tensor(dst[:, k, 1, :], stage[:, k, :], WS, dst[:, k, 0, :], ALU.mult, ALU.subtract).then_inc(lo, 1)

                    @block.scalar
                    def _(act):
                        act.wait_ge(b_in, 16)
                        for i in range(8):
                            hi_part(act, 0, i)

                        def expert(e, more):
                            for f in range(4):
                                n = 4 * e + f
                                act.wait_ge(a_ok, n + 1)
                                act.wait_ge(hl, n + 1)
                                act.activation(g32[:, f % 2, :], flat[:, SET[f % 2] * HALF:SET[f % 2] * HALF + NP], ACT.Gelu_apprx_tanh,
                                               bias=b1s[:, bass.ds(e, 1), f:f + 1].rearrange("p a b -> p (a b)"), scale=1 / (AS * WS)).then_inc(a_free, 1)
                                act.wait_ge(a_free, n + 1 + 2)
                                act.activation(HT[:, f, 0, :], g32[:, f % 2, :], ACT.Copy, scale=AS).then_inc(hh, 1)
                                for i in (2 * f, 2 * f + 1):
                                    hi_part(act, e, 8 + i)
                            if more:
                                for i in range(8):
                                    hi_part(act, e + 1, i)

                        with act.Fori(0, 7) as e:
                            expert(e, True)
                        expert(7, False)

                    @block.vector
                    def _(dve):
                        dve.sem_inc(lo, 8)
                        dve.sem_inc(hl, 2)
                        dve.sem_inc(a_free, 2)
                        dve.sem_inc(y_free, 4)
                        for i in range(8):
                            lo_part(dve, 0, i)

                        def expert(e, more):
                            for f in range(4):
                                n = 4 * e + f
                                dve.wait_ge(hh, n + 1)
                                dve.scalar_tensor_tensor(HT[:, f, 1, :], g32[:, f % 2, :], AS, HT[:, f, 0, :], ALU.mult, ALU.subtract).then_inc(hl, 1)
                                for i in (2 * f, 2 * f + 1):
                                    lo_part(dve, e, 8 + i)
                            for j in range(NT):
                                dve.wait_ge(y_ok, NT * e + j + 1)
                                pair = flat[:, (j % 4) * 2 * HALF:(j % 4 + 1) * 2 * HALF]
                                dve.scalar_tensor_tensor(X[:, j, :], pair, chosen[:, j, bass.ds(e, 1)],
                                                         X[:, j, :], ALU.mult, ALU.add).then_inc(y_free, 1)
                                if more and j < 8:
                                    lo_part(dve, e + 1, j)

                        with dve.Fori(0, 7) as e:
                            expert(e, True)
                        expert(7, False)

                    @block.tensor
                    def _(pe):
                        with pe.Fori(0, 8) as e:
                            for f in range(4):
                                if f < 2:
                                    pe.wait_ge(y_free, NT * e + (2 if f == 0 else 4))
                                pe.wait_ge(a_free, 4 * e + f + 1)
                                for k in range(KD):
                                    pe.wait_ge(lo, 16 * e + k + 1 + 8) if f == 0 else None
                                    for a, b in ((0, 0), (0, 1), (1, 0)):
                                        for c_, w in COLS:
                                            o = flat[:, SET[f % 2] * HALF + c_:SET[f % 2] * HALF + c_ + w]
                                            mm = pe.matmul(o, w1s[:, k, a, f * P:(f + 1) * P], FEAT[:, k, b, c_:c_ + w],
                                                           start=(k == 0 and (a, b) == (0, 0)), stop=(k == KD - 1 and (a, b) == (1, 0)))
                                mm.then_inc(a_ok, 1)
                            pe.wait_ge(hl, 4 * e + 4 + 2)
                            pe.wait_ge(lo, 16 * e + 16 + 8)
                            for j in range(NT):
                                if j >= 4:
                                    pe.wait_ge(y_free, NT * e + j + 1)
                                for k in range(4):
                                    for a, b in ((0, 0), (0, 1), (1, 0)):
                                        for h in range(2):
                                            o = flat[:, ((j % 4) * 2 + h) * HALF:((j % 4) * 2 + h + 1) * HALF]
                                            mm = pe.matmul(o, HT[:, k, a, j * P:(j + 1) * P], w2s[:, 2 * k + h, b, :],
                                                           start=(k == 0 and (a, b) == (0, 0)), stop=(k == 3 and (a, b) == (1, 0)))
                                mm.then_inc(y_ok, 1)

        def ternary_ffn():
            with ExitStack() as c:
                w32 = BIG[:, 20480:20480 + 24576].bitcast(F32).rearrange("p (m n) -> p m n", m=3)
                wt = B1[:, :, :].rearrange("p j n -> p (j n)")[:, 0:12288].rearrange("p (m n) -> p m n", m=3)
                wsum = sb("wsum", [P, 3], F32, c)
                wmean = sb("wmean", [P, 3], F32, c)
                wscale = sb("wscale", [P, 3], F32, c)
                gk = sb("gk", [P, 2, HALF], F32, c)
                gq = sb("gq", [P, 2, HALF], F16, c)
                gT = sb("gT", [P, 2, 4, P], F16, c)
                k_gate, k_up, vmax, vscale, k_down = (sb(f"ffn_{n}", [P, NT], F32, c) for n in range(5))
                pm = c.enter_context(nc.psum_tensor("pm", [P, HALF], F32))
                pg = c.enter_context(nc.psum_tensor("pg", [P, 2, HALF], F32))
                pu = c.enter_context(nc.psum_tensor("pu", [P, HALF], F32))
                ptr = c.enter_context(nc.psum_tensor("ptr", [P, 2, 2 * HALF], F16))
                pd = c.enter_context(nc.psum_tensor("pd", [P, 2, HALF], F32))
                m_in = [sem(f"ffn_in{m}") for m in range(3)]
                s_sum, s_all, s_mean, s_wt, g_ok, g_free, v_ok, q_ok, t_ok, t_out, d_ok, x_ok, chain, k_ok, chain2 = (sem(f"ffn{n}_s") for n in range(15))
                with nc.Block() as block:
                    @block.sync
                    def _(sp):
                        for m, w in enumerate((wg, wu, wd)):
                            K = w.shape[0] // P
                            sp.dma_start(w32[:, m, :].rearrange("p (k n) -> p k n", k=K), w.rearrange("(k p) n -> p k n", p=P)).then_inc(m_in[m], 16)

                    @block.scalar
                    def _(act):
                        for m in range(3):
                            act.wait_ge(m_in[m], 16)
                            act.activation(wt[:, m, :], w32[:, m, :], ACT.Abs, accum_out=wsum[:, m:m + 1]).then_inc(s_sum, 1)
                        for j in range(NT):
                            act.wait_ge(g_ok, j + 1)
                            act.wait_ge(k_ok, 2)
                            if j >= 2:
                                act.wait_ge(q_ok, j - 1)
                            act.activation(gk[:, j % 2, :], pg[:, 0, :], ACT.Silu, scale=k_gate[:, j:j + 1]).then_inc(g_free, 1)
                            act.wait_ge(t_ok, j + 1)
                            act.activation(gT[:, j % 2, :, :], ptr[:, j % 2, 0:HALF].rearrange("p (k n) -> p k n", k=4), ACT.Copy).then_inc(t_out, 1)

                    @block.tensor
                    def _(pe):
                        pe.wait_ge(s_sum, 3)
                        pe.matmul(pm[:, 0:3], ones32[:, :], wsum[:, :], start=True, stop=True).then_inc(s_all, 1)
                        pe.wait_ge(s_wt, 3)

                        def up(j):
                            if j:
                                pe.wait_ge(g_free, j)
                                pe.wait_ge(v_ok, j)
                            for m, o in ((0, pg[:, 0, :]), (1, pu[:, :])):
                                for k in range(KD):
                                    mm = pe.matmul(o, FEAT[:, k, 0, j * P:(j + 1) * P], wt[:, m, k * HALF:(k + 1) * HALF], start=(k == 0), stop=(k == KD - 1))
                            mm.then_inc(g_ok, 1)

                        def down(j):
                            pe.wait_ge(q_ok, j + 1)
                            for k in range(4):
                                mm = pe.transpose(ptr[:, j % 2, k * P:(k + 1) * P], gq[:, j % 2, k * P:(k + 1) * P], ident[:, :])
                            mm.then_inc(t_ok, 1)
                            pe.wait_ge(t_out, j + 1)
                            if j:
                                pe.wait_ge(x_ok, j)
                            for k in range(4):
                                for h in range(2):
                                    mm = pe.matmul(pd[:, h, :], gT[:, j % 2, k, :], wt[:, 2, k * D + h * HALF:k * D + (h + 1) * HALF], start=(k == 0), stop=(k == 3))
                            mm.then_inc(d_ok, 1)

                        for j in range(NT):
                            up(j)
                            if j:
                                down(j - 1)
                        down(NT - 1)

                    @block.vector
                    def _(dve):
                        dve.wait_ge(s_all, 1)
                        dve.tensor_scalar(wmean[:, :], pm[:, 0:3], 1.0 / (D * HALF), 1e-5, ALU.mult, ALU.max).then_inc(s_mean, 1)
                        dve.wait_ge(s_mean, 1)
                        dve.reciprocal(wscale[:, :], wmean[:, :]).then_inc(s_mean, 1)
                        dve.wait_ge(s_mean, 2)
                        for m in range(3):
                            dve.tensor_scalar(w32[:, m, :], w32[:, m, :], wscale[:, m:m + 1], MAGIC, ALU.mult, ALU.add).then_inc(chain, 1)
                            dve.wait_ge(chain, 2 * m + 1)
                            dve.tensor_scalar(w32[:, m, :], w32[:, m, :], MAGIC, -1.0, ALU.subtract, ALU.max).then_inc(chain, 1)
                            dve.wait_ge(chain, 2 * m + 2)
                            dve.tensor_scalar(wt[:, m, :], w32[:, m, :], 1.0, None, ALU.min).then_inc(s_wt, 1)
                        dve.tensor_scalar(k_gate[:, :], qmax[:, :], wmean[:, 0:1], None, ALU.mult).then_inc(k_ok, 1)
                        dve.tensor_scalar(k_up[:, :], qmax[:, :], wmean[:, 1:2], None, ALU.mult).then_inc(k_ok, 1)
                        dve.wait_ge(k_ok, 2)

                        def add(j):
                            dve.wait_ge(d_ok, j + 1)
                            dve.wait_ge(chain2, 5 * j + 5)
                            dve.scalar_tensor_tensor(X[:, j, :], pd[:, :, :].rearrange("p h n -> p (h n)"), k_down[:, j:j + 1],
                                                     X[:, j, :], ALU.mult, ALU.add).then_inc(x_ok, 1)

                        for j in range(NT):
                            v = gk[:, j % 2, :]
                            dve.wait_ge(g_free, j + 1)
                            dve.scalar_tensor_tensor(v, pu[:, :], k_up[:, j:j + 1], v, ALU.mult, ALU.mult).then_inc(v_ok, 1)
                            quantise(dve, v, v_ok, j + 1, vmax[:, j:j + 1], vscale[:, j:j + 1], gq[:, j % 2, :], chain2, 5 * j, q_ok)
                            dve.tensor_scalar(k_down[:, j:j + 1], vmax[:, j:j + 1], wmean[:, 2:3], None, ALU.mult).then_inc(chain2, 1)
                            if j:
                                add(j - 1)
                        add(NT - 1)

        gather("l0", None)
        end_phase()
        early.close()
        if stop > 2:
            project("l0", [l0_w], 8, None, False)
            end_phase()
        if stop > 3:
            normalise("m", False)
            end_phase()
            route()
            end_phase()
        if stop > 4:
            experts()
            end_phase()
        if stop > 5:
            normalise("s", False)
            end_phase()
            gather("s0", None)
            end_phase()
            project("s0", [s0, n0], 0, c0, True)
            end_phase()
            turn_hidden("h")
            end_phase()
            gather("s1", None)
            end_phase()
            project("s1", [s1, n1], 0, c1, False)
            end_phase()
        if stop > 6:
            normalise("f", True)
            end_phase()
            ternary_ffn()
            end_phase()

        x_out = sem("x_out")
        with nc.Block() as block:
            @block.sync
            def _(sp):
                sp.dma_start(out[0:(NT - 1) * P, :].rearrange("(j p) d -> p j d", p=P), X[:, 0:NT - 1, :]).then_inc(x_out, 16)
                sp.dma_start(out[(NT - 1) * P:NODES, :], X[0:LAST, NT - 1, :]).then_inc(x_out, 16)
                sp.wait_ge(x_out, 32)


def kernel(**inputs):
    import numpy as np
    import concourse.bacc as bacc
    from concourse.bass_utils import run_bass_kernel_spmd as run

    nc = bacc.Bacc("TRN2", target_bir_lowering=False, num_devices=1)

    def chunks(e):
        padded = np.full(CHP * P, NOWHERE, e.dtype)
        padded[:EDGES] = e
        return padded.reshape(CHP, P).T

    laid = {
        "x": inputs["x"], "src": chunks(np.asarray(inputs["src"])), "dst": chunks(np.asarray(inputs["dst"])),
        "l0_w": np.asarray(inputs["L0_gnn_W"]).T, "l0_b": inputs["L0_gnn_b"],
        "gate": np.asarray(inputs["L0_ffn_gate_w"]).T,
        "w1": np.asarray(inputs["L0_ffn_w1"]).transpose(1, 2, 0).reshape(8 * D, HALF),
        "b1": np.asarray(inputs["L0_ffn_b1"]).reshape(8, 4, P).transpose(2, 0, 1),
        "w2": np.asarray(inputs["L0_ffn_w2"]).transpose(1, 2, 0).reshape(8 * HALF, D),
        "b2": inputs["L0_ffn_b2"],
        "s0": inputs["L1_gnn_W_self0"], "n0": inputs["L1_gnn_W_neigh0"], "c0": inputs["L1_gnn_b0"],
        "s1": inputs["L1_gnn_W_self1"], "n1": inputs["L1_gnn_W_neigh1"], "c1": inputs["L1_gnn_b1"],
        "wg": np.asarray(inputs["L1_ffn_w_gate"]).T, "wu": np.asarray(inputs["L1_ffn_w_up"]).T,
        "wd": np.asarray(inputs["L1_ffn_w_down"]).T,
    }
    laid = {k: np.ascontiguousarray(v) for k, v in laid.items()}
    aps = {k: nc.dram_tensor(k, v.shape, mybir.dt.from_np(v.dtype), kind="ExternalInput").ap() for k, v in laid.items()}
    out = nc.dram_tensor("out", (NODES, D), F32, kind="ExternalOutput").ap()
    gnn_ffn_kernel(nc, **aps, out=out, stop=STOP)
    r = run(nc, [laid], core_ids=[0])
    return r.results[0]["out"]


STOP = 9
```

```python
from contextlib import ExitStack

import concourse.bass as bass
from concourse import mybir

P = 128
F32 = mybir.dt.float32
F16 = mybir.dt.float16
I32 = mybir.dt.int32
U32 = mybir.dt.uint32
ALU = mybir.AluOpType
ACT = mybir.ActivationFunctionType
AX_X = mybir.AxisListType.X

NODES, D = 1250, 1024
EDGES = 20000
NT = -(-NODES // P)
NP = NT * P
LAST = NODES - (NT - 1) * P
CH = -(-EDGES // P)
KD = D // P
STEP = 4
CHP = CH + STEP - 1
TURNS = -(-CH // STEP)
NOWHERE = 2047
ST = (2 * NODES + 8 * (P - 1)) // P
ST_LEAST = -(-2 * NODES // P)
HALF = 512
COLS = [(0, 512), (512, 512), (1024, 256)]
EPS = 1e-5
MAGIC = 12582912.0
AS = 8.0
WS = 64.0


def gnn_ffn_kernel(nc, x, src, dst, l0_w, l0_b, gate, w1, b1, w2, b2, s0, n0, c0, s1, n1, c1, wg, wu, wd, out, stop):
    ctx = ExitStack()
    with ctx:
        def sb(name, shape, dt, c=ctx):
            return c.enter_context(nc.sbuf_tensor(name, shape, dt))

        held = []

        def sem(name):
            held.append(nc.alloc_semaphore(name))
            return held[-1]

        def end_phase():
            nc.clear_and_free_semaphores(held)
            nc.all_engine_barrier()
            held.clear()

        X = sb("X", [P, NT, D], F32)
        BIG = sb("BIG", [P, 61440], F16)
        FEAT = BIG[:, 0:40960].rearrange("p (k h n) -> p k h n", k=16, h=2)
        N = BIG[:, 40960:61440].rearrange("p (j h d) -> p j h d", j=NT, h=2)
        B0 = BIG[:, 0:NT * NP].rearrange("p (t n) -> p t n", t=NT)
        B1 = sb("B1", [P, NT, NP], F16)
        ident = sb("ident", [P, P], F16)
        ident32 = sb("ident32", [P, P], F32)
        ones32 = sb("ones32", [P, P], F32)
        bn = sb("bn", [P, NT, 2, 6], F32)
        mv = sb("mv", [P, NT, 2], F32)
        rstd = sb("rstd", [P, NT], F32)
        shift = sb("shift", [P, NT], F32)
        pw = sb("pw", [P, NT], F32)
        indeg = sb("indeg", [P, NT], F32)
        outdeg = sb("outdeg", [P, NT], F32)
        dinv = sb("dinv", [P, NT], F32)
        dinv8 = sb("dinv8", [P, NT], F32)
        degi = sb("degi", [P, NT], F32)
        bsum = sb("bsum", [P, NT], F32)
        chosen = sb("chosen", [P, NT, 8], F32)

        qmax = sb("qmax", [P, NT], F32)
        qscale = sb("qscale", [P, NT], F32)
        weight = sb("weight", [P, 2, NT], F32)
        slot_i = sb("slot_i", [P, 2, NT], U32)
        node_i = sb("node_i", [P, ST + 1], U32)
        bounds_i = sb("bounds_i", [P, 9], I32)
        rows = nc.dram_tensor("rows", (NP, 2 * D), F16, kind="Internal").ap()
        results = nc.dram_tensor("results", (ST * P, D), F32, kind="Internal").ap()

        early = ctx.enter_context(ExitStack())
        rowscale = sb("rowscale", [P, NP], F32, early)

        with ExitStack() as pctx:
            n32 = BIG[:, 20480:40960].bitcast(F32).rearrange("p (j d) -> p j d", j=NT)
            tmp = BIG[:, 12800:20480]
            iota = tmp[:, 0:1280]
            hot_src = tmp[:, 1280:6400].rearrange("p (s n) -> p s n", s=STEP)
            hot_dst = tmp[:, 6400:6912].rearrange("p (s n) -> p s n", s=STEP)
            edges_i = tmp[:, 6912:6912 + 4 * CHP].bitcast(I32).rearrange("p (a c) -> p a c", a=2)
            zero = N[:, 1, 0, 0:HALF]
            edges = sb("edges", [P, 2, CHP], F32, pctx)
            above = N[:, 0:1, :, :].rearrange("p j h d -> p (j h d)")[:, 0:11 * CH].rearrange("p (t c) -> p t c", t=11)
            band = sb("band", [P, 24], F16, pctx)
            chunk_lo = sb("chunk_lo", [P, CH], F32, pctx)
            chunk_hi = sb("chunk_hi", [P, CH], F32, pctx)
            pick = sb("pick", [NT, 2, CH], F32, pctx)
            span = sb("span", [NT, 2], F32, pctx)
            span_i = sb("span_i", [NT, 2], I32, pctx)
            cnt = pctx.enter_context(nc.psum_tensor("cnt", [P, 2, 3 * HALF], F32))
            there = pctx.enter_context(nc.psum_tensor("there", [P, 2, HALF], F32))

            flip = cnt[:, :, 0:640].bitcast(F16)
            diag = tmp[:, 0:2560].bitcast(F32).rearrange("p (j n) -> p j n", j=NT)

            e_in = sem("e_in")
            x_in = sem("x_in")
            filled = sem("filled")
            x_pad = sem("x_pad")
            consts = sem("consts")
            edges_f = sem("edges_f")
            above_ok = sem("above_ok")
            there_ok = sem("there_ok")
            picked = sem("picked")
            span_ok = sem("span_ok")
            flipped = sem("flipped")
            flip_free = sem("flip_free")
            deg_ok = sem("deg_ok")
            dinv_ok = sem("dinv_ok")
            scaled = sem("scaled")
            diag_ok = sem("diag_ok")
            spread = sem("spread")
            hi_ok = sem("hi_ok")
            lo_ok = sem("lo_ok")
            looped = sem("looped")
            row_ok = sem("row_ok")
            hot = sem("hot")
            hot_used = sem("hot_used")
            cnt_full = sem("cnt_full")
            cnt_free = sem("cnt_free")
            stats = sem("stats")
            moments = sem("moments")
            root = sem("root")
            n32_ok = sem("n32_ok")

            with nc.Block() as block:
                @block.sync
                def _(sp):
                    sp.dma_start(edges_i[:, 0, :], src).then_inc(e_in, 16)
                    sp.dma_start(edges_i[:, 1, :], dst).then_inc(e_in, 16)
                    sp.dma_start(X[:, 0:NT - 1, :], x[0:(NT - 1) * P, :].rearrange("(j p) d -> p j d", p=P)).then_inc(x_in, 16)
                    sp.wait_ge(x_pad, 1)
                    sp.dma_start(X[0:LAST, NT - 1, :], x[(NT - 1) * P:NODES, :]).then_inc(x_in, 16)
                    sp.dma_start(results[ST_LEAST * P:ST * P, :], x[0:(ST - ST_LEAST) * P, :]).then_inc(filled, 16)
                    sp.wait_ge(filled, 16)

                @block.gpsimd
                def _(pool):
                    pool.iota(iota, [[1, NP]], base=0, channel_multiplier=0, allow_small_or_imprecise_dtypes=True).then_inc(hot_used, STEP)
                    pool.memset(band[:, :], 0.0).then_inc(consts, 1)
                    pool.memset(zero, 0.0).then_inc(consts, 1)
                    pool.iota(chunk_lo[:, :], [[1, CH]], base=-CH, channel_multiplier=0, allow_small_or_imprecise_dtypes=True).then_inc(consts, 1)
                    pool.iota(chunk_hi[:, :], [[1, CH]], base=1, channel_multiplier=0, allow_small_or_imprecise_dtypes=True).then_inc(consts, 1)
                    pool.wait_ge(consts, 1)
                    pool.memset(band[:, 10:11], -1.0).then_inc(consts, 1)
                    pool.memset(band[:, 11:12], 1.0).then_inc(consts, 1)
                    pool.memset(pw[:, :], -0.5).then_inc(consts, 1)
                    pool.memset(ident[:, :], 0.0).then_inc(consts, 1)
                    pool.memset(ident32[:, :], 0.0).then_inc(consts, 1)
                    pool.memset(ones32[:, :], 1.0).then_inc(consts, 1)
                    pool.wait_ge(consts, 10)
                    for m in (ident, ident32):
                        pool.affine_select(out=m[:, :], in_=m[:, :], compare_op=ALU.not_equal, fill=1.0,
                                           base=0, pattern=[[-1, P]], channel_multiplier=1).then_inc(consts, 1)
                    for j in range(NT):
                        pool.wait_ge(moments, j + 1)
                        pool.tensor_scalar(rstd[:, j:j + 1], mv[:, j, 1:2], 1.0, EPS, ALU.mult, ALU.add).then_inc(root, 1)
                        pool.tensor_scalar(shift[:, j:j + 1], mv[:, j, 0:1], -1.0, 0.0, ALU.mult, ALU.add).then_inc(root, 1)
                        pool.wait_ge(root, 4 * j + 2)
                        pool.tensor_tensor(rstd[:, j:j + 1], rstd[:, j:j + 1], pw[:, j:j + 1], ALU.pow).then_inc(root, 1)
                        pool.wait_ge(root, 4 * j + 3)
                        pool.tensor_tensor(shift[:, j:j + 1], shift[:, j:j + 1], rstd[:, j:j + 1], ALU.mult).then_inc(root, 1)
                    pool.wait_ge(deg_ok, 1)
                    pool.tensor_tensor(dinv[:, :], dinv[:, :], pw[:, :], ALU.pow).then_inc(dinv_ok, 1)

                @block.scalar
                def _(act):
                    for t in range(NT):
                        act.wait_ge(cnt_full, t + 1)
                        act.activation(B0[:, t, :], cnt[:, t % 2, 0:NP], ACT.Copy, accum_out=indeg[:, t:t + 1]).then_inc(cnt_free, 1)
                        act.wait_ge(root, 4 * t + 4)
                        act.activation(n32[:, t, :], X[:, t, :], ACT.Identity, bias=shift[:, t:t + 1],
                                       scale=rstd[:, t:t + 1]).then_inc(n32_ok, 1)
                    for j in range(NT):
                        act.wait_ge(flipped, j + 1)
                        act.activation(B1[:, j, :], flip[:, j % 2, 0:NP], ACT.Copy, accum_out=outdeg[:, j:j + 1]).then_inc(flip_free, 1)
                    act.wait_ge(scaled, 1)
                    act.wait_ge(n32_ok, NT)
                    for j in range(NT):
                        act.activation(N[:, j, 0, :], n32[:, j, :], ACT.Copy, scale=dinv8[:, j:j + 1]).then_inc(hi_ok, 1)
                    act.wait_ge(spread, 1)
                    act.activation(rowscale[:, :], cnt[:, 0, 0:NP], ACT.Copy).then_inc(row_ok, 1)

                @block.tensor
                def _(pe):
                    pe.wait_ge(consts, 6)
                    for t in range(NT + 1):
                        pe.wait_ge(above_ok, t + 1)
                        mm = pe.matmul(there[0:NT, 0, 0:CH], band[:, 11 - t:11 - t + NT], above[:, t, :],
                                       start=(t == 0), stop=(t == NT))
                    mm.then_inc(there_ok, 1)
                    pe.wait_ge(span_ok, 1)
                    done = 0
                    for t in range(NT):
                        n = pe.value_load(span_i[t:t + 1, 1:2], min_val=1, max_val=TURNS)
                        if t >= 2:
                            pe.wait_ge(cnt_free, t - 1)
                        for c, w in COLS:
                            pe.matmul(cnt[:, t % 2, c:c + w], zero[:, 0:P], zero[:, 0:w], start=True, stop=False)
                        with pe.Fori(done, done + n) as turn:
                            for u in range(STEP):
                                pe.wait_ge(hot, STEP * turn + u + 1)
                                for c, w in COLS:
                                    mm = pe.matmul(cnt[:, t % 2, c:c + w], hot_dst[:, u, :], hot_src[:, u, c:c + w], start=False, stop=False)
                                mm.then_inc(hot_used, 1)
                        for c, w in COLS:
                            mm = pe.matmul(cnt[:, t % 2, c:c + w], zero[:, 0:P], zero[:, 0:w], start=False, stop=True)
                        mm.then_inc(cnt_full, 1)
                        done = pe.snap(done + n)

                    pe.wait_ge(cnt_free, NT)
                    pe.wait_ge(consts, 12)
                    for j in range(NT):
                        if j >= 2:
                            pe.wait_ge(flip_free, j - 1)
                        for t in range(NT):
                            mm = pe.transpose(flip[:, j % 2, t * P:(t + 1) * P], B0[:, t, j * P:(j + 1) * P], ident[:, :])
                        mm.then_inc(flipped, 1)
                    pe.wait_ge(diag_ok, NT)
                    pe.wait_ge(flip_free, NT)
                    dg = diag.rearrange("p j n -> p (j n)")
                    for c, w in COLS:
                        mm = pe.matmul(cnt[:, 0, c:c + w], ones32[:, :], dg[:, c:c + w], start=True, stop=True)
                    mm.then_inc(spread, 1)

                @block.vector
                def _(dve):
                    dve.memset(X[96:P, NT - 1, :], 0.0).then_inc(x_pad, 1)
                    dve.wait_ge(e_in, 32)
                    dve.tensor_copy(edges[:, :, :], edges_i).then_inc(edges_f, 1)
                    dve.wait_ge(edges_f, 1)
                    for t in range(NT + 1):
                        dve.tensor_scalar(above[:, t, :], edges[:, 1, 0:CH], float(P * t), None, ALU.is_ge).then_inc(above_ok, 1)
                    dve.wait_ge(there_ok, 1)
                    dve.wait_ge(consts, 4)
                    dve.scalar_tensor_tensor(pick[:, 0, :], there[0:NT, 0, 0:CH], 0.0, chunk_lo[0:NT, :], ALU.is_gt, ALU.mult).then_inc(picked, 1)
                    dve.scalar_tensor_tensor(pick[:, 1, :], there[0:NT, 0, 0:CH], 0.0, chunk_hi[0:NT, :], ALU.is_gt, ALU.mult).then_inc(picked, 1)
                    dve.wait_ge(picked, 2)
                    dve.tensor_reduce(span[:, 0:1], pick[:, 0, :], AX_X, ALU.min).then_inc(picked, 1)
                    dve.tensor_reduce(span[:, 1:2], pick[:, 1, :], AX_X, ALU.max).then_inc(picked, 1)
                    dve.wait_ge(picked, 4)
                    dve.tensor_scalar(span[:, 0:1], span[:, 0:1], float(CH), float(CH - 1), ALU.add, ALU.min).then_inc(picked, 1)
                    dve.wait_ge(picked, 5)
                    dve.scalar_tensor_tensor(span[:, 1:2], span[:, 0:1], -1.0, span[:, 1:2], ALU.mult, ALU.add).then_inc(picked, 1)
                    dve.wait_ge(picked, 6)
                    dve.tensor_scalar(span[:, 1:2], span[:, 1:2], 1.0, 1 / STEP, ALU.max, ALU.mult).then_inc(picked, 1)
                    dve.wait_ge(picked, 7)
                    dve.tensor_scalar(span[:, 1:2], span[:, 1:2], 0.375, MAGIC, ALU.add, ALU.add).then_inc(picked, 1)
                    dve.wait_ge(picked, 8)
                    dve.tensor_scalar(span[:, 1:2], span[:, 1:2], MAGIC, None, ALU.subtract).then_inc(picked, 1)
                    dve.wait_ge(picked, 9)
                    dve.tensor_copy(span_i[:, :], span[:, :]).then_inc(span_ok, 1)
                    dve.wait_ge(span_ok, 1)
                    dve.wait_ge(x_in, 32)
                    done = 0
                    for t in range(NT):
                        lo = dve.value_load(span_i[t:t + 1, 0:1], min_val=0, max_val=CH - 1)
                        n = dve.value_load(span_i[t:t + 1, 1:2], min_val=1, max_val=TURNS)
                        back = dve.snap(lo - STEP * done)
                        with dve.Fori(done, done + n) as turn:
                            first = nc.s_assert_within(dve.snap(STEP * turn + back), 0, CH - 1, skip_runtime_bounds_check_because="the turns of a tile start in its span of chunks")
                            for u in range(STEP):
                                dve.wait_ge(hot_used, STEP * turn + u + 1)
                                dve.tensor_scalar(hot_dst[:, u, :], iota[:, t * P:(t + 1) * P], edges[:, 1, bass.ds(first + u, 1)], None, ALU.is_equal)
                                dve.tensor_scalar(hot_src[:, u, :], iota, edges[:, 0, bass.ds(first + u, 1)], None, ALU.is_equal).then_inc(hot, 1)
                        for h in range(2):
                            dve.bn_stats(bn[:, t, h, :], X[:, t, h * HALF:(h + 1) * HALF]).then_inc(stats, 1)
                        dve.wait_ge(stats, 2 * t + 2)
                        dve.bn_aggr(mv[:, t, :], bn[:, t, :, :]).then_inc(moments, 1)
                        done = dve.snap(done + n)
                    dve.wait_ge(flip_free, NT)
                    dve.tensor_scalar(dinv[:, :], outdeg[:, :], 1.0, None, ALU.add).then_inc(deg_ok, 1)
                    dve.wait_ge(dinv_ok, 1)
                    dve.tensor_scalar(dinv8[:, :], dinv[:, :], AS, None, ALU.mult).then_inc(scaled, 1)
                    for j in range(NT):
                        dve.tensor_scalar(diag[:, j, :], ident32[:, :], dinv[:, j:j + 1], None, ALU.mult).then_inc(diag_ok, 1)
                    dve.wait_ge(scaled, 1)
                    for j in range(NT):
                        own = B0[:, j, j * P:(j + 1) * P]
                        dve.tensor_tensor(own, own, ident[:, :], ALU.add).then_inc(looped, 1)
                        dve.wait_ge(hi_ok, j + 1)
                        dve.scalar_tensor_tensor(N[:, j, 1, :], n32[:, j, :], dinv8[:, j:j + 1], N[:, j, 0, :], ALU.mult, ALU.subtract).then_inc(lo_ok, 1)


        end_phase()

        def gather(tag, last_scale):
            with ExitStack() as c:
                counts = B0 if tag == "l0" else B1
                acc = c.enter_context(nc.psum_tensor(f"acc_{tag}", [P, 2, 3 * HALF], F32))
                if tag == "l0":
                    t32 = BIG[:, 12800:17920].bitcast(F32).rearrange("p (s n) -> p s n", s=2)
                else:
                    t32 = sb(f"t32_{tag}", [P, 2, NP], F32, c)
                summed = sem(f"summed_{tag}")
                scaled_ok, hi_w, lo_w = sem(f"scaled_{tag}"), sem(f"hi_w_{tag}"), sem(f"lo_w_{tag}")
                if tag == "l0":
                    bias_in, bsum_ok, bias_ok = sem("bias_in"), sem("bsum_ok"), sem("bias_ok")
                brow = BIG[:, 17920:19968].bitcast(F32)
                rs = rowscale if tag == "l0" else sb(f"rowscale_{tag}", [P, NP], F32, c)
                diag = None if tag == "l0" else t32[:, 0, :].rearrange("p (j n) -> p j n", j=NT)
                if tag != "l0":
                    deg_ok, diag_ok, spread, row_ok = (sem(f"{n}_{tag}") for n in ("degree_ok", "diag_ok", "spread", "row_ok"))
                junk = sb(f"junk_{tag}", [P, NP], F32, c) if tag == "l0" else None
                with nc.Block() as block:
                    @block.tensor
                    def _(pe):
                        if tag != "l0":
                            pe.wait_ge(diag_ok, NT)
                            for c_, w in COLS:
                                mm = pe.matmul(acc[:, 0, c_:c_ + w], ones32[:, :], t32[:, 0, c_:c_ + w], start=True, stop=True)
                            mm.then_inc(spread, 1)
                            pe.wait_ge(row_ok, 1)
                        with pe.Fori(0, KD // 2) as g:
                            for s in range(2):
                                pe.wait_ge(scaled_ok, 2 * g + s + 1)
                                f = (2 * g + s) * P
                                for j in range(NT):
                                    for h in range(2):
                                        for c_, w in COLS:
                                            mm = pe.matmul(acc[:, s, c_:c_ + w], N[:, j, h, bass.ds(f, P)], counts[:, j, c_:c_ + w],
                                                           start=(j == 0 and h == 0), stop=(j == NT - 1 and h == 1))
                                mm.then_inc(summed, 1)

                    @block.scalar
                    def _(act):
                        if tag != "l0":
                            act.wait_ge(spread, 1)
                            act.activation(rs[:, :], acc[:, 0, 0:NP], ACT.Copy).then_inc(row_ok, 1)
                        with act.Fori(0, KD // 2) as g:
                            for s in range(2):
                                act.wait_ge(scaled_ok, 2 * g + s + 3)
                                act.activation(FEAT[:, bass.ds(8 + 2 * g + s, 1), 0, :], t32[:, s:s + 1, :], ACT.Copy).then_inc(hi_w, 1)

                    @block.vector
                    def _(dve):
                        dve.sem_inc(scaled_ok, 2)
                        dve.sem_inc(lo_w, 1)
                        if tag == "l0":
                            for j in range(NT):
                                if j:
                                    dve.wait_ge(bsum_ok, j)
                                dve.tensor_tensor_reduce(junk[:, :], B1[:, j, :], rowscale[:, :], 1.0, 0.0, ALU.mult, ALU.add,
                                                         bsum[:, j:j + 1]).then_inc(bsum_ok, 1)
                            dve.wait_ge(bsum_ok, NT)
                            dve.tensor_tensor(bsum[:, :], bsum[:, :], dinv[:, :], ALU.add).then_inc(bsum_ok, 1)
                            dve.wait_ge(bsum_ok, NT + 1)
                            dve.tensor_tensor(bsum[:, :], bsum[:, :], dinv[:, :], ALU.mult).then_inc(bsum_ok, 1)
                            dve.wait_ge(bsum_ok, NT + 2)
                            dve.wait_ge(bias_in, 16)
                            for j in range(NT):
                                dve.scalar_tensor_tensor(X[:, j, :], brow, bsum[:, j:j + 1], X[:, j, :], ALU.mult, ALU.add).then_inc(bias_ok, 1)
                        else:
                            dve.tensor_scalar(degi[:, :], indeg[:, :], 1.0, None, ALU.max).then_inc(deg_ok, 1)
                            dve.wait_ge(deg_ok, 1)
                            dve.reciprocal(degi[:, :], degi[:, :]).then_inc(deg_ok, 1)
                            dve.wait_ge(deg_ok, 2)
                            for j in range(NT):
                                dve.tensor_scalar(diag[:, j, :], ident32[:, :], degi[:, j:j + 1], None, ALU.mult).then_inc(diag_ok, 1)
                            dve.wait_ge(row_ok, 1)
                        with dve.Fori(0, KD // 2) as g:
                            for s in range(2):
                                dve.wait_ge(summed, 2 * g + s + 1)
                                dve.wait_ge(lo_w, 2 * g + s + 1)
                                dve.tensor_tensor(t32[:, s, :], acc[:, s, 0:NP], rs[:, :], ALU.mult).then_inc(scaled_ok, 1)
                                dve.wait_ge(hi_w, 2 * g + s + 1)
                                dve.tensor_tensor(FEAT[:, bass.ds(8 + 2 * g + s, 1), 1, :], t32[:, s:s + 1, :],
                                                  FEAT[:, bass.ds(8 + 2 * g + s, 1), 0, :], ALU.subtract).then_inc(lo_w, 1)

                    if tag == "l0":
                        @block.sync
                        def _(sp):
                            sp.dma_start(brow, l0_b.partition_broadcast(P)).then_inc(bias_in, 16)

        def project(tag, mats, k0, bias, hidden):
            K = KD * len(mats)
            Q = K // 4
            with ExitStack() as c:
                stage = sb(f"stage_{tag}", [P, 4, HALF], F32, c)
                wr = sb(f"wr_{tag}", [P, 4, 2, HALF], F16, c)
                if bias is not None:
                    bst = sb(f"bst_{tag}", [64, D], F16, c)
                    one = sb(f"one_{tag}", [64, P], F16, c)
                    b32 = stage[0:1, 0:2, :].rearrange("p a n -> p (a n)")
                ps = c.enter_context(nc.psum_tensor(f"ps_{tag}", [P, 8, HALF], F32))
                w_in = [sem(f"w_in{r}_{tag}") for r in range(4)]
                w_hi, w_lo, w_used = sem(f"w_hi_{tag}"), sem(f"w_lo_{tag}"), sem(f"w_used_{tag}")
                out_ok, out_free = sem(f"out_ok_{tag}"), sem(f"out_free_{tag}")
                if hidden:
                    h_ok, l_ok = sem(f"h_ok_{tag}"), sem(f"l_ok_{tag}")
                if bias is not None:
                    b_in, b_ok = sem(f"b_in_{tag}"), sem(f"b_ok_{tag}")
                bank = [[0, 1, 2, 3, 4], [5, 6, 7, 0, 1]]
                with nc.Block() as block:
                    @block.sync
                    def _(sp):
                        if bias is not None:
                            sp.dma_start(b32, bias.rearrange("(a d) -> a d", a=1)).then_inc(b_in, 16)
                            sp.wait_ge(b_ok, 3)
                        for s in range(4):
                            for m, w in enumerate(mats):
                                with sp.Fori(0, 2) as q:
                                    for r in range(4):
                                        n = (s * len(mats) + m) * 8 + q * 4 + r
                                        sp.wait_ge(w_lo, n + 1)
                                        sp.dma_start(stage[:, r, :], w[bass.ds((q * 4 + r) * P, P), (s % 2) * HALF:(s % 2 + 1) * HALF]).then_inc(w_in[r], 16)

                    @block.scalar
                    def _(act):
                        if bias is not None:
                            act.wait_ge(b_in, 16)
                            act.wait_ge(b_ok, 1)
                            act.activation(bst[0:1, :], b32, ACT.Copy, scale=AS * WS).then_inc(b_ok, 1)

                        def hi(s, q, r):
                            n = s * K + q * 4 + r
                            act.wait_ge(w_in[r], 16 * (s * Q + q + 1))
                            if not isinstance(q, int) or q:
                                act.wait_ge(w_used, n - 3 - s)
                            elif s and r < 3:
                                act.wait_ge(w_used, n - 2 - s)
                            elif s:
                                act.wait_ge(out_ok, 5 * s)
                            act.activation(wr[:, r, 0, :], stage[:, r, :], ACT.Copy, scale=WS).then_inc(w_hi, 1)

                        def evac(s):
                            if hidden:
                                for i in range(5):
                                    j, h = 5 * (s // 2) + i, s % 2
                                    act.wait_ge(l_ok, 5 * s + i + 1)
                                    act.activation(N[:, j, 0, h * HALF:(h + 1) * HALF], ps[:, bank[h][i], :], ACT.Copy).then_inc(h_ok, 1)

                        for s in range(4):
                            for r in range(4):
                                hi(s, 0, r)
                            if s:
                                evac(s - 1)
                            with act.Fori(1, Q) as q:
                                for r in range(4):
                                    hi(s, q, r)
                        evac(3)

                    @block.vector
                    def _(dve):
                        dve.sem_inc(w_lo, 4)
                        dve.sem_inc(out_free, 10)
                        if bias is not None:
                            dve.memset(bst[:, :], 0.0).then_inc(b_ok, 1)
                            dve.wait_ge(b_ok, 2)
                            dve.scalar_tensor_tensor(bst[32:33, :], b32, AS * WS, bst[0:1, :], ALU.mult, ALU.subtract).then_inc(b_ok, 1)
                            dve.memset(one[:, :], 1.0).then_inc(b_ok, 1)

                        def lo(s, q, r):
                            n = s * K + q * 4 + r
                            dve.wait_ge(w_hi, n + 1)
                            dve.scalar_tensor_tensor(wr[:, r, 1, :], stage[:, r, :], WS, wr[:, r, 0, :], ALU.mult, ALU.subtract).then_inc(w_lo, 1)

                        def evac(s):
                            for i in range(5):
                                j, h, u = 5 * (s // 2) + i, s % 2, 5 * s + i
                                cols = slice(h * HALF, (h + 1) * HALF)
                                dve.wait_ge(out_ok, u + 1)
                                if hidden:
                                    o = ps[:, bank[h][i], :]
                                    dve.tensor_scalar(o, o, 1 / WS, 0.0, ALU.mult, ALU.max).then_inc(l_ok, 1)
                                    dve.wait_ge(h_ok, u + 1)
                                    dve.tensor_tensor(N[:, j, 1, cols], o, N[:, j, 0, cols], ALU.subtract).then_inc(out_free, 1)
                                else:
                                    dve.scalar_tensor_tensor(X[:, j, cols], ps[:, bank[h][i], :], 1 / (AS * WS), X[:, j, cols],
                                                             ALU.mult, ALU.add).then_inc(out_free, 1)

                        for s in range(4):
                            for r in range(4):
                                lo(s, 0, r)
                            if s:
                                evac(s - 1)
                            with dve.Fori(1, Q) as q:
                                for r in range(4):
                                    lo(s, q, r)
                        evac(3)

                    @block.tensor
                    def _(pe):
                        if bias is not None:
                            pe.wait_ge(b_ok, 4)
                        for s in range(4):
                            g, h = s // 2, s % 2
                            for k in range(K):
                                n = s * K + k
                                pe.wait_ge(w_lo, n + 1 + 4)
                                for i in range(5):
                                    o = ps[:, bank[h][i], :]
                                    if k == 0:
                                        ahead = (i + 9 if i < 2 else i + 1) if h == 0 else (i + 6 if i < 3 else i + 8)
                                        pe.wait_ge(out_free, 10 * g + ahead)
                                        if bias is not None:
                                            pe.matmul(o, one[:, :], bst[:, h * HALF:(h + 1) * HALF], start=True, stop=False)
                                    at = slice((5 * g + i) * P, (5 * g + i + 1) * P)
                                    for a, b in ((0, 0), (0, 1), (1, 0)):
                                        mm = pe.matmul(o, FEAT[:, k0 + k, a, at], wr[:, k % 4, b, :],
                                                       start=(k == 0 and bias is None and (a, b) == (0, 0)),
                                                       stop=(k == K - 1 and (a, b) == (1, 0)))
                                    if k == K - 1:
                                        mm.then_inc(out_ok, 1)
                                if k < K - 1:
                                    mm.then_inc(w_used, 1)

        def normalise(tag, quant):
            with ExitStack() as c:
                n32 = FEAT[:, 8:12, :, :].rearrange("p k h n -> p (k h n)")[:, 0:4096].bitcast(F32).rearrange("p (s d) -> p s d", s=2)
                ps = c.enter_context(nc.psum_tensor(f"tp_{tag}", [P, 4, 2 * HALF], F16))
                stats, moments, root, n32_ok, lo_ok, turned, out_hi = (
                    sem(f"{n}_{tag}") for n in "stats moments root n32_ok lo_ok turned out_hi".split())
                if quant:
                    quant_chain = sem(f"quant_chain_{tag}")
                else:
                    hi_ok, out_lo = sem(f"hi_ok_{tag}"), sem(f"out_lo_{tag}")
                with nc.Block() as block:
                    @block.gpsimd
                    def _(pool):
                        pool.sem_inc(out_hi, 2)
                        if not quant:
                            pool.sem_inc(out_lo, 2)
                        for j in range(NT):
                            pool.wait_ge(moments, j + 1)
                            pool.tensor_scalar(rstd[:, j:j + 1], mv[:, j, 1:2], 1.0, EPS, ALU.mult, ALU.add).then_inc(root, 1)
                            pool.tensor_scalar(shift[:, j:j + 1], mv[:, j, 0:1], -1.0, 0.0, ALU.mult, ALU.add).then_inc(root, 1)
                            pool.wait_ge(root, 5 * j + 2)
                            pool.tensor_tensor(rstd[:, j:j + 1], rstd[:, j:j + 1], pw[:, j:j + 1], ALU.pow).then_inc(root, 1)
                            pool.wait_ge(root, 5 * j + 3)
                            pool.tensor_scalar(rstd[:, j:j + 1], rstd[:, j:j + 1], 1.0 if quant else AS, 0.0, ALU.mult, ALU.add).then_inc(root, 1)
                            pool.wait_ge(root, 5 * j + 4)
                            pool.tensor_tensor(shift[:, j:j + 1], shift[:, j:j + 1], rstd[:, j:j + 1], ALU.mult).then_inc(root, 1)

                    @block.scalar
                    def _(act):
                        def step(j, before):
                            act.wait_ge(root, 5 * j + 5)
                            if j >= 2:
                                act.wait_ge(lo_ok, j - 1)
                            act.activation(n32[:, j % 2, :], X[:, j, :], ACT.Identity, bias=shift[:, j:j + 1],
                                           scale=rstd[:, j:j + 1]).then_inc(n32_ok, 1)
                            if not quant:
                                act.wait_ge(n32_ok, j + 1)
                                act.activation(N[:, j, 0, :], n32[:, j % 2, :], ACT.Copy).then_inc(hi_ok, 1)
                            if before:
                                put(j - 1)

                        def put(j):
                            at = FEAT[:, 0:8, 0, j * P:(j + 1) * P]
                            act.wait_ge(turned, (1 if quant else 2) * j + 1)
                            act.activation(at, ps[:, (2 * j) % 4, :].rearrange("p (k n) -> p k n", k=8), ACT.Copy).then_inc(out_hi, 1)

                        for j in range(NT):
                            step(j, j > 0)
                        put(NT - 1)

                    @block.tensor
                    def _(pe):
                        for j in range(NT):
                            pe.wait_ge(lo_ok, j + 1)
                            for h in range(1 if quant else 2):
                                pe.wait_ge(out_lo if h else out_hi, j + 1)
                                for k in range(KD):
                                    mm = pe.transpose(ps[:, (2 * j + h) % 4, k * P:(k + 1) * P], N[:, j, h, k * P:(k + 1) * P], ident[:, :])
                                mm.then_inc(turned, 1)

                    @block.vector
                    def _(dve):
                        def moment(j):
                            for h in range(2):
                                dve.bn_stats(bn[:, j, h, :], X[:, j, h * HALF:(h + 1) * HALF]).then_inc(stats, 1)
                            dve.wait_ge(stats, 2 * j + 2)
                            dve.bn_aggr(mv[:, j, :], bn[:, j, :, :]).then_inc(moments, 1)

                        def put(j):
                            at = FEAT[:, 0:8, 1, j * P:(j + 1) * P]
                            dve.wait_ge(turned, 2 * j + 2)
                            dve.tensor_copy(at, ps[:, (2 * j + 1) % 4, :].rearrange("p (k n) -> p k n", k=8)).then_inc(out_lo, 1)

                        moment(0)
                        for j in range(NT):
                            if j < NT - 1:
                                moment(j + 1)
                            if quant:
                                quantise(dve, n32[:, j % 2, :], n32_ok, j + 1, qmax[:, j:j + 1], qscale[:, j:j + 1], N[:, j, 0, :], quant_chain, 4 * j, lo_ok)
                            else:
                                dve.wait_ge(hi_ok, j + 1)
                                dve.tensor_tensor(N[:, j, 1, :], n32[:, j % 2, :], N[:, j, 0, :], ALU.subtract).then_inc(lo_ok, 1)
                                if j:
                                    put(j - 1)
                        if not quant:
                            put(NT - 1)

        def quantise(dve, v, v_ok, count, vmax, vscale, whole, chain, n, done):
            dve.wait_ge(v_ok, count)
            dve.tensor_reduce(vmax, v, AX_X, ALU.max, apply_absolute_value=True).then_inc(chain, 1)
            dve.wait_ge(chain, n + 1)
            dve.tensor_scalar(vmax, vmax, 1e-5, 1 / 127.0, ALU.max, ALU.mult).then_inc(chain, 1)
            dve.wait_ge(chain, n + 2)
            dve.reciprocal(vscale, vmax).then_inc(chain, 1)
            dve.wait_ge(chain, n + 3)
            dve.tensor_scalar(v, v, vscale, MAGIC, ALU.mult, ALU.add).then_inc(chain, 1)
            dve.wait_ge(chain, n + 4)
            dve.tensor_scalar(whole, v, MAGIC, 127.0, ALU.subtract, ALU.min).then_inc(done, 1)

        def turn_hidden(tag):
            with ExitStack() as c:
                ps = c.enter_context(nc.psum_tensor(f"tp_{tag}", [P, 4, 2 * HALF], F16))
                turned, out_hi, out_lo = sem(f"turned_{tag}"), sem(f"out_hi_{tag}"), sem(f"out_lo_{tag}")
                with nc.Block() as block:
                    @block.tensor
                    def _(pe):
                        pe.sem_inc(out_hi, 2)
                        pe.sem_inc(out_lo, 2)
                        with pe.Fori(0, NT // 2) as g:
                            for s in range(2):
                                for h in range(2):
                                    pe.wait_ge(out_lo if h else out_hi, 2 * g + s + 1)
                                    for k in range(KD):
                                        mm = pe.transpose(ps[:, 2 * s + h, k * P:(k + 1) * P],
                                                          N[:, bass.ds(2 * g + s, 1), h, k * P:(k + 1) * P], ident[:, :])
                                    mm.then_inc(turned, 1)

                    @block.scalar
                    def _(act):
                        with act.Fori(0, NT // 2) as g:
                            for s in range(2):
                                act.wait_ge(turned, 4 * g + 2 * s + 1)
                                act.activation(FEAT[:, 0:8, 0, bass.ds((2 * g + s) * P, P)],
                                               ps[:, 2 * s, :].rearrange("p (k n) -> p k n", k=8), ACT.Copy).then_inc(out_hi, 1)

                    @block.vector
                    def _(dve):
                        with dve.Fori(0, NT // 2) as g:
                            for s in range(2):
                                dve.wait_ge(turned, 4 * g + 2 * s + 2)
                                dve.tensor_copy(FEAT[:, 0:8, 1, bass.ds((2 * g + s) * P, P)],
                                                ps[:, 2 * s + 1, :].rearrange("p (k n) -> p k n", k=8)).then_inc(out_lo, 1)

        def route():
            with ExitStack() as c:
                g32 = sb("g32", [P, KD, 8], F32, c)
                g2 = sb("g2", [P, KD, 2, 8], F16, c)
                both = sb("both", [P, NT, 2, 8], F32, c)
                logit = sb("logit", [P, NT, 8], F32, c)
                best = sb("best", [P, NT, 8], F32, c)
                where = sb("where", [P, NT, 8], mybir.dt.uint32, c)
                where_f = sb("where_f", [P, NT, 8], F32, c)
                mask = sb("mask", [P, NT, 8], F32, c)
                which = sb("which", [P, 8], F32, c)
                total = sb("total", [P, NT], F32, c)
                neg = sb("neg", [P, NT], F32, c)
                b2s = sb("b2s", [8, D], F32, c)
                byx = sb("byx", [8, NP], F32, c)
                pl = c.enter_context(nc.psum_tensor("pl", [P, 4, HALF], F32))
                pt = c.enter_context(nc.psum_tensor("pt", [P, 2, HALF], F32))
                py = c.enter_context(nc.psum_tensor("py", [P, 2, HALF], F32))
                node = sb("node", [P, NT], F32, c)
                live = sb("live", [P, NT], F32, c)
                before = sb("before", [P, P], F32, c)
                sel = sb("sel", [P, NT, 8], F32, c)
                per_tile = sb("per_tile", [P, NT, 8], F32, c)
                start = sb("start", [P, 9], F32, c)
                tiles = sb("tiles", [P, 8], F32, c)
                offset = sb("offset", [P, NT, 8], F32, c)
                pair = sb("pair", [P, 2, NT, 8], F32, c)
                slot = sb("slot", [P, 2, NT], F32, c)
                slot_tile = sb("slot_tile", [P, 2, NT], F32, c)
                slot_row = sb("slot_row", [P, 2, NT], F32, c)
                ramp = sb("ramp", [P, P], F32, c)
                hot_row = sb("hot_row", [P, 2, P], F16, c)
                hot_tile = sb("hot_tile", [P, 2, ST + 1], F16, c)
                chain, rows_out, ramps, sel_ok, ranked, hot_ok, hot_used, placed, place_free = (sem(f"route_{n}") for n in
                    "chain rows_out ramps sel_ok ranked hot_ok hot_used placed place_free".split())
                r_in, r2_in, g_ok, w_ok, l_ok, c1, c2, c3, p_ok, x_ok, e_ok = (sem(f"route_{n}") for n in range(11))
                t_ok, b_ok, y_ok, y_free = (sem(f"routeb_{n}") for n in range(4))
                with nc.Block() as block:
                    @block.sync
                    def _(sp):
                        sp.dma_start(g32[:, :, :], gate.rearrange("(k p) e -> p k e", p=P)).then_inc(r_in, 16)
                        sp.dma_start(b2s[:, :], b2).then_inc(r2_in, 16)
                        sp.dma_start(rows.rearrange("(j p) d -> p j d", p=P), N.rearrange("p j h d -> p j (h d)")).then_inc(rows_out, 16)
                        sp.wait_ge(rows_out, 16)

                    @block.gpsimd
                    def _(pool):
                        pool.iota(which[:, :], [[1, 8]], base=0, channel_multiplier=0, allow_small_or_imprecise_dtypes=True).then_inc(w_ok, 1)
                        pool.iota(node[:, :], [[P, NT]], base=0, channel_multiplier=1, allow_small_or_imprecise_dtypes=True).then_inc(ramps, 1)
                        pool.iota(ramp[:, :], [[1, P]], base=0, channel_multiplier=0, allow_small_or_imprecise_dtypes=True).then_inc(ramps, 1)
                        pool.memset(before[:, :], 1.0).then_inc(ramps, 1)
                        pool.wait_ge(ramps, 3)
                        pool.affine_select(out=before[:, :], in_=before[:, :], compare_op=ALU.is_ge, fill=0.0,
                                           base=-1, pattern=[[1, P]], channel_multiplier=-1).then_inc(ramps, 1)

                    @block.scalar
                    def _(act):
                        act.wait_ge(r_in, 16)
                        act.activation(g2[:, :, 0, :], g32[:, :, :], ACT.Copy, scale=WS).then_inc(g_ok, 1)
                        act.wait_ge(c2, NT)
                        for j in range(NT):
                            act.activation(mask[:, j, :], logit[:, j, :], ACT.Exp, bias=neg[:, j:j + 1], accum_out=total[:, j:j + 1]).then_inc(e_ok, 1)
                        act.wait_ge(t_ok, NT)
                        act.activation(byx[:, 0:512], pt[0:8, 0, :], ACT.Copy).then_inc(b_ok, 1)
                        act.activation(byx[:, 512:1024], pt[0:8, 1, :], ACT.Copy).then_inc(b_ok, 1)
                        act.activation(byx[:, 1024:1280], pl[0:8, 3, 0:256], ACT.Copy).then_inc(b_ok, 1)

                    @block.tensor
                    def _(pe):
                        pe.wait_ge(g_ok, 2)
                        for j in range(NT):
                            o = pl[:, 0, 16 * j:16 * j + 16]
                            for k in range(KD):
                                pe.matmul(o, FEAT[:, k, 0, j * P:(j + 1) * P], g2[:, k, :, :].rearrange("p a e -> p (a e)"),
                                          start=(k == 0), stop=False)
                                mm = pe.matmul(o[:, 0:8], FEAT[:, k, 1, j * P:(j + 1) * P], g2[:, k, 0, :], start=False, stop=(k == KD - 1))
                            mm.then_inc(l_ok, 1)
                        pe.wait_ge(p_ok, 1)
                        for j in range(NT):
                            o = pt[0:8, j // 4, (j % 4) * P:(j % 4 + 1) * P] if j < 8 else pl[0:8, 3, (j - 8) * P:(j - 7) * P]
                            pe.transpose(o, chosen[:, j, :], ident32[:, :]).then_inc(t_ok, 1)
                        pe.wait_ge(ramps, 4)
                        pe.wait_ge(sel_ok, 1)
                        pe.matmul(pl[:, 1, 0:8 * NT], before[:, :], sel.rearrange("p j e -> p (j e)"), start=True, stop=True)
                        pe.matmul(pl[:, 1, 8 * NT:16 * NT], ones32[:, :], sel.rearrange("p j e -> p (j e)"), start=True, stop=True).then_inc(ranked, 1)
                        for i in range(2 * NT):
                            pe.wait_ge(hot_ok, i + 1)
                            pe.matmul(pl[:, 2, 0:ST + 1], hot_row[:, i % 2, :], hot_tile[:, i % 2, :], start=(i == 0), stop=(i == 2 * NT - 1)).then_inc(hot_used, 1)
                        pe.wait_ge(r2_in, 16)
                        pe.wait_ge(b_ok, 3)
                        for j in range(NT):
                            for h in range(2):
                                pe.wait_ge(y_free, 2 * j + h + 1)
                                pe.matmul(py[:, h, :], byx[:, j * P:(j + 1) * P], b2s[:, h * HALF:(h + 1) * HALF], start=True, stop=True).then_inc(y_ok, 1)

                    @block.vector
                    def _(dve):
                        dve.sem_inc(y_free, 2)
                        dve.wait_ge(g_ok, 1)
                        dve.scalar_tensor_tensor(g2[:, :, 1, :], g32[:, :, :], WS, g2[:, :, 0, :], ALU.mult, ALU.subtract).then_inc(g_ok, 1)
                        dve.wait_ge(l_ok, NT)
                        dve.tensor_scalar(both[:, :, :, :].rearrange("p j a e -> p (j a e)"), pl[:, 0, 0:16 * NT], 1 / (AS * WS), None, ALU.mult).then_inc(c1, 1)
                        dve.wait_ge(c1, 1)
                        dve.tensor_tensor(logit[:, :, :], both[:, :, 0, :], both[:, :, 1, :], ALU.add).then_inc(c1, 1)
                        dve.wait_ge(c1, 2)
                        for j in range(NT):
                            dve.max(best[:, j, :], logit[:, j, :]).then_inc(c1, 1)
                        dve.wait_ge(c1, NT + 2)
                        for j in range(NT):
                            dve.tensor_scalar(neg[:, j:j + 1], best[:, j, 0:1], -1.0, None, ALU.mult).then_inc(c2, 1)
                            dve.max_index(where[:, j, :], best[:, j, :], logit[:, j, :]).then_inc(c3, 1)
                        dve.wait_ge(c3, NT)
                        dve.tensor_copy(where_f[:, :, :], where[:, :, :]).then_inc(c3, 1)
                        dve.wait_ge(c3, NT + 1)
                        dve.wait_ge(w_ok, 1)
                        dve.wait_ge(e_ok, NT)
                        for j in range(NT):
                            dve.tensor_scalar(both[:, j, 0, :], which[:, :], where_f[:, j, 0:1], None, ALU.is_equal).then_inc(x_ok, 1)
                            dve.tensor_scalar(both[:, j, 1, :], which[:, :], where_f[:, j, 1:2], None, ALU.is_equal).then_inc(x_ok, 1)
                        dve.reciprocal(total[:, :], total[:, :]).then_inc(x_ok, 1)
                        dve.wait_ge(x_ok, 2 * NT + 1)
                        dve.tensor_tensor(logit[:, :, :], both[:, :, 0, :], both[:, :, 1, :], ALU.add).then_inc(x_ok, 1)
                        dve.wait_ge(x_ok, 2 * NT + 2)
                        for j in range(NT):
                            last = dve.scalar_tensor_tensor(chosen[:, j, :], mask[:, j, :], total[:, j:j + 1], logit[:, j, :], ALU.mult, ALU.mult)
                        last.then_inc(p_ok, 1)
                        dve.wait_ge(ramps, 4)
                        dve.tensor_scalar(live[:, :], node[:, :], float(NODES), None, ALU.is_lt).then_inc(chain, 1)
                        dve.wait_ge(chain, 1)
                        dve.tensor_tensor(node[:, :], node[:, :], live[:, :], ALU.mult).then_inc(chain, 1)
                        dve.tensor_tensor(sel[:, :, :], logit[:, :, :], live[:, :].unsqueeze(2).to_broadcast([P, NT, 8]), ALU.mult).then_inc(sel_ok, 1)
                        dve.wait_ge(ranked, 1)
                        dve.tensor_copy(per_tile.rearrange("p j e -> p (j e)"), pl[:, 1, 8 * NT:16 * NT]).then_inc(chain, 1)
                        dve.wait_ge(chain, 3)
                        dve.tensor_reduce(tiles[:, :], per_tile.rearrange("p j e -> p e j"), AX_X, ALU.add).then_inc(chain, 1)
                        dve.wait_ge(chain, 4)
                        dve.tensor_scalar(tiles[:, :], tiles[:, :], 1.0 / P, 0.498, ALU.mult, ALU.add).then_inc(chain, 1)
                        dve.wait_ge(chain, 5)
                        dve.tensor_scalar(tiles[:, :], tiles[:, :], MAGIC, None, ALU.add).then_inc(chain, 1)
                        dve.wait_ge(chain, 6)
                        dve.tensor_scalar(tiles[:, :], tiles[:, :], MAGIC, 1.0, ALU.subtract, ALU.max).then_inc(chain, 1)
                        dve.memset(start[:, :], 0.0).then_inc(chain, 1)
                        for e in range(8):
                            dve.wait_ge(chain, 8 + e)
                            dve.tensor_tensor(start[:, e + 1:e + 2], start[:, e:e + 1], tiles[:, e:e + 1], ALU.add).then_inc(chain, 1)
                        dve.wait_ge(chain, 16)
                        dve.tensor_copy(bounds_i[:, :], start[:, :]).then_inc(chain, 1)
                        dve.tensor_scalar(offset[:, 0, :], start[:, 0:8], float(P), None, ALU.mult).then_inc(chain, 1)
                        for j in range(1, NT):
                            dve.wait_ge(chain, 17 + j)
                            dve.tensor_tensor(offset[:, j, :], offset[:, j - 1, :], per_tile[:, j - 1, :], ALU.add).then_inc(chain, 1)
                        dve.wait_ge(chain, 17 + NT)
                        dve.tensor_tensor(offset.rearrange("p j e -> p (j e)"), offset.rearrange("p j e -> p (j e)"), pl[:, 1, 0:8 * NT], ALU.add).then_inc(chain, 1)
                        dve.wait_ge(chain, 18 + NT)
                        for i in range(2):
                            dve.tensor_tensor(pair[:, i, :, :], both[:, :, i, :], offset[:, :, :], ALU.mult).then_inc(chain, 1)
                        dve.wait_ge(chain, 20 + NT)
                        dve.tensor_reduce(slot[:, :, :], pair[:, :, :, :], AX_X, ALU.add).then_inc(chain, 1)
                        dve.wait_ge(chain, 21 + NT)
                        for i in range(2):
                            dve.tensor_tensor(pair[:, i, :, :], both[:, :, i, :], chosen[:, :, :], ALU.mult).then_inc(chain, 1)
                        dve.wait_ge(chain, 23 + NT)
                        dve.tensor_reduce(weight[:, :, :], pair[:, :, :, :], AX_X, ALU.add).then_inc(chain, 1)
                        dve.wait_ge(chain, 24 + NT)
                        dve.tensor_scalar(weight[:, :, :], weight[:, :, :], 1 / (AS * WS), None, ALU.mult).then_inc(chain, 1)
                        dve.tensor_scalar(slot_tile[:, :, :], slot[:, :, :], 1.0 / P, -0.498, ALU.mult, ALU.add).then_inc(chain, 1)
                        dve.wait_ge(chain, 26 + NT)
                        dve.tensor_scalar(slot_tile[:, :, :], slot_tile[:, :, :], MAGIC, None, ALU.add).then_inc(chain, 1)
                        dve.wait_ge(chain, 27 + NT)
                        dve.tensor_scalar(slot_tile[:, :, :], slot_tile[:, :, :], MAGIC, None, ALU.subtract).then_inc(chain, 1)
                        dve.wait_ge(chain, 28 + NT)
                        dve.scalar_tensor_tensor(slot_row[:, :, :], slot_tile[:, :, :], -float(P), slot[:, :, :], ALU.mult, ALU.add).then_inc(chain, 1)
                        dve.wait_ge(chain, 29 + NT)
                        for i in range(2):
                            dve.tensor_tensor(slot[:, i, :], slot[:, i, :], live[:, :], ALU.mult).then_inc(chain, 1)
                        dve.wait_ge(chain, 31 + NT)
                        dve.tensor_copy(slot_i[:, :, :], slot[:, :, :]).then_inc(chain, 1)
                        for i in range(2 * NT):
                            c_, j = i // NT, i % NT
                            if i >= 2:
                                dve.wait_ge(hot_used, i - 1)
                            dve.tensor_scalar(hot_row[:, i % 2, :], ramp[:, :], slot_row[:, c_, j:j + 1], None, ALU.is_equal)
                            dve.tensor_scalar(hot_tile[:, i % 2, :], ramp[:, 0:ST + 1], slot_tile[:, c_, j:j + 1], node[:, j:j + 1], ALU.is_equal, ALU.mult).then_inc(hot_ok, 1)
                        dve.wait_ge(hot_used, 2 * NT)
                        dve.tensor_copy(node_i[:, :], pl[:, 2, 0:ST + 1]).then_inc(chain, 1)
                        for j in range(NT):
                            for h in range(2):
                                cols = slice(h * HALF, (h + 1) * HALF)
                                dve.wait_ge(y_ok, 2 * j + h + 1)
                                dve.tensor_tensor(X[:, j, cols], py[:, h, :], X[:, j, cols], ALU.add).then_inc(y_free, 1)

        def experts():
            with ExitStack() as c:
                def w_set(at):
                    return (BIG[:, at:at + 8192].rearrange("p (k h f) -> p k h f", k=8, h=2),
                            BIG[:, at + 8192:at + 16384].rearrange("p (k h d) -> p k h d", k=4, h=2))

                W = [w_set(0), w_set(16384)]
                stage = BIG[:, 32768:40960].bitcast(F32).rearrange("p (r n) -> p r n", r=4)
                g_row = BIG[:, 40960:43008]
                xT = BIG[:, 43008:45056].rearrange("p (h k n) -> p h k n", h=2, k=KD)
                h32 = BIG[:, 45056:46080].bitcast(F32)
                hid = BIG[:, 46080:47104].rearrange("p (h f) -> p h f", h=2)
                hT = BIG[:, 47104:48128].rearrange("p (h k n) -> p h k n", h=2, k=4)
                y32 = BIG[:, 48128:50176].bitcast(F32)
                back = BIG[:, 50176:58368].bitcast(F32).rearrange("p (r d) -> p r d", r=4)
                b1_32 = BIG[0:1, 58368:59392].bitcast(F32)
                b1_row = sb("b1_row", [64, 2, HALF], F16, c)
                one = sb("one_moe", [64, P], F16, c)
                tile_nodes = sb("tile_nodes", [P, 1], U32, c)
                x_ps = c.enter_context(nc.psum_tensor("x_ps", [P, 2, 2 * HALF], F16))
                h_ps = c.enter_context(nc.psum_tensor("h_ps", [P, HALF], F32))
                t_ps = c.enter_context(nc.psum_tensor("t_ps", [P, 2, 2 * HALF], F16))
                y_ps = c.enter_context(nc.psum_tensor("y_ps", [P, 2, HALF], F32))
                w_in = [sem(f"moe_w_in{r}") for r in range(4)]
                back_in = [sem(f"moe_back_in{r}") for r in range(4)]
                w_hi, w_lo, b_in, b_hi, b_lo, one_ok = (sem(f"moe_{n}") for n in "w_hi w_lo b_in b_hi b_lo one_ok".split())
                nodes_ok, nodes_seen, rows_in, x_turned, x_hi, x_lo = (sem(f"moe_{n}") for n in "nodes_ok nodes_seen rows_in x_turned x_hi x_lo".split())
                h_ok, gelu_ok, h_hi, h_lo, h_turned, hT_hi, hT_lo = (sem(f"moe_{n}") for n in "h_ok gelu_ok h_hi h_lo h_turned hT_hi hT_lo".split())
                y_ok, y_left, y_right, stored, added = (sem(f"moe_{n}") for n in "y_ok y_left y_right stored added".split())

                def sweep(eng, expert):
                    def one_expert(e, s):
                        if isinstance(e, int):
                            a, b = bounds_i[0:1, e:e + 1], bounds_i[0:1, e + 1:e + 2]
                        else:
                            a, b = bounds_i[0:1, bass.ds(e, 1)], bounds_i[0:1, bass.ds(e + 1, 1)]
                        first = 0 if isinstance(e, int) and e == 0 else eng.value_load(a, min_val=1, max_val=ST - 1)
                        expert(e, s, first, eng.value_load(b, min_val=1, max_val=ST))

                    one_expert(0, 0)
                    with eng.Fori(0, 3) as g:
                        one_expert(2 * g + 1, 1)
                        one_expert(2 * g + 2, 0)
                    one_expert(7, 1)

                with nc.Block() as block:
                    @block.sync
                    def _(sp):
                        def load_bias(e):
                            sp.wait_ge(b_lo, e + 1)
                            sp.dma_start(b1_32, b1[bass.ds(e, 1), :]).then_inc(b_in, 16)

                        def load(e, some):
                            for i in some:
                                sp.wait_ge(w_lo, 8 * e + i + 1)
                                if i < 4:
                                    sp.dma_start(stage[:, i, :].rearrange("p (k f) -> p k f", k=2),
                                                 w1[bass.ds(e * D + i * 2 * P, 2 * P), :].rearrange("(k p) f -> p k f", p=P)).then_inc(w_in[i], 16)
                                else:
                                    sp.dma_start(stage[:, i - 4, :], w2[bass.ds(e * HALF + (i - 4) * P, P), :]).then_inc(w_in[i - 4], 16)

                        def store(t):
                            sp.wait_ge(y_left, t + 2)
                            sp.wait_ge(y_right, t + 2)
                            sp.dma_start(results[bass.ds(t * P, P), :], y32).then_inc(stored, 16)

                        def expert(e, s, first, end):
                            last = isinstance(e, int) and e == 7
                            if not last:
                                load(e + 1, range(4, 8))
                            if not (isinstance(e, int) and e == 0):
                                store(first - 1)
                            if isinstance(e, int) and e == 0:
                                load_bias(2)
                                load(2, range(4))
                            elif not last:
                                if s == 1:
                                    load_bias(e + 2)
                                    load(e + 2, range(4))
                                else:
                                    with sp.If(e < 6):
                                        later = nc.s_assert_within(e + 2, 4, 7, skip_runtime_bounds_check_because="e < 6")
                                        load_bias(later)
                                        load(later, range(4))
                            with sp.Fori(first + 1, end) as t:
                                store(t - 1)

                        load_bias(0)
                        load(0, range(8))
                        load_bias(1)
                        load(1, range(4))
                        sweep(sp, expert)
                        total = sp.value_load(bounds_i[0:1, 8:9], min_val=8, max_val=ST)
                        store(total - 1)

                    @block.gpsimd
                    def _(pool):
                        total = pool.value_load(bounds_i[0:1, 8:9], min_val=8, max_val=ST)
                        with pool.Fori(0, total + 1) as t:
                            pool.wait_ge(x_turned, t + 1)
                            pool.tensor_copy(tile_nodes[:, :], node_i[:, bass.ds(t, 1)]).then_inc(nodes_ok, 1)
                            pool.wait_ge(nodes_ok, t + 1)
                            pool.sem_inc(nodes_seen, 1)
                            pool.indirect_dma_start(g_row, None, rows[:, :], bass.IndirectOffsetOnAxis(ap=tile_nodes[:, :], axis=0)).then_inc(rows_in, 16)
                        pool.wait_ge(stored, 16 * total + 16)
                        pool.sem_inc(nodes_seen, 1)
                        for i in range(2 * NT):
                            j, c_ = i // 2, i % 2
                            if i >= 4:
                                pool.wait_ge(added, i - 3)
                            pool.indirect_dma_start(back[:, i % 4, :], None, results[:, :],
                                                    bass.IndirectOffsetOnAxis(ap=slot_i[:, c_, j:j + 1], axis=0)).then_inc(back_in[i % 4], 16)

                    def place(i, h, s):
                        w1s, w2s = W[s]
                        if i < 4:
                            return w1s[:, 2 * i:2 * i + 2, h, :], stage[:, i, :].rearrange("p (k f) -> p k f", k=2)
                        return w2s[:, i - 4, h, :], stage[:, i - 4, :]

                    @block.scalar
                    def _(act):
                        def split(e, s, some):
                            for i in some:
                                act.wait_ge(w_in[i % 4], 32 * e + (16 if i < 4 else 32))
                                part, src = place(i, 0, s)
                                act.activation(part, src, ACT.Copy, scale=WS).then_inc(w_hi, 1)

                        def bias(e, s):
                            act.wait_ge(b_in, 16 * e + 16)
                            act.activation(b1_row[0:1, s, :], b1_32, ACT.Copy, scale=AS * WS).then_inc(b_hi, 1)

                        def turned(t):
                            act.wait_ge(x_turned, t + 2)
                            act.activation(xT[:, 0, :, :].rearrange("p k n -> p (k n)"), x_ps[:, 0, :], ACT.Copy).then_inc(x_hi, 1)

                        def hidden(t):
                            act.wait_ge(h_ok, t + 1)
                            act.wait_ge(h_lo, t + 1)
                            act.activation(h32, h_ps[:, :], ACT.Gelu_apprx_tanh, scale=1 / (AS * WS)).then_inc(gelu_ok, 1)
                            act.wait_ge(gelu_ok, t + 2)
                            act.wait_ge(h_turned, t + 1)
                            act.activation(hid[:, 0, :], h32, ACT.Copy, scale=AS).then_inc(h_hi, 1)

                        def leave(t):
                            act.wait_ge(y_ok, t + 1)
                            act.wait_ge(stored, 16 * t + 16)
                            act.activation(y32[:, 0:HALF], y_ps[:, 0, :], ACT.Copy).then_inc(y_left, 1)

                        def hidden_turned(t):
                            act.wait_ge(h_turned, t + 2)
                            act.activation(hT[:, 0, :, :].rearrange("p k n -> p (k n)"), t_ps[:, 0, 0:HALF], ACT.Copy).then_inc(hT_hi, 1)

                        def expert(e, s, first, end):
                            ahead = not (isinstance(e, int) and e == 7)
                            hidden(first)
                            turned(first + 1)
                            if ahead:
                                bias(e + 1, 1 - s)
                                split(e + 1, 1 - s, range(4))
                            if not (isinstance(e, int) and e == 0):
                                leave(first - 1)
                            hidden_turned(first)
                            if ahead:
                                split(e + 1, 1 - s, range(4, 8))
                            with act.Fori(first + 1, end) as t:
                                hidden(t)
                                turned(t + 1)
                                leave(t - 1)
                                hidden_turned(t)

                        act.wait_ge(one_ok, 2)
                        bias(0, 0)
                        split(0, 0, range(8))
                        turned(0)
                        sweep(act, expert)
                        total = act.value_load(bounds_i[0:1, 8:9], min_val=8, max_val=ST)
                        leave(total - 1)

                    @block.vector
                    def _(dve):
                        dve.sem_inc(w_lo, 4)
                        for free in (b_lo, x_turned, gelu_ok, h_lo, h_turned, x_hi, x_lo, hT_hi, hT_lo, y_left, y_right):
                            dve.sem_inc(free, 1)
                        dve.sem_inc(stored, 16)
                        dve.memset(b1_row[:, :, :], 0.0).then_inc(one_ok, 1)
                        dve.memset(one[:, :], 1.0).then_inc(one_ok, 1)

                        def split(e, s, some):
                            for i in some:
                                dve.wait_ge(w_hi, 8 * e + i + 1)
                                hi_, src = place(i, 0, s)
                                lo_, src = place(i, 1, s)
                                dve.scalar_tensor_tensor(lo_, src, WS, hi_, ALU.mult, ALU.subtract).then_inc(w_lo, 1)

                        def bias(e, s):
                            dve.wait_ge(b_hi, e + 1)
                            dve.scalar_tensor_tensor(b1_row[32:33, s, :], b1_32, AS * WS, b1_row[0:1, s, :], ALU.mult, ALU.subtract).then_inc(b_lo, 1)

                        def turned(t):
                            dve.wait_ge(x_turned, t + 2)
                            dve.tensor_copy(xT[:, 1, :, :].rearrange("p k n -> p (k n)"), x_ps[:, 1, :]).then_inc(x_lo, 1)

                        def hidden(t):
                            dve.wait_ge(h_hi, t + 1)
                            dve.scalar_tensor_tensor(hid[:, 1, :], h32, AS, hid[:, 0, :], ALU.mult, ALU.subtract).then_inc(h_lo, 1)

                        def leave(t):
                            dve.wait_ge(y_ok, t + 1)
                            dve.wait_ge(stored, 16 * t + 16)
                            dve.tensor_copy(y32[:, HALF:D], y_ps[:, 1, :]).then_inc(y_right, 1)

                        def hidden_turned(t):
                            dve.wait_ge(h_turned, t + 2)
                            dve.tensor_copy(hT[:, 1, :, :].rearrange("p k n -> p (k n)"), t_ps[:, 1, 0:HALF]).then_inc(hT_lo, 1)

                        def expert(e, s, first, end):
                            ahead = not (isinstance(e, int) and e == 7)
                            hidden(first)
                            turned(first + 1)
                            if ahead:
                                bias(e + 1, 1 - s)
                                split(e + 1, 1 - s, range(4))
                            if not (isinstance(e, int) and e == 0):
                                leave(first - 1)
                            hidden_turned(first)
                            if ahead:
                                split(e + 1, 1 - s, range(4, 8))
                            with dve.Fori(first + 1, end) as t:
                                hidden(t)
                                turned(t + 1)
                                leave(t - 1)
                                hidden_turned(t)

                        dve.wait_ge(one_ok, 2)
                        bias(0, 0)
                        split(0, 0, range(8))
                        turned(0)
                        sweep(dve, expert)
                        total = dve.value_load(bounds_i[0:1, 8:9], min_val=8, max_val=ST)
                        leave(total - 1)
                        for i in range(2 * NT):
                            j, c_ = i // 2, i % 2
                            dve.wait_ge(back_in[i % 4], 16 * (i // 4 + 1))
                            if c_:
                                dve.wait_ge(added, i)
                            dve.scalar_tensor_tensor(X[:, j, :], back[:, i % 4, :], weight[:, c_, j:j + 1], X[:, j, :], ALU.mult, ALU.add).then_inc(added, 1)

                    @block.tensor
                    def _(pe):
                        def turn_rows(t):
                            pe.wait_ge(rows_in, 16 * t + 16)
                            for h, free in ((0, x_hi), (1, x_lo)):
                                pe.wait_ge(free, t + 1)
                                for k in range(KD):
                                    mm = pe.transpose(x_ps[:, h, k * P:(k + 1) * P], g_row[:, h * D + k * P:h * D + (k + 1) * P], ident[:, :])
                            mm.then_inc(x_turned, 1)

                        def first_products(t, s):
                            w1s, w2s = W[s]
                            pe.wait_ge(gelu_ok, t + 1)
                            pe.wait_ge(x_hi, t + 2)
                            pe.wait_ge(x_lo, t + 2)
                            pe.matmul(h_ps[:, :], one[:, :], b1_row[:, s, :], start=True, stop=False)
                            for k in range(KD):
                                for a, b in ((0, 0), (0, 1), (1, 0)):
                                    mm = pe.matmul(h_ps[:, :], xT[:, a, k, :], w1s[:, k, b, :], start=False, stop=(k == KD - 1 and a == 1))
                            mm.then_inc(h_ok, 1)

                        def second_products(t, s):
                            w1s, w2s = W[s]
                            for ok in (hT_hi, hT_lo):
                                pe.wait_ge(ok, t + 2)
                            for free in (y_left, y_right):
                                pe.wait_ge(free, t + 1)
                            for k in range(4):
                                for a, b in ((0, 0), (0, 1), (1, 0)):
                                    for h in range(2):
                                        mm = pe.matmul(y_ps[:, h, :], hT[:, a, k, :], w2s[:, k, b, h * HALF:(h + 1) * HALF],
                                                       start=(k == 0 and (a, b) == (0, 0)), stop=(k == 3 and a == 1))
                            mm.then_inc(y_ok, 1)

                        def turn_hidden_rows(t):
                            pe.wait_ge(h_lo, t + 2)
                            for h, free in ((0, hT_hi), (1, hT_lo)):
                                pe.wait_ge(free, t + 1)
                                for k in range(4):
                                    mm = pe.transpose(t_ps[:, h, k * P:(k + 1) * P], hid[:, h, k * P:(k + 1) * P], ident[:, :])
                            mm.then_inc(h_turned, 1)

                        def expert(e, s, first, end):
                            pe.wait_ge(w_lo, 8 * e + 8 + 4)
                            pe.wait_ge(b_lo, e + 2)
                            first_products(first, s)
                            turn_rows(first + 1)
                            if not (isinstance(e, int) and e == 0):
                                second_products(first - 1, 1 - s)
                            turn_hidden_rows(first)
                            with pe.Fori(first + 1, end) as t:
                                first_products(t, s)
                                turn_rows(t + 1)
                                second_products(t - 1, s)
                                turn_hidden_rows(t)

                        pe.wait_ge(one_ok, 2)
                        turn_rows(0)
                        sweep(pe, expert)
                        total = pe.value_load(bounds_i[0:1, 8:9], min_val=8, max_val=ST)
                        second_products(total - 1, 1)

        def ternary_ffn():
            with ExitStack() as c:
                w32 = BIG[:, 20480:20480 + 24576].bitcast(F32).rearrange("p (m n) -> p m n", m=3)
                wt = B1[:, :, :].rearrange("p j n -> p (j n)")[:, 0:12288].rearrange("p (m n) -> p m n", m=3)
                wsum = sb("wsum", [P, 3], F32, c)
                wmean = sb("wmean", [P, 3], F32, c)
                wscale = sb("wscale", [P, 3], F32, c)
                gk = sb("gk", [P, 2, HALF], F32, c)
                gq = sb("gq", [P, 2, HALF], F16, c)
                gT = sb("gT", [P, 2, 4, P], F16, c)
                k_gate, k_up, vmax, vscale, k_down = (sb(f"ffn_{n}", [P, NT], F32, c) for n in range(5))
                pm = c.enter_context(nc.psum_tensor("pm", [P, HALF], F32))
                pg = c.enter_context(nc.psum_tensor("pg", [P, 2, HALF], F32))
                pu = c.enter_context(nc.psum_tensor("pu", [P, HALF], F32))
                ptr = c.enter_context(nc.psum_tensor("ptr", [P, 2, 2 * HALF], F16))
                pd = c.enter_context(nc.psum_tensor("pd", [P, 2, HALF], F32))
                m_in = [sem(f"ffn_in{m}") for m in range(3)]
                s_sum, s_all, s_mean, s_wt, g_ok, g_free, v_ok, q_ok, t_ok, t_out, d_ok, x_ok, chain, k_ok, chain2 = (sem(f"ffn{n}_s") for n in range(15))
                with nc.Block() as block:
                    @block.sync
                    def _(sp):
                        for m, w in enumerate((wg, wu, wd)):
                            K = w.shape[0] // P
                            sp.dma_start(w32[:, m, :].rearrange("p (k n) -> p k n", k=K), w.rearrange("(k p) n -> p k n", p=P)).then_inc(m_in[m], 16)

                    @block.scalar
                    def _(act):
                        for m in range(3):
                            act.wait_ge(m_in[m], 16)
                            act.activation(wt[:, m, :], w32[:, m, :], ACT.Abs, accum_out=wsum[:, m:m + 1]).then_inc(s_sum, 1)
                        for j in range(NT):
                            act.wait_ge(g_ok, j + 1)
                            act.wait_ge(k_ok, 2)
                            if j >= 2:
                                act.wait_ge(q_ok, j - 1)
                            act.activation(gk[:, j % 2, :], pg[:, 0, :], ACT.Silu, scale=k_gate[:, j:j + 1]).then_inc(g_free, 1)
                            act.wait_ge(t_ok, j + 1)
                            act.activation(gT[:, j % 2, :, :], ptr[:, j % 2, 0:HALF].rearrange("p (k n) -> p k n", k=4), ACT.Copy).then_inc(t_out, 1)

                    @block.tensor
                    def _(pe):
                        pe.wait_ge(s_sum, 3)
                        pe.matmul(pm[:, 0:3], ones32[:, :], wsum[:, :], start=True, stop=True).then_inc(s_all, 1)
                        pe.wait_ge(s_wt, 3)

                        def up(j):
                            if j:
                                pe.wait_ge(g_free, j)
                                pe.wait_ge(v_ok, j)
                            for m, o in ((0, pg[:, 0, :]), (1, pu[:, :])):
                                for k in range(KD):
                                    mm = pe.matmul(o, FEAT[:, k, 0, j * P:(j + 1) * P], wt[:, m, k * HALF:(k + 1) * HALF], start=(k == 0), stop=(k == KD - 1))
                            mm.then_inc(g_ok, 1)

                        def down(j):
                            pe.wait_ge(q_ok, j + 1)
                            for k in range(4):
                                mm = pe.transpose(ptr[:, j % 2, k * P:(k + 1) * P], gq[:, j % 2, k * P:(k + 1) * P], ident[:, :])
                            mm.then_inc(t_ok, 1)
                            pe.wait_ge(t_out, j + 1)
                            if j:
                                pe.wait_ge(x_ok, j)
                            for k in range(4):
                                for h in range(2):
                                    mm = pe.matmul(pd[:, h, :], gT[:, j % 2, k, :], wt[:, 2, k * D + h * HALF:k * D + (h + 1) * HALF], start=(k == 0), stop=(k == 3))
                            mm.then_inc(d_ok, 1)

                        for j in range(NT):
                            up(j)
                            if j:
                                down(j - 1)
                        down(NT - 1)

                    @block.vector
                    def _(dve):
                        dve.wait_ge(s_all, 1)
                        dve.tensor_scalar(wmean[:, :], pm[:, 0:3], 1.0 / (D * HALF), 1e-5, ALU.mult, ALU.max).then_inc(s_mean, 1)
                        dve.wait_ge(s_mean, 1)
                        dve.reciprocal(wscale[:, :], wmean[:, :]).then_inc(s_mean, 1)
                        dve.wait_ge(s_mean, 2)
                        for m in range(3):
                            dve.tensor_scalar(w32[:, m, :], w32[:, m, :], wscale[:, m:m + 1], MAGIC, ALU.mult, ALU.add).then_inc(chain, 1)
                            dve.wait_ge(chain, 2 * m + 1)
                            dve.tensor_scalar(w32[:, m, :], w32[:, m, :], MAGIC, -1.0, ALU.subtract, ALU.max).then_inc(chain, 1)
                            dve.wait_ge(chain, 2 * m + 2)
                            dve.tensor_scalar(wt[:, m, :], w32[:, m, :], 1.0, None, ALU.min).then_inc(s_wt, 1)
                        dve.tensor_scalar(k_gate[:, :], qmax[:, :], wmean[:, 0:1], None, ALU.mult).then_inc(k_ok, 1)
                        dve.tensor_scalar(k_up[:, :], qmax[:, :], wmean[:, 1:2], None, ALU.mult).then_inc(k_ok, 1)
                        dve.wait_ge(k_ok, 2)

                        def add(j):
                            dve.wait_ge(d_ok, j + 1)
                            dve.wait_ge(chain2, 5 * j + 5)
                            dve.scalar_tensor_tensor(X[:, j, :], pd[:, :, :].rearrange("p h n -> p (h n)"), k_down[:, j:j + 1],
                                                     X[:, j, :], ALU.mult, ALU.add).then_inc(x_ok, 1)

                        for j in range(NT):
                            v = gk[:, j % 2, :]
                            dve.wait_ge(g_free, j + 1)
                            dve.scalar_tensor_tensor(v, pu[:, :], k_up[:, j:j + 1], v, ALU.mult, ALU.mult).then_inc(v_ok, 1)
                            quantise(dve, v, v_ok, j + 1, vmax[:, j:j + 1], vscale[:, j:j + 1], gq[:, j % 2, :], chain2, 5 * j, q_ok)
                            dve.tensor_scalar(k_down[:, j:j + 1], vmax[:, j:j + 1], wmean[:, 2:3], None, ALU.mult).then_inc(chain2, 1)
                            if j:
                                add(j - 1)
                        add(NT - 1)

        gather("l0", None)
        end_phase()
        early.close()
        if stop > 2:
            project("l0", [l0_w], 8, None, False)
            end_phase()
        if stop > 3:
            normalise("m", False)
            end_phase()
            route()
            end_phase()
        if stop > 4:
            experts()
            end_phase()
        if stop > 5:
            normalise("s", False)
            end_phase()
            gather("s0", None)
            end_phase()
            project("s0", [s0, n0], 0, c0, True)
            end_phase()
            turn_hidden("h")
            end_phase()
            gather("s1", None)
            end_phase()
            project("s1", [s1, n1], 0, c1, False)
            end_phase()
        if stop > 6:
            normalise("f", True)
            end_phase()
            ternary_ffn()
            end_phase()

        x_out = sem("x_out")
        with nc.Block() as block:
            @block.sync
            def _(sp):
                sp.dma_start(out[0:(NT - 1) * P, :].rearrange("(j p) d -> p j d", p=P), X[:, 0:NT - 1, :]).then_inc(x_out, 16)
                sp.dma_start(out[(NT - 1) * P:NODES, :], X[0:LAST, NT - 1, :]).then_inc(x_out, 16)
                sp.wait_ge(x_out, 32)


def kernel(**inputs):
    import numpy as np
    import concourse.bacc as bacc
    from concourse.bass_utils import run_bass_kernel_spmd as run

    nc = bacc.Bacc("TRN2", target_bir_lowering=False, num_devices=1)

    def chunks(e):
        padded = np.full(CHP * P, NOWHERE, e.dtype)
        padded[:EDGES] = e
        return padded.reshape(CHP, P).T

    laid = {
        "x": inputs["x"], "src": chunks(np.asarray(inputs["src"])), "dst": chunks(np.asarray(inputs["dst"])),
        "l0_w": np.asarray(inputs["L0_gnn_W"]).T, "l0_b": inputs["L0_gnn_b"],
        "gate": np.asarray(inputs["L0_ffn_gate_w"]).T,
        "w1": np.asarray(inputs["L0_ffn_w1"]).transpose(1, 2, 0).reshape(8 * D, HALF),
        "b1": inputs["L0_ffn_b1"],
        "w2": np.asarray(inputs["L0_ffn_w2"]).transpose(1, 2, 0).reshape(8 * HALF, D),
        "b2": inputs["L0_ffn_b2"],
        "s0": inputs["L1_gnn_W_self0"], "n0": inputs["L1_gnn_W_neigh0"], "c0": inputs["L1_gnn_b0"],
        "s1": inputs["L1_gnn_W_self1"], "n1": inputs["L1_gnn_W_neigh1"], "c1": inputs["L1_gnn_b1"],
        "wg": np.asarray(inputs["L1_ffn_w_gate"]).T, "wu": np.asarray(inputs["L1_ffn_w_up"]).T,
        "wd": np.asarray(inputs["L1_ffn_w_down"]).T,
    }
    laid = {k: np.ascontiguousarray(v) for k, v in laid.items()}
    aps = {k: nc.dram_tensor(k, v.shape, mybir.dt.from_np(v.dtype), kind="ExternalInput").ap() for k, v in laid.items()}
    out = nc.dram_tensor("out", (NODES, D), F32, kind="ExternalOutput").ap()
    gnn_ffn_kernel(nc, **aps, out=out, stop=STOP)
    r = run(nc, [laid], core_ids=[0])
    return r.results[0]["out"]


STOP = 9
```

```python
from contextlib import ExitStack

import concourse.bass as bass
from concourse import mybir

P = 128
F32 = mybir.dt.float32
F16 = mybir.dt.float16
I32 = mybir.dt.int32
U32 = mybir.dt.uint32
ALU = mybir.AluOpType
ACT = mybir.ActivationFunctionType
AX_X = mybir.AxisListType.X

NODES, D = 1250, 1024
EDGES = 20000
NT = -(-NODES // P)
NP = NT * P
LAST = NODES - (NT - 1) * P
CH = -(-EDGES // P)
KD = D // P
STEP = 4
CHP = CH + STEP - 1
TURNS = -(-CH // STEP)
NOWHERE = 2047
ST = (2 * NODES + 8 * (P - 1)) // P
ST_LEAST = -(-2 * NODES // P)
EARLY = 4
HALF = 512
COLS = [(0, 512), (512, 512), (1024, 256)]
EPS = 1e-5
MAGIC = 12582912.0
AS = 8.0
WS = 64.0


def gnn_ffn_kernel(nc, x, src, dst, l0_w, l0_b, gate, w1, b1, w2, b2, s0, n0, c0, s1, n1, c1, wg, wu, wd, out):
    ctx = ExitStack()
    with ctx:
        def sb(name, shape, dt, c=ctx):
            return c.enter_context(nc.sbuf_tensor(name, shape, dt))

        held = []

        def sem(name):
            held.append(nc.alloc_semaphore(name))
            return held[-1]

        def end_phase():
            nc.clear_and_free_semaphores(held)
            nc.all_engine_barrier()
            held.clear()

        X = sb("X", [P, NT, D], F32)
        BIG = sb("BIG", [P, 61440], F16)
        FEAT = BIG[:, 0:40960].rearrange("p (k h n) -> p k h n", k=16, h=2)
        N = BIG[:, 40960:61440].rearrange("p (j h d) -> p j h d", j=NT, h=2)
        whole_early = BIG[:, 57344:61440].rearrange("p (j d) -> p j d", j=EARLY)
        B0 = BIG[:, 0:NT * NP].rearrange("p (t n) -> p t n", t=NT)
        B1 = sb("B1", [P, NT, NP], F16)
        ident = sb("ident", [P, P], F16)
        ident32 = sb("ident32", [P, P], F32)
        ones32 = sb("ones32", [P, P], F32)
        bn = sb("bn", [P, NT, 2, 6], F32)
        mv = sb("mv", [P, NT, 2], F32)
        rstd = sb("rstd", [P, NT], F32)
        shift = sb("shift", [P, NT], F32)
        minus_half = sb("minus_half", [P, NT], F32)
        indeg = sb("indeg", [P, NT], F32)
        outdeg = sb("outdeg", [P, NT], F32)
        dinv = sb("dinv", [P, NT], F32)
        dinv8 = sb("dinv8", [P, NT], F32)
        dinv_back = sb("dinv_back", [P, NT], F32)
        degi = sb("degi", [P, NT], F32)
        chosen = sb("chosen", [P, NT, 8], F32)

        qmax = sb("qmax", [P, NT], F32)
        qscale = sb("qscale", [P, NT], F32)
        weight = sb("weight", [P, 2, NT], F32)
        slot_i = sb("slot_i", [P, 2, NT], U32)
        node_i = sb("node_i", [P, ST + 1], U32)
        bounds_i = sb("bounds_i", [P, 9], I32)
        wmean = sb("wmean", [P, 3], F32)
        wscale = sb("wscale", [P, 3], F32)
        wsum = sb("wsum", [P, 6], F32)
        b1_rows = BIG[:, 58368:58880]
        b2_rows = BIG[:, 58880:59904]
        of_expert = BIG[:, 59904:60928].rearrange("p (e n) -> p e n", e=8)
        rows = nc.dram_tensor("rows", (NP, 2 * D), F16, kind="Internal").ap()
        results = nc.dram_tensor("results", (ST * P, D), F32, kind="Internal").ap()

        def moments_of(dve, j, n, stats, moments):
            for h in range(2):
                dve.bn_stats(bn[:, j, h, :], X[:, j, h * HALF:(h + 1) * HALF]).then_inc(stats, 1)
            dve.wait_ge(stats, 2 * n + 2)
            dve.bn_aggr(mv[:, j, :], bn[:, j, :, :]).then_inc(moments, 1)

        def root_of(pool, j, n, moments, root, scale=AS):
            pool.wait_ge(moments, n + 1)
            pool.tensor_scalar(rstd[:, j:j + 1], mv[:, j, 1:2], 1.0, EPS, ALU.mult, ALU.add).then_inc(root, 1)
            pool.tensor_scalar(shift[:, j:j + 1], mv[:, j, 0:1], -1.0, 0.0, ALU.mult, ALU.add).then_inc(root, 1)
            pool.wait_ge(root, 5 * n + 2)
            pool.tensor_tensor(rstd[:, j:j + 1], rstd[:, j:j + 1], minus_half[:, j:j + 1], ALU.pow).then_inc(root, 1)
            pool.wait_ge(root, 5 * n + 3)
            pool.tensor_scalar(rstd[:, j:j + 1], rstd[:, j:j + 1], scale, 0.0, ALU.mult, ALU.add).then_inc(root, 1)
            pool.wait_ge(root, 5 * n + 4)
            pool.tensor_tensor(shift[:, j:j + 1], shift[:, j:j + 1], rstd[:, j:j + 1], ALU.mult).then_inc(root, 1)

        with ExitStack() as c:
            h32 = BIG[:, 20480:40960].bitcast(F32).rearrange("p (j d) -> p j d", j=NT)
            tmp = BIG[:, 12800:20480]
            iota = tmp[:, 0:1280]
            hot_src = tmp[:, NP:(STEP + 1) * NP].rearrange("p (s n) -> p s n", s=STEP)
            hot_dst = tmp[:, 6400:6400 + STEP * P].rearrange("p (s n) -> p s n", s=STEP)
            edges_i = tmp[:, 6912:6912 + 4 * CHP].bitcast(I32).rearrange("p (a c) -> p a c", a=2)
            w = BIG[:, 40960:57344].rearrange("p (k h d) -> p k h d", k=KD, h=2)
            above = BIG[:, 57344:57344 + 11 * CH].rearrange("p (t c) -> p t c", t=11)
            b1e = B1.rearrange("p j n -> p (j n)")
            n32 = b1e[:, 0:4096].bitcast(F32).rearrange("p (s d) -> p s d", s=2)
            n16 = b1e[:, 4096:6144].rearrange("p (h d) -> p h d", h=2)
            w_stage = BIG[:, 20480:36864].bitcast(F32).rearrange("p (k d) -> p k d", k=KD)
            xT = [b1e[:, 6144:8192].rearrange("p (h k n) -> p h k n", h=2, k=KD),
                  BIG[:, 59392:61440].rearrange("p (h k n) -> p h k n", h=2, k=KD)]
            zero = sb("zero", [P, HALF], F16, c)
            edges = sb("edges", [P, 2, CHP], F32, c)
            band = sb("band", [P, 24], F16, c)
            chunk_lo = sb("chunk_lo", [P, CH], F32, c)
            chunk_hi = sb("chunk_hi", [P, CH], F32, c)
            pick = sb("pick", [NT, 2, CH], F32, c)
            span = sb("span", [NT, 2], F32, c)
            span_i = sb("span_i", [NT, 2], I32, c)
            b_stage = sb("b_stage", [1, D], F32, c)
            b_rows = sb("b_rows", [64, D], F16, c)
            one = sb("one_l0", [64, P], F16, c)
            ps = c.enter_context(nc.psum_tensor("ps_l0", [P, 8, HALF], F32))
            flat = ps.rearrange("p b n -> p (b n)")
            cnt = flat[:, 0:NP]
            x_ps = [ps[:, 3, :].bitcast(F16), ps[:, 4, :].bitcast(F16)]
            h_ps = ps[:, 5:7, :]
            there = ps[:, 7, :]
            flip = [flat[:, 0:1024].bitcast(F16)[:, 0:NP], flat[:, 1024:2048].bitcast(F16)[:, 0:NP]]

            names = "e_in x_in x_pad consts edges_f above_ok there_ok picked span_ok flipped flip_free deg_ok dinv_ok hot hot_used"
            (e_in, x_in, x_pad, consts, edges_f, above_ok, there_ok, picked, span_ok, flipped, flip_free, deg_ok, dinv_ok, hot,
             hot_used) = (sem(n) for n in names.split())
            names = "cnt_full cnt_free stats moments root n32_ok hi_ok lo_ok turned x_hi x_lo w_hi w_lo b_in b_ok h_ok h_out filled"
            (cnt_full, cnt_free, stats, moments, root, n32_ok, hi_ok, lo_ok, turned, x_hi, x_lo, w_hi, w_lo, b_in, b_ok, h_ok, h_out,
             filled) = (sem(n) for n in names.split())
            w_in = [sem(f"w_in{r}_l0") for r in range(2)]

            with nc.Block() as block:
                @block.sync
                def _(sp):
                    sp.dma_start(edges_i[:, 0, :], src).then_inc(e_in, 16)
                    sp.dma_start(edges_i[:, 1, :], dst).then_inc(e_in, 16)
                    sp.dma_start(X[:, 0:3, :], x[0:3 * P, :].rearrange("(j p) d -> p j d", p=P)).then_inc(x_in, 16)
                    sp.dma_start(b_stage[:, :], l0_b.rearrange("(a d) -> a d", a=1)).then_inc(b_in, 16)
                    for r in range(2):
                        k = slice(r * KD // 2, (r + 1) * KD // 2)
                        sp.dma_start(w_stage[:, k, :], l0_w[r * D // 2:(r + 1) * D // 2, :].rearrange("(k p) d -> p k d", p=P)).then_inc(w_in[r], 16)
                    sp.wait_ge(x_in, 16)
                    sp.dma_start(X[:, 3:NT - 1, :], x[3 * P:(NT - 1) * P, :].rearrange("(j p) d -> p j d", p=P)).then_inc(x_in, 16)
                    sp.wait_ge(x_pad, 1)
                    sp.wait_ge(x_in, 32)
                    sp.dma_start(X[0:LAST, NT - 1, :], x[(NT - 1) * P:NODES, :]).then_inc(x_in, 16)
                    sp.dma_start(results[ST_LEAST * P:ST * P, :], x[0:(ST - ST_LEAST) * P, :]).then_inc(filled, 16)
                    sp.wait_ge(filled, 16)

                @block.gpsimd
                def _(pool):
                    pool.iota(iota, [[1, NP]], base=0, channel_multiplier=0, allow_small_or_imprecise_dtypes=True).then_inc(hot_used, STEP)
                    pool.memset(band[:, :], 0.0).then_inc(consts, 1)
                    pool.memset(zero[:, :], 0.0).then_inc(consts, 1)
                    pool.iota(chunk_lo[:, :], [[1, CH]], base=-CH, channel_multiplier=0, allow_small_or_imprecise_dtypes=True).then_inc(consts, 1)
                    pool.iota(chunk_hi[:, :], [[1, CH]], base=1, channel_multiplier=0, allow_small_or_imprecise_dtypes=True).then_inc(consts, 1)
                    pool.wait_ge(consts, 1)
                    pool.memset(band[:, 10:11], -1.0).then_inc(consts, 1)
                    pool.memset(band[:, 11:12], 1.0).then_inc(consts, 1)
                    pool.memset(minus_half[:, :], -0.5).then_inc(consts, 1)
                    pool.memset(ident[:, :], 0.0).then_inc(consts, 1)
                    pool.memset(ident32[:, :], 0.0).then_inc(consts, 1)
                    pool.memset(ones32[:, :], 1.0).then_inc(consts, 1)
                    pool.wait_ge(consts, 10)
                    for m in (ident, ident32):
                        pool.affine_select(out=m[:, :], in_=m[:, :], compare_op=ALU.not_equal, fill=1.0,
                                           base=0, pattern=[[-1, P]], channel_multiplier=1).then_inc(consts, 1)
                    for j in range(NT):
                        root_of(pool, j, j, moments, root)
                    pool.wait_ge(deg_ok, 1)
                    pool.tensor_tensor(dinv[:, :], dinv[:, :], minus_half[:, :], ALU.pow).then_inc(dinv_ok, 1)

                @block.scalar
                def _(act):
                    def norm(j):
                        act.wait_ge(root, 5 * j + 5)
                        if j >= 2:
                            act.wait_ge(lo_ok, j - 1)
                        act.activation(n32[:, j % 2, :], X[:, j, :], ACT.Identity, bias=shift[:, j:j + 1], scale=rstd[:, j:j + 1]).then_inc(n32_ok, 1)
                        act.wait_ge(n32_ok, j + 1)
                        if j:
                            act.wait_ge(turned, j)
                        act.activation(n16[:, 0, :], n32[:, j % 2, :], ACT.Copy).then_inc(hi_ok, 1)

                    def x_out(j):
                        act.wait_ge(turned, j + 1)
                        act.activation(xT[j % 2][:, 0, :, :].rearrange("p k n -> p (k n)"), x_ps[0], ACT.Copy).then_inc(x_hi, 1)

                    act.wait_ge(b_in, 16)
                    act.wait_ge(b_ok, 1)
                    act.activation(b_rows[0:1, :], b_stage[:, :], ACT.Copy, scale=AS * WS).then_inc(b_ok, 1)
                    norm(0)
                    for k in range(KD):
                        act.wait_ge(w_in[k // 4], 16)
                        act.activation(w[:, k, 0, :], w_stage[:, k, :], ACT.Copy, scale=WS).then_inc(w_hi, 1)
                    x_out(0)
                    norm(1)
                    for t in range(NT):
                        act.wait_ge(cnt_full, t + 1)
                        act.activation(B0[:, t, :], cnt, ACT.Copy, accum_out=indeg[:, t:t + 1]).then_inc(cnt_free, 1)
                        if t + 1 < NT:
                            x_out(t + 1)
                        if t + 2 < NT:
                            norm(t + 2)
                        act.wait_ge(h_ok, t + 1)
                        act.activation(h32[:, t, :], h_ps.rearrange("p b n -> p (b n)"), ACT.Copy, scale=1 / (AS * WS)).then_inc(h_out, 1)
                    for j in range(NT):
                        act.wait_ge(flipped, j + 1)
                        act.activation(B1[:, j, :], flip[j % 2], ACT.Copy, accum_out=outdeg[:, j:j + 1]).then_inc(flip_free, 1)

                @block.tensor
                def _(pe):
                    def turn(j):
                        pe.wait_ge(lo_ok, j + 1)
                        if j:
                            pe.wait_ge(x_hi, j)
                            pe.wait_ge(x_lo, j)
                        for h in range(2):
                            for k in range(KD):
                                mm = pe.transpose(x_ps[h][:, k * P:(k + 1) * P], n16[:, h, k * P:(k + 1) * P], ident[:, :])
                        mm.then_inc(turned, 1)

                    pe.wait_ge(consts, 6)
                    for t in range(NT + 1):
                        pe.wait_ge(above_ok, t + 1)
                        mm = pe.matmul(there[0:NT, 0:CH], band[:, 11 - t:11 - t + NT], above[:, t, :], start=(t == 0), stop=(t == NT))
                    mm.then_inc(there_ok, 1)
                    pe.wait_ge(consts, 12)
                    turn(0)
                    pe.wait_ge(span_ok, 1)
                    done = 0
                    for t in range(NT):
                        n = pe.value_load(span_i[t:t + 1, 1:2], min_val=1, max_val=TURNS)
                        if t:
                            pe.wait_ge(cnt_free, t)
                        for c_, width in COLS:
                            pe.matmul(cnt[:, c_:c_ + width], zero[:, 0:P], zero[:, 0:width], start=True, stop=False)
                        with pe.Fori(done, done + n) as turn_:
                            for u in range(STEP):
                                pe.wait_ge(hot, STEP * turn_ + u + 1)
                                for c_, width in COLS:
                                    mm = pe.matmul(cnt[:, c_:c_ + width], hot_dst[:, u, :], hot_src[:, u, c_:c_ + width],
                                                   start=False, stop=False)
                                mm.then_inc(hot_used, 1)
                        for c_, width in COLS:
                            mm = pe.matmul(cnt[:, c_:c_ + width], zero[:, 0:P], zero[:, 0:width], start=False, stop=True)
                        mm.then_inc(cnt_full, 1)
                        done = pe.snap(done + n)
                        if t + 1 < NT:
                            turn(t + 1)
                        if t == 0:
                            pe.wait_ge(w_lo, KD)
                            pe.wait_ge(b_ok, 4)
                        else:
                            pe.wait_ge(h_out, t)
                        pe.wait_ge(x_hi, t + 1)
                        pe.wait_ge(x_lo, t + 1)
                        for h in range(2):
                            cols = slice(h * HALF, (h + 1) * HALF)
                            pe.matmul(h_ps[:, h, :], one[:, :], b_rows[:, cols], start=True, stop=False)
                            for k in range(KD):
                                for a, b in ((0, 0), (0, 1), (1, 0)):
                                    mm = pe.matmul(h_ps[:, h, :], xT[t % 2][:, a, k, :], w[:, k, b, cols], start=False, stop=(k == KD - 1 and a == 1))
                        mm.then_inc(h_ok, 1)

                    pe.wait_ge(cnt_free, NT)
                    for j in range(NT):
                        if j >= 2:
                            pe.wait_ge(flip_free, j - 1)
                        for t in range(NT):
                            mm = pe.transpose(flip[j % 2][:, t * P:(t + 1) * P], B0[:, t, j * P:(j + 1) * P], ident[:, :])
                        mm.then_inc(flipped, 1)

                @block.vector
                def _(dve):
                    def moment(j):
                        if j in (0, 3, NT - 1):
                            dve.wait_ge(x_in, 16 * (1 + (j >= 3) + (j == NT - 1)))
                        moments_of(dve, j, j, stats, moments)

                    def split(j):
                        dve.wait_ge(hi_ok, j + 1)
                        dve.tensor_tensor(n16[:, 1, :], n32[:, j % 2, :], n16[:, 0, :], ALU.subtract).then_inc(lo_ok, 1)

                    def x_out(j):
                        dve.wait_ge(turned, j + 1)
                        dve.tensor_copy(xT[j % 2][:, 1, :, :].rearrange("p k n -> p (k n)"), x_ps[1]).then_inc(x_lo, 1)

                    dve.memset(X[96:P, NT - 1, :], 0.0).then_inc(x_pad, 1)
                    dve.memset(b_rows[:, :], 0.0).then_inc(b_ok, 1)
                    dve.memset(one[:, :], 1.0).then_inc(b_ok, 1)
                    dve.wait_ge(e_in, 32)
                    dve.tensor_copy(edges[:, :, :], edges_i).then_inc(edges_f, 1)
                    dve.wait_ge(edges_f, 1)
                    for t in range(NT + 1):
                        dve.tensor_scalar(above[:, t, :], edges[:, 1, 0:CH], float(P * t), None, ALU.is_ge).then_inc(above_ok, 1)
                    moment(0)
                    moment(1)
                    moment(2)
                    dve.wait_ge(b_ok, 3)
                    dve.scalar_tensor_tensor(b_rows[32:33, :], b_stage[:, :], AS * WS, b_rows[0:1, :], ALU.mult, ALU.subtract).then_inc(b_ok, 1)
                    split(0)
                    dve.wait_ge(there_ok, 1)
                    dve.wait_ge(consts, 4)
                    dve.scalar_tensor_tensor(pick[:, 0, :], there[0:NT, 0:CH], 0.0, chunk_lo[0:NT, :], ALU.is_gt, ALU.mult).then_inc(picked, 1)
                    dve.scalar_tensor_tensor(pick[:, 1, :], there[0:NT, 0:CH], 0.0, chunk_hi[0:NT, :], ALU.is_gt, ALU.mult).then_inc(picked, 1)
                    dve.wait_ge(picked, 2)
                    dve.tensor_reduce(span[:, 0:1], pick[:, 0, :], AX_X, ALU.min).then_inc(picked, 1)
                    dve.tensor_reduce(span[:, 1:2], pick[:, 1, :], AX_X, ALU.max).then_inc(picked, 1)
                    dve.wait_ge(picked, 4)
                    dve.tensor_scalar(span[:, 0:1], span[:, 0:1], float(CH), float(CH - 1), ALU.add, ALU.min).then_inc(picked, 1)
                    dve.wait_ge(picked, 5)
                    dve.scalar_tensor_tensor(span[:, 1:2], span[:, 0:1], -1.0, span[:, 1:2], ALU.mult, ALU.add).then_inc(picked, 1)
                    dve.wait_ge(picked, 6)
                    dve.tensor_scalar(span[:, 1:2], span[:, 1:2], 1.0, 1 / STEP, ALU.max, ALU.mult).then_inc(picked, 1)
                    dve.wait_ge(picked, 7)
                    dve.tensor_scalar(span[:, 1:2], span[:, 1:2], (STEP - 1) / (2 * STEP), MAGIC, ALU.add, ALU.add).then_inc(picked, 1)
                    dve.wait_ge(picked, 8)
                    dve.tensor_scalar(span[:, 1:2], span[:, 1:2], MAGIC, None, ALU.subtract).then_inc(picked, 1)
                    dve.wait_ge(picked, 9)
                    dve.tensor_copy(span_i[:, :], span[:, :]).then_inc(span_ok, 1)
                    for k in range(KD):
                        dve.wait_ge(w_hi, k + 1)
                        dve.scalar_tensor_tensor(w[:, k, 1, :], w_stage[:, k, :], WS, w[:, k, 0, :], ALU.mult, ALU.subtract).then_inc(w_lo, 1)
                    x_out(0)
                    split(1)
                    dve.wait_ge(span_ok, 1)
                    done = 0
                    for t in range(NT):
                        lo = dve.value_load(span_i[t:t + 1, 0:1], min_val=0, max_val=CH - 1)
                        n = dve.value_load(span_i[t:t + 1, 1:2], min_val=1, max_val=TURNS)
                        back = dve.snap(lo - STEP * done)
                        with dve.Fori(done, done + n) as turn_:
                            first = nc.s_assert_within(dve.snap(STEP * turn_ + back), 0, CH - 1,
                                                       skip_runtime_bounds_check_because="the turns of a tile start in its span of chunks")
                            for u in range(STEP):
                                dve.wait_ge(hot_used, STEP * turn_ + u + 1)
                                dve.tensor_scalar(hot_dst[:, u, :], iota[:, t * P:(t + 1) * P], edges[:, 1, bass.ds(first + u, 1)], None, ALU.is_equal)
                                dve.tensor_scalar(hot_src[:, u, :], iota, edges[:, 0, bass.ds(first + u, 1)], None, ALU.is_equal).then_inc(hot, 1)
                        done = dve.snap(done + n)
                        if t + 1 < NT:
                            x_out(t + 1)
                        if t + 3 < NT:
                            moment(t + 3)
                        if t + 2 < NT:
                            split(t + 2)
                    dve.wait_ge(flip_free, NT)
                    dve.tensor_scalar(dinv[:, :], outdeg[:, :], 1.0, None, ALU.add).then_inc(deg_ok, 1)
                    for j in range(NT):
                        own = B0[:, j, j * P:(j + 1) * P]
                        dve.tensor_tensor(own, own, ident[:, :], ALU.add).then_inc(deg_ok, 1)
                    dve.wait_ge(dinv_ok, 1)
                    dve.tensor_scalar(dinv8[:, :], dinv[:, :], AS, None, ALU.mult).then_inc(deg_ok, 1)
                    dve.tensor_scalar(dinv_back[:, :], dinv[:, :], 1 / AS, None, ALU.mult).then_inc(deg_ok, 1)
        end_phase()

        with ExitStack() as c:
            h32 = BIG[:, 20480:40960].bitcast(F32).rearrange("p (j d) -> p j d", j=NT)
            n32 = BIG[:, 12800:14848].bitcast(F32)
            n16 = BIG[:, 14848:18944].rearrange("p (s h d) -> p s h d", s=2, h=2)
            ps = c.enter_context(nc.psum_tensor("ps_sum", [P, 8, HALF], F32))
            x_ps = [ps[:, 6, :].bitcast(F16), ps[:, 7, :].bitcast(F16)]
            g_hi, g_lo, summed, bank_free, stats, moments, root, n32_ok, hi_ok, lo_ok, turned, x_hi, x_lo, = (
                sem(f"sum_{n}") for n in "g_hi g_lo summed bank_free stats moments root n32_ok hi_ok lo_ok turned x_hi x_lo".split())
            stored = [sem(f"rows_stored{s}") for s in range(2)]

            with nc.Block() as block:
                @block.sync
                def _(sp):
                    for j in range(NT):
                        sp.wait_ge(lo_ok, j + 1)
                        sp.dma_start(rows[j * P:(j + 1) * P, :], n16[:, j % 2, :, :].rearrange("p h d -> p (h d)")).then_inc(stored[j % 2], 16)
                    for s in range(2):
                        sp.wait_ge(stored[s], 16 * (NT // 2))

                @block.gpsimd
                def _(pool):
                    for j in range(NT):
                        root_of(pool, j, j, moments, root)

                @block.tensor
                def _(pe):
                    def product(n, h, m, a):
                        return pe.matmul(ps[:, (2 * n + h) % 6, :], B0[:, m, n * P:(n + 1) * P], N[:, m, a, h * HALF:(h + 1) * HALF],
                                         start=(m == 0 and a == 0), stop=(m == NT - 1 and a == 1))

                    def turn(j):
                        pe.wait_ge(lo_ok, j + 1)
                        if j:
                            pe.wait_ge(x_hi, j)
                            pe.wait_ge(x_lo, j)
                        for h in range(2):
                            for k in range(KD):
                                mm = pe.transpose(x_ps[h][:, k * P:(k + 1) * P], n16[:, j % 2, h, k * P:(k + 1) * P], ident[:, :])
                        mm.then_inc(turned, 1)

                    for m in range(NT):
                        pe.wait_ge(g_lo, m + 1)
                        for n in range(3):
                            for h in range(2):
                                for a in range(2):
                                    mm = product(n, h, m, a)
                                if m == NT - 1:
                                    mm.then_inc(summed, 1)
                    for n in range(3, NT):
                        for h in range(2):
                            pe.wait_ge(bank_free, 2 * n + h - 5)
                            for m in range(NT):
                                for a in range(2):
                                    mm = product(n, h, m, a)
                            mm.then_inc(summed, 1)
                        turn(n - 3)
                    for j in range(NT - 3, NT):
                        turn(j)

                @block.scalar
                def _(act):
                    for j in range(NT):
                        act.activation(N[:, j, 0, :], h32[:, j, :], ACT.Copy, scale=dinv8[:, j:j + 1]).then_inc(g_hi, 1)

                    def put(j):
                        act.wait_ge(turned, j + 1)
                        if j == 0:
                            act.wait_ge(g_lo, NT)
                        act.activation(FEAT[:, 8:16, 0, j * P:(j + 1) * P], x_ps[0].rearrange("p (k n) -> p k n", k=KD), ACT.Copy).then_inc(x_hi, 1)

                    for j in range(NT):
                        act.wait_ge(root, 5 * j + 5)
                        if j:
                            act.wait_ge(lo_ok, j)
                        act.activation(n32, X[:, j, :], ACT.Identity, bias=shift[:, j:j + 1], scale=rstd[:, j:j + 1]).then_inc(n32_ok, 1)
                        act.wait_ge(n32_ok, j + 1)
                        if j >= 2:
                            act.wait_ge(turned, j - 1)
                            act.wait_ge(stored[j % 2], 16 * (j // 2))
                        act.activation(n16[:, j % 2, 0, :], n32, ACT.Copy).then_inc(hi_ok, 1)
                        if j:
                            put(j - 1)
                    put(NT - 1)

                @block.vector
                def _(dve):
                    for j in range(NT):
                        dve.wait_ge(g_hi, j + 1)
                        dve.scalar_tensor_tensor(N[:, j, 1, :], h32[:, j, :], dinv8[:, j:j + 1], N[:, j, 0, :], ALU.mult, ALU.subtract).then_inc(g_lo, 1)

                    def arrive(j):
                        for h in range(2):
                            u = 2 * j + h
                            cols = slice(h * HALF, (h + 1) * HALF)
                            dve.wait_ge(summed, u + 1)
                            dve.scalar_tensor_tensor(X[:, j, cols], ps[:, u % 6, :], dinv_back[:, j:j + 1], X[:, j, cols], ALU.mult, ALU.add).then_inc(bank_free, 1)
                        dve.wait_ge(bank_free, 2 * j + 2)
                        moments_of(dve, j, j, stats, moments)

                    def put(j):
                        dve.wait_ge(turned, j + 1)
                        dve.tensor_copy(FEAT[:, 8:16, 1, j * P:(j + 1) * P], x_ps[1].rearrange("p (k n) -> p k n", k=KD)).then_inc(x_lo, 1)

                    arrive(0)
                    for j in range(NT):
                        if j + 1 < NT:
                            arrive(j + 1)
                        dve.wait_ge(hi_ok, j + 1)
                        dve.tensor_tensor(n16[:, j % 2, 1, :], n32, n16[:, j % 2, 0, :], ALU.subtract).then_inc(lo_ok, 1)
                        if j:
                            put(j - 1)
                    put(NT - 1)
        end_phase()

        def sage(tag, mats, bias, hidden):
            turn = not hidden
            K = KD * len(mats)
            Q = K // 4
            with ExitStack() as c:
                stage = sb(f"stage_{tag}", [P, 2, HALF], F32, c)
                wr = sb(f"wr_{tag}", [P, 4, 2, HALF], F16, c)
                bst = sb(f"bst_{tag}", [64, D], F16, c)
                one = sb(f"one_{tag}", [64, P], F16, c)
                b32 = stage[0:1, 0:2, :].rearrange("p a n -> p (a n)")
                ps = c.enter_context(nc.psum_tensor(f"ps_{tag}", [P, 8, HALF], F32))
                flat = ps.rearrange("p b n -> p (b n)")
                names = "summed scaled hi_w lo_w w_hi w_lo w_used out_ok out_free b_in b_ok"
                summed, scaled_ok, hi_w, lo_w, w_hi, w_lo, w_used, out_ok, out_free, b_in, b_ok = (sem(f"{n}_{tag}") for n in names.split())
                w_in = [sem(f"w_in{r}_{tag}") for r in range(4)]
                if hidden:
                    h_ok, l_ok = sem(f"h_ok_{tag}"), sem(f"l_ok_{tag}")
                else:
                    w32 = BIG[:, 40960:57344].bitcast(F32).rearrange("p (m n) -> p m n", m=2)
                    down32 = B1.rearrange("p j n -> p (j n)")[:, 4608:12800].bitcast(F32)
                    wt = B1.rearrange("p j n -> p (j n)")[:, 0:12288]
                    n32 = w32.rearrange("p m n -> p (m n)")[:, 4096:8192].rearrange("p (j d) -> p j d", j=EARLY)
                    early_stats, early_moments, early_root, early_n32, early_chain, early_rounded, early_ok = (
                        sem(f"early_{n}") for n in "stats moments root n32 chain rounded ok".split())
                    t_in = [sem(f"ternary_in{m}") for m in range(4)]
                    t_sum, t_all, t_mean, t_chain, t_ok = (sem(f"ternary_{n}") for n in "sum all mean chain ok".split())
                    turned, turned_hi, turned_lo = (sem(f"{n}_{tag}") for n in "turned turned_hi turned_lo".split())

                def bank(u):
                    return ps[:, (6 + u) % 8, :]

                def sums(s):
                    return flat[:, s * 3 * HALF:s * 3 * HALF + NP]

                with nc.Block() as block:
                    @block.sync
                    def _(sp):
                        sp.dma_start(b32, bias.rearrange("(a d) -> a d", a=1)).then_inc(b_in, 16)
                        sp.wait_ge(b_ok, 3)
                        for s in range(4):
                            for m, w in enumerate(mats):
                                with sp.Fori(0, 2) as q:
                                    for r in range(4):
                                        n = (s * len(mats) + m) * 8 + q * 4 + r
                                        sp.wait_ge(w_lo, n + 1)
                                        sp.dma_start(stage[:, r % 2, :], w[bass.ds((q * 4 + r) * P, P), (s % 2) * HALF:(s % 2 + 1) * HALF]).then_inc(w_in[r], 16)

                    @block.scalar
                    def _(act):
                        act.wait_ge(b_in, 16)
                        act.wait_ge(b_ok, 1)
                        act.activation(bst[0:1, :], b32, ACT.Copy, scale=AS * WS).then_inc(b_ok, 1)

                        def hi(s, q, r):
                            n = s * K + q * 4 + r
                            act.wait_ge(w_in[r], 16 * (s * Q + q + 1))
                            if not isinstance(q, int) or q:
                                act.wait_ge(w_used, n - 3 - s)
                            elif s and r < 3:
                                act.wait_ge(w_used, n - 2 - s)
                            elif s:
                                act.wait_ge(out_ok, 5 * s)
                            act.activation(wr[:, r, 0, :], stage[:, r % 2, :], ACT.Copy, scale=WS).then_inc(w_hi, 1)

                        def put(j, n):
                            act.wait_ge(turned, n + 1)
                            act.activation(FEAT[:, 0:8, 0, bass.ds(j * P, P)], ps[:, 6, :].bitcast(F16).rearrange("p (k n) -> p k n", k=8),
                                           ACT.Copy).then_inc(turned_hi, 1)

                        def evac(s):
                            if hidden:
                                for i in range(5):
                                    j, h = 5 * (s // 2) + i, s % 2
                                    act.wait_ge(l_ok, 5 * s + i + 1)
                                    act.activation(N[:, j, 0, h * HALF:(h + 1) * HALF], bank(5 * s + i), ACT.Copy).then_inc(h_ok, 1)

                        def early_norm(j):
                            act.wait_ge(early_root, 5 * j + 5)
                            act.wait_ge(t_ok, 4)
                            act.activation(n32[:, j, :], X[:, j, :], ACT.Identity, bias=shift[:, j:j + 1], scale=rstd[:, j:j + 1]).then_inc(early_n32, 1)

                        def magnitude(i):
                            m, half = i // 2, slice((i % 2) * 2048, (i % 2 + 1) * 2048)
                            act.wait_ge(t_in[m], 16)
                            if i:
                                act.wait_ge(t_sum, i)
                            act.activation(wt[:, 0:2048], w32[:, m, half] if m < 2 else down32[:, half], ACT.Abs, accum_out=wsum[:, i:i + 1]).then_inc(t_sum, 1)

                        for r in range(4):
                            hi(0, 0, r)
                        if turn:
                            put(NT - 1, 0)
                        with act.Fori(0, KD // 2) as g:
                            for s in range(2):
                                act.wait_ge(scaled_ok, 2 * g + s + 1)
                                act.activation(FEAT[:, bass.ds(8 + 2 * g + s, 1), 0, :], sums(s), ACT.Copy).then_inc(hi_w, 1)
                                if turn:
                                    put(2 * g + s, 2 * g + s + 1)
                        if turn:
                            put(KD, NT - 1)
                        for s in range(4):
                            if s:
                                for r in range(4):
                                    hi(s, 0, r)
                                evac(s - 1)
                            if turn and s == 0:
                                for q in range(1, Q):
                                    for r in range(4):
                                        hi(s, q, r)
                                        if r % 2:
                                            magnitude(2 * (q - 1) + r // 2)
                            elif turn and s == 3:
                                for q in range(1, Q):
                                    for r in range(4):
                                        hi(s, q, r)
                                        if r % 2 and q > 1:
                                            early_norm(2 * (q - 2) + r // 2)
                            else:
                                with act.Fori(1, Q) as q:
                                    for r in range(4):
                                        hi(s, q, r)
                        evac(3)

                    @block.gpsimd
                    def _(pool):
                        if turn:
                            pool.wait_ge(summed, KD)
                            pool.wait_ge(turned, NT)
                            for m, w in enumerate((wg, wu)):
                                pool.dma_start(w32[:, m, :].rearrange("p (k n) -> p k n", k=8), w.rearrange("(k p) n -> p k n", p=P)).then_inc(t_in[m], 16)
                            pool.dma_start(down32.rearrange("p (k n) -> p k n", k=4), wd.rearrange("(k p) n -> p k n", p=P)).then_inc(t_in[2], 16)
                            pool.wait_ge(t_ok, 2)
                            pool.dma_start(w32[:, 0, :].rearrange("p (k n) -> p k n", k=4), wd.rearrange("(k p) n -> p k n", p=P)).then_inc(t_in[3], 16)
                            for j in range(EARLY):
                                root_of(pool, j, j, early_moments, early_root, 1.0)

                    @block.vector
                    def _(dve):
                        dve.sem_inc(w_lo, 2)
                        dve.sem_inc(lo_w, 2)
                        if turn:
                            dve.sem_inc(turned_hi, 1)
                            dve.sem_inc(turned_lo, 1)
                        dve.memset(bst[:, :], 0.0).then_inc(b_ok, 1)
                        dve.wait_ge(b_ok, 2)
                        dve.scalar_tensor_tensor(bst[32:33, :], b32, AS * WS, bst[0:1, :], ALU.mult, ALU.subtract).then_inc(b_ok, 1)
                        dve.memset(one[:, :], 1.0).then_inc(b_ok, 1)
                        def lo(s, q, r):
                            n = s * K + q * 4 + r
                            dve.wait_ge(w_hi, n + 1)
                            dve.scalar_tensor_tensor(wr[:, r, 1, :], stage[:, r % 2, :], WS, wr[:, r, 0, :], ALU.mult, ALU.subtract).then_inc(w_lo, 1)

                        def put(j, n):
                            dve.wait_ge(turned, n + 1)
                            dve.tensor_copy(FEAT[:, 0:8, 1, bass.ds(j * P, P)], ps[:, 7, :].bitcast(F16).rearrange("p (k n) -> p k n", k=8)).then_inc(turned_lo, 1)

                        def evac(s):
                            for i in range(5):
                                j, h, u = 5 * (s // 2) + i, s % 2, 5 * s + i
                                cols = slice(h * HALF, (h + 1) * HALF)
                                o = bank(u)
                                dve.wait_ge(out_ok, u + 1)
                                if hidden:
                                    dve.tensor_scalar(o, o, 1 / WS, 0.0, ALU.mult, ALU.max).then_inc(l_ok, 1)
                                    dve.wait_ge(h_ok, u + 1)
                                    dve.tensor_tensor(N[:, j, 1, cols], o, N[:, j, 0, cols], ALU.subtract).then_inc(out_free, 1)
                                else:
                                    dve.scalar_tensor_tensor(X[:, j, cols], o, 1 / (AS * WS), X[:, j, cols], ALU.mult, ALU.add).then_inc(out_free, 1)

                        for r in range(4):
                            lo(0, 0, r)
                        if turn:
                            put(NT - 1, 0)
                        with dve.Fori(0, KD // 2) as g:
                            for s in range(2):
                                dve.wait_ge(summed, 2 * g + s + 1)
                                dve.tensor_tensor(sums(s), sums(s), degree_row[:, :], ALU.mult).then_inc(scaled_ok, 1)
                                dve.wait_ge(hi_w, 2 * g + s + 1)
                                dve.tensor_tensor(FEAT[:, bass.ds(8 + 2 * g + s, 1), 1, :], sums(s), FEAT[:, bass.ds(8 + 2 * g + s, 1), 0, :],
                                                  ALU.subtract).then_inc(lo_w, 1)
                                if turn:
                                    put(2 * g + s, 2 * g + s + 1)
                        if turn:
                            put(KD, NT - 1)

                        def means():
                            dve.wait_ge(t_all, 1)
                            dve.tensor_copy(wsum[:, :], ps[:, 0, 0:6]).then_inc(t_mean, 1)
                            dve.wait_ge(t_mean, 1)
                            dve.tensor_reduce(wmean[:, :], wsum.rearrange("p (m h) -> p m h", m=3), AX_X, ALU.add).then_inc(t_mean, 1)
                            dve.wait_ge(t_mean, 2)
                            dve.tensor_scalar(wmean[:, :], wmean[:, :], 1.0 / (D * HALF), 1e-5, ALU.mult, ALU.max).then_inc(t_mean, 1)
                            dve.wait_ge(t_mean, 3)
                            dve.reciprocal(wscale[:, :], wmean[:, :]).then_inc(t_mean, 1)
                            dve.wait_ge(t_mean, 4)

                        def early_whole(j):
                            dve.wait_ge(early_n32, j + 1)
                            scale_to_whole(dve, n32[:, j, :], qmax[:, j:j + 1], qscale[:, j:j + 1], early_chain, 3 * j, early_rounded)
                            dve.wait_ge(early_rounded, j + 1)
                            dve.tensor_scalar(whole_early[:, j, :], n32[:, j, :], MAGIC, 127.0, ALU.subtract, ALU.min).then_inc(early_ok, 1)

                        def ternary(i):
                            m, n = i // 2, (i % 2) * 2048
                            if m == 2:
                                dve.wait_ge(t_in[3], 16)
                            w = w32[:, m % 2, n:n + 2048]
                            o = wt[:, m * 4096 + n:m * 4096 + n + 2048]
                            dve.tensor_scalar(w, w, wscale[:, m:m + 1], MAGIC, ALU.mult, ALU.add).then_inc(t_chain, 1)
                            dve.wait_ge(t_chain, 2 * i + 1)
                            dve.tensor_scalar(o, w, MAGIC, 1.0, ALU.subtract, ALU.min).then_inc(t_chain, 1)
                            dve.wait_ge(t_chain, 2 * i + 2)
                            dve.tensor_scalar(o, o, -1.0, None, ALU.max).then_inc(t_ok, 1)

                        for s in range(4):
                            if turn and s == 2:
                                means()
                            if s:
                                for r in range(4):
                                    lo(s, 0, r)
                                evac(s - 1)
                            if turn and s >= 2:
                                for q in range(1, Q):
                                    for r in range(4):
                                        lo(s, q, r)
                                        if r == 1:
                                            ternary(3 * (s - 2) + q - 1)
                                    if s == 2:
                                        moments_of(dve, q - 1, q - 1, early_stats, early_moments)
                                    elif q == 1:
                                        moments_of(dve, 3, 3, early_stats, early_moments)
                                    else:
                                        early_whole(q - 2)
                            else:
                                with dve.Fori(1, Q) as q:
                                    for r in range(4):
                                        lo(s, q, r)
                        if turn:
                            early_whole(2)
                            early_whole(3)
                        evac(3)

                    @block.tensor
                    def _(pe):
                        def turn_tile(j, n):
                            pe.wait_ge(turned_hi, n + 1)
                            pe.wait_ge(turned_lo, n + 1)
                            for h in range(2):
                                to = ps[:, 6 + h, :].bitcast(F16)
                                for k in range(KD):
                                    mm = pe.transpose(to[:, k * P:(k + 1) * P], N[:, bass.ds(j, 1), h, k * P:(k + 1) * P], ident[:, :])
                            mm.then_inc(turned, 1)

                        if turn:
                            turn_tile(NT - 1, 0)
                        with pe.Fori(0, KD // 2) as g:
                            for s in range(2):
                                pe.wait_ge(lo_w, 2 * g + s + 1)
                                f = (2 * g + s) * P
                                for j in range(NT):
                                    for h in range(2):
                                        for c_, w in COLS:
                                            mm = pe.matmul(flat[:, s * 3 * HALF + c_:s * 3 * HALF + c_ + w], N[:, j, h, bass.ds(f, P)], B1[:, j, c_:c_ + w],
                                                           start=(j == 0 and h == 0), stop=(j == NT - 1 and h == 1))
                                mm.then_inc(summed, 1)
                                if turn:
                                    turn_tile(2 * g + s, 2 * g + s + 1)
                        if turn:
                            turn_tile(KD, NT - 1)
                        pe.wait_ge(b_ok, 4)
                        if turn:
                            pe.wait_ge(turned_hi, NT + 1)
                            pe.wait_ge(turned_lo, NT + 1)
                        for s in range(4):
                            h = s % 2
                            for k in range(K):
                                pe.wait_ge(w_lo, s * K + k + 1 + 2)
                                if turn and s == 1 and k == KD:
                                    pe.wait_ge(t_sum, 6)
                                    pe.wait_ge(out_free, 3)
                                    pe.matmul(ps[:, 0, 0:6], ones32[:, :], wsum[:, :], start=True, stop=True).then_inc(t_all, 1)
                                if s == 0 and k == K - 1:
                                    pe.wait_ge(lo_w, KD + 2)
                                for i in range(5):
                                    u = 5 * s + i
                                    o = bank(u)
                                    if k == 0:
                                        if u == 2:
                                            pe.wait_ge(lo_w, KD - 1 + 2)
                                        if u >= 8:
                                            pe.wait_ge(out_free, u - 7)
                                        if turn and u == 10:
                                            pe.wait_ge(t_mean, 1)
                                        pe.matmul(o, one[:, :], bst[:, h * HALF:(h + 1) * HALF], start=True, stop=False)
                                    at = slice((5 * (s // 2) + i) * P, (5 * (s // 2) + i + 1) * P)
                                    for a, b in ((0, 0), (0, 1), (1, 0)):
                                        mm = pe.matmul(o, FEAT[:, k, a, at], wr[:, k % 4, b, :], start=False, stop=(k == K - 1 and a == 1))
                                    if k == K - 1:
                                        mm.then_inc(out_ok, 1)
                                if k < K - 1:
                                    mm.then_inc(w_used, 1)

        def merge_and_normalise():
            with ExitStack() as c:
                n32 = FEAT[:, 8:12, :, :].rearrange("p k h n -> p (k h n)")[:, 0:4096].bitcast(F32).rearrange("p (s d) -> p s d", s=2)
                ps = c.enter_context(nc.psum_tensor("tp", [P, 4, 2 * HALF], F16))
                stats, moments, root, n32_ok, lo_ok, turned, out_hi = (
                    sem(f"merge_{n}") for n in "stats moments root n32_ok lo_ok turned out_hi".split())
                fetched = BIG[:, 24576:40960].bitcast(F32).rearrange("p (r d) -> p r d", r=8)
                fetched_in = [sem(f"fetched_in{r}") for r in range(8)]
                added = sem("added")
                diag = sb("degree_diag", [P, NT, P], F32, c)
                row_ps = c.enter_context(nc.psum_tensor("row_ps", [P, 3 * HALF], F32))
                degree_ok, diag_ok, spread, row_ok = (sem(n) for n in "degree_ok diag_ok spread row_ok".split())
                hi_ok, out_lo = sem("merge_hi_ok"), sem("merge_out_lo")
                with nc.Block() as block:
                    @block.gpsimd
                    def _(pool):
                        pool.sem_inc(out_hi, 2)
                        pool.sem_inc(out_lo, 2)

                        def fetch(i):
                            if i >= 8:
                                pool.wait_ge(added, i - 7)
                            pool.indirect_dma_start(fetched[:, i % 8, :], None, results[:, :],
                                                    bass.IndirectOffsetOnAxis(ap=slot_i[:, i % 2, i // 2:i // 2 + 1], axis=0)).then_inc(fetched_in[i % 8], 16)

                        for i in range(8):
                            fetch(i)
                        for j in range(NT):
                            root_of(pool, j, j, moments, root)
                            if j < NT - 4:
                                fetch(2 * j + 8)
                                fetch(2 * j + 9)

                    @block.scalar
                    def _(act):
                        def step(j, before):
                            act.wait_ge(root, 5 * j + 5)
                            if j >= 2:
                                act.wait_ge(lo_ok, j - 1)
                            act.activation(n32[:, j % 2, :], X[:, j, :], ACT.Identity, bias=shift[:, j:j + 1],
                                           scale=rstd[:, j:j + 1]).then_inc(n32_ok, 1)
                            act.wait_ge(n32_ok, j + 1)
                            act.activation(N[:, j, 0, :], n32[:, j % 2, :], ACT.Copy).then_inc(hi_ok, 1)
                            if before:
                                put(j - 1)

                        def put(j):
                            at = FEAT[:, 0:8, 0, j * P:(j + 1) * P]
                            act.wait_ge(turned, 2 * j + 1)
                            act.activation(at, ps[:, (2 * j) % 4, :].rearrange("p (k n) -> p k n", k=8), ACT.Copy).then_inc(out_hi, 1)
                            act.wait_ge(turned, 2 * j + 2)
                            act.activation(FEAT[:, 0:8, 1, j * P:(j + 1) * P], ps[:, (2 * j + 1) % 4, :].rearrange("p (k n) -> p k n", k=8), ACT.Copy).then_inc(out_lo, 1)

                        act.wait_ge(spread, 1)
                        act.activation(degree_row[:, :], row_ps[:, 0:NP], ACT.Copy).then_inc(row_ok, 1)
                        for j in range(NT):
                            step(j, j > 0)
                        put(NT - 1)

                    @block.tensor
                    def _(pe):
                        pe.wait_ge(diag_ok, NT)
                        flat_diag = diag.rearrange("p j n -> p (j n)")
                        for c_, w in COLS:
                            mm = pe.matmul(row_ps[:, c_:c_ + w], ones32[:, :], flat_diag[:, c_:c_ + w], start=True, stop=True)
                        mm.then_inc(spread, 1)
                        for j in range(NT):
                            pe.wait_ge(lo_ok, j + 1)
                            for h in range(2):
                                pe.wait_ge(out_lo if h else out_hi, j + 1)
                                for k in range(KD):
                                    mm = pe.transpose(ps[:, (2 * j + h) % 4, k * P:(k + 1) * P], N[:, j, h, k * P:(k + 1) * P], ident[:, :])
                                mm.then_inc(turned, 1)

                    @block.vector
                    def _(dve):
                        def merge(j):
                            for i in (2 * j, 2 * j + 1):
                                dve.wait_ge(fetched_in[i % 8], 16 * (i // 8 + 1))
                                if i % 2:
                                    dve.wait_ge(added, i)
                                dve.scalar_tensor_tensor(X[:, j, :], fetched[:, i % 8, :], weight[:, i % 2, j:j + 1], X[:, j, :],
                                                         ALU.mult, ALU.add).then_inc(added, 1)
                            dve.wait_ge(added, 2 * j + 2)
                            moments_of(dve, j, j, stats, moments)

                        dve.tensor_scalar(degi[:, :], indeg[:, :], 1.0, None, ALU.max).then_inc(degree_ok, 1)
                        dve.wait_ge(degree_ok, 1)
                        dve.reciprocal(degi[:, :], degi[:, :]).then_inc(degree_ok, 1)
                        dve.wait_ge(degree_ok, 2)
                        for j in range(NT):
                            dve.tensor_scalar(diag[:, j, :], ident32[:, :], degi[:, j:j + 1], None, ALU.mult).then_inc(diag_ok, 1)
                        merge(0)
                        for j in range(NT):
                            if j < NT - 1:
                                merge(j + 1)
                            dve.wait_ge(hi_ok, j + 1)
                            dve.tensor_tensor(N[:, j, 1, :], n32[:, j % 2, :], N[:, j, 0, :], ALU.subtract).then_inc(lo_ok, 1)

        def experts():
            with ExitStack() as c:
                gate32 = sb("gate32", [P, KD, 8], F32, c)
                gate16 = sb("gate16", [P, KD, 2, 8], F16, c)
                both = sb("both", [P, NT, 2, 8], F32, c)
                logit = sb("logit", [P, NT, 8], F32, c)
                best = sb("best", [P, NT, 8], F32, c)
                where = sb("where", [P, NT, 8], U32, c)
                where_f = sb("where_f", [P, NT, 8], F32, c)
                exps = sb("exps", [P, NT, 8], F32, c)
                which = sb("which", [P, 8], F32, c)
                exp_sum = sb("exp_sum", [P, NT], F32, c)
                neg = sb("neg", [P, NT], F32, c)
                b1_32 = sb("b1_32", [8, HALF], F32, c)
                b2_32 = sb("b2_32", [8, D], F32, c)
                node = sb("node", [P, NT], F32, c)
                live = sb("live", [P, NT], F32, c)
                before = sb("before", [P, P], F32, c)
                sel = sb("sel", [P, NT, 8], F32, c)
                per_tile = sb("per_tile", [P, NT, 8], F32, c)
                start = sb("start", [P, 9], F32, c)
                tiles = sb("tiles", [P, 8], F32, c)
                offset = sb("offset", [P, NT, 8], F32, c)
                pair = sb("pair", [P, 2, NT, 8], F32, c)
                slot = sb("slot", [P, 2, NT], F32, c)
                slot_tile = sb("slot_tile", [P, 2, NT], F32, c)
                slot_row = sb("slot_row", [P, 2, NT], F32, c)
                ramp = sb("ramp", [P, P], F32, c)
                hot_row = sb("hot_row", [P, 2, P], F16, c)
                hot_tile = sb("hot_tile", [P, 2, ST + 1], F16, c)
                chain, ramps, sel_ok, ranked, hot_ok, hot_used, placed = (sem(f"route_{n}") for n in
                    "chain ramps sel_ok ranked hot_ok hot_used placed".split())
                gate_in, biases_in, gate_ok, which_ok, logits_ok, logit_chain, neg_ok, where_ok, probs_ok, best_ok, exp_ok = (
                    sem(f"route_{n}") for n in
                    "gate_in biases_in gate_ok which_ok logits_ok logit_chain neg_ok where_ok probs_ok best_ok exp_ok".split())
                rows_zero, b_hi, b_lo, picks = (sem(f"route_{n}") for n in "rows_zero b_hi b_lo picks".split())

                def w_set(at):
                    return (BIG[:, at:at + 8192].rearrange("p (k h f) -> p k h f", k=8, h=2),
                            BIG[:, at + 8192:at + 16384].rearrange("p (k h d) -> p k h d", k=4, h=2))

                W = [w_set(0), w_set(16384)]
                stage = BIG[:, 50176:58368].bitcast(F32).rearrange("p (r n) -> p r n", r=4)
                g_row = BIG[:, 40960:43008]
                xT = BIG[:, 43008:45056].rearrange("p (h k n) -> p h k n", h=2, k=KD)
                h32 = BIG[:, 45056:46080].bitcast(F32)
                hid = BIG[:, 46080:47104].rearrange("p (h f) -> p h f", h=2)
                hT = BIG[:, 47104:48128].rearrange("p (h k n) -> p h k n", h=2, k=4)
                y32 = BIG[:, 48128:50176].bitcast(F32)
                tile_nodes = sb("tile_nodes", [P, 1], U32, c)
                x_ps = c.enter_context(nc.psum_tensor("x_ps", [P, 2, 2 * HALF], F16))
                h_ps = c.enter_context(nc.psum_tensor("h_ps", [P, HALF], F32))
                t_ps = c.enter_context(nc.psum_tensor("t_ps", [P, 2, 2 * HALF], F16))
                y_ps = c.enter_context(nc.psum_tensor("y_ps", [P, 2, HALF], F32))
                logit_ps = c.enter_context(nc.psum_tensor("logit_ps", [P, HALF], F32))
                rank_ps, node_ps = y_ps[:, 0, :], y_ps[:, 1, :]
                w_in = [sem(f"moe_w_in{r}") for r in range(4)]
                w_hi, w_lo = sem("moe_w_hi"), sem("moe_w_lo")
                nodes_ok, nodes_seen, rows_in, x_turned, x_hi, x_lo = (sem(f"moe_{n}") for n in "nodes_ok nodes_seen rows_in x_turned x_hi x_lo".split())
                h_ok, gelu_ok, h_hi, h_lo, h_turned, hT_hi, hT_lo = (sem(f"moe_{n}") for n in "h_ok gelu_ok h_hi h_lo h_turned hT_hi hT_lo".split())
                y_ok, y_left, y_right, stored = (sem(f"moe_{n}") for n in "y_ok y_left y_right stored".split())

                def sweep(eng, expert):
                    def one_expert(e, s):
                        if isinstance(e, int):
                            a, b = bounds_i[0:1, e:e + 1], bounds_i[0:1, e + 1:e + 2]
                        else:
                            a, b = bounds_i[0:1, bass.ds(e, 1)], bounds_i[0:1, bass.ds(e + 1, 1)]
                        first = 0 if isinstance(e, int) and e == 0 else eng.value_load(a, min_val=1, max_val=ST - 1)
                        expert(e, s, first, eng.value_load(b, min_val=1, max_val=ST))

                    one_expert(0, 0)
                    with eng.Fori(0, 3) as g:
                        one_expert(2 * g + 1, 1)
                        one_expert(2 * g + 2, 0)
                    one_expert(7, 1)

                with nc.Block() as block:
                    def place(i, h, s):
                        w1s, w2s = W[s]
                        if i < 4:
                            return w1s[:, 2 * i:2 * i + 2, h, :], stage[:, i, :].rearrange("p (k f) -> p k f", k=2)
                        return w2s[:, i - 4, h, :], stage[:, i - 4, :]

                    @block.sync
                    def _(sp):
                        sp.dma_start(gate32[:, :, :], gate.rearrange("(k p) e -> p k e", p=P)).then_inc(gate_in, 16)
                        sp.dma_start(b1_32[:, :], b1).then_inc(biases_in, 16)
                        sp.dma_start(b2_32[:, :], b2).then_inc(biases_in, 16)

                        def load(e, some):
                            for i in some:
                                sp.wait_ge(w_lo, 8 * e + i + 1)
                                if i < 4:
                                    sp.dma_start(stage[:, i, :].rearrange("p (k f) -> p k f", k=2),
                                                 w1[bass.ds(e * D + i * 2 * P, 2 * P), :].rearrange("(k p) f -> p k f", p=P)).then_inc(w_in[i], 16)
                                else:
                                    sp.dma_start(stage[:, i - 4, :], w2[bass.ds(e * HALF + (i - 4) * P, P), :]).then_inc(w_in[i - 4], 16)

                        def store(t):
                            sp.wait_ge(y_left, t + 2)
                            sp.wait_ge(y_right, t + 2)
                            sp.dma_start(results[bass.ds(t * P, P), :], y32).then_inc(stored, 16)

                        def expert(e, s, first, end):
                            last = isinstance(e, int) and e == 7
                            if not last:
                                load(e + 1, range(4, 8))
                            if not (isinstance(e, int) and e == 0):
                                store(first - 1)
                            if isinstance(e, int) and e == 0:
                                load(2, range(4))
                            elif not last:
                                if s == 1:
                                    load(e + 2, range(4))
                                else:
                                    with sp.If(e < 6):
                                        later = nc.s_assert_within(e + 2, 4, 7, skip_runtime_bounds_check_because="e < 6")
                                        load(later, range(4))
                            with sp.If(first + 1 < end):
                                with sp.Fori(first + 1, end) as t:
                                    store(t - 1)

                        load(0, range(8))
                        load(1, range(4))
                        sp.wait_ge(placed, 1)
                        sweep(sp, expert)
                        total = sp.value_load(bounds_i[0:1, 8:9], min_val=8, max_val=ST)
                        store(total - 1)

                    @block.gpsimd
                    def _(pool):
                        pool.iota(which[:, :], [[1, 8]], base=0, channel_multiplier=0, allow_small_or_imprecise_dtypes=True).then_inc(which_ok, 1)
                        pool.iota(node[:, :], [[P, NT]], base=0, channel_multiplier=1, allow_small_or_imprecise_dtypes=True).then_inc(ramps, 1)
                        pool.iota(ramp[:, :], [[1, P]], base=0, channel_multiplier=0, allow_small_or_imprecise_dtypes=True).then_inc(ramps, 1)
                        pool.memset(before[:, :], 1.0).then_inc(ramps, 1)
                        pool.memset(of_expert[:, :, :], 0.0).then_inc(picks, 1)
                        for at in (0, 32):
                            pool.wait_ge(picks, 1 + at // 32)
                            pool.affine_select(out=of_expert[:, :, :], in_=of_expert[:, :, :], compare_op=ALU.not_equal, fill=1.0,
                                               base=-at, pattern=[[-1, 8], [0, P]], channel_multiplier=1).then_inc(picks, 1)
                        pool.wait_ge(ramps, 3)
                        pool.affine_select(out=before[:, :], in_=before[:, :], compare_op=ALU.is_ge, fill=0.0,
                                           base=-1, pattern=[[1, P]], channel_multiplier=-1).then_inc(ramps, 1)

                        pool.wait_ge(placed, 1)
                        total = pool.value_load(bounds_i[0:1, 8:9], min_val=8, max_val=ST)
                        with pool.Fori(0, total + 1) as t:
                            pool.wait_ge(x_turned, t + 1)
                            pool.tensor_copy(tile_nodes[:, :], node_i[:, bass.ds(t, 1)]).then_inc(nodes_ok, 1)
                            pool.wait_ge(nodes_ok, t + 1)
                            pool.sem_inc(nodes_seen, 1)
                            pool.indirect_dma_start(g_row, None, rows[:, :], bass.IndirectOffsetOnAxis(ap=tile_nodes[:, :], axis=0)).then_inc(rows_in, 16)
                        pool.wait_ge(stored, 16 * total + 16)

                    @block.scalar
                    def _(act):
                        def split(e, s, some):
                            for i in some:
                                act.wait_ge(w_in[i % 4], 32 * e + (16 if i < 4 else 32))
                                part, src = place(i, 0, s)
                                act.activation(part, src, ACT.Copy, scale=WS).then_inc(w_hi, 1)

                        def turned(t):
                            act.wait_ge(x_turned, t + 2)
                            act.activation(xT[:, 0, :, :].rearrange("p k n -> p (k n)"), x_ps[:, 0, :], ACT.Copy).then_inc(x_hi, 1)

                        def hidden(t):
                            act.wait_ge(h_ok, t + 1)
                            act.wait_ge(h_lo, t + 1)
                            act.activation(h32, h_ps[:, :], ACT.Gelu_apprx_tanh, scale=1 / (AS * WS)).then_inc(gelu_ok, 1)
                            act.wait_ge(gelu_ok, t + 2)
                            act.wait_ge(h_turned, t + 1)
                            act.activation(hid[:, 0, :], h32, ACT.Copy, scale=AS).then_inc(h_hi, 1)

                        def leave(t):
                            act.wait_ge(y_ok, t + 1)
                            act.wait_ge(stored, 16 * t + 16)
                            act.activation(y32[:, 0:HALF], y_ps[:, 0, :], ACT.Copy).then_inc(y_left, 1)

                        def hidden_turned(t):
                            act.wait_ge(h_turned, t + 2)
                            act.activation(hT[:, 0, :, :].rearrange("p k n -> p (k n)"), t_ps[:, 0, 0:HALF], ACT.Copy).then_inc(hT_hi, 1)

                        def expert(e, s, first, end):
                            ahead = not (isinstance(e, int) and e == 7)
                            hidden(first)
                            turned(first + 1)
                            if ahead:
                                split(e + 1, 1 - s, range(4))
                            if not (isinstance(e, int) and e == 0):
                                leave(first - 1)
                            hidden_turned(first)
                            if ahead:
                                split(e + 1, 1 - s, range(4, 8))
                            with act.If(first + 1 < end):
                                with act.Fori(first + 1, end) as t:
                                    hidden(t)
                                    turned(t + 1)
                                    leave(t - 1)
                                    hidden_turned(t)

                        act.wait_ge(gate_in, 16)
                        act.activation(gate16[:, :, 0, :], gate32[:, :, :], ACT.Copy, scale=WS).then_inc(gate_ok, 1)
                        split(0, 0, range(4))
                        act.wait_ge(neg_ok, 1)
                        for j in range(NT):
                            act.activation(exps[:, j, :], logit[:, j, :], ACT.Exp, bias=neg[:, j:j + 1], accum_out=exp_sum[:, j:j + 1]).then_inc(exp_ok, 1)
                        act.wait_ge(biases_in, 32)
                        act.wait_ge(rows_zero, 2)
                        act.activation(b1_rows[0:8, :], b1_32[:, :], ACT.Copy, scale=AS * WS).then_inc(b_hi, 1)
                        act.activation(b2_rows[0:8, :], b2_32[:, :], ACT.Copy, scale=AS * WS).then_inc(b_hi, 1)
                        turned(0)
                        split(0, 0, range(4, 8))
                        act.wait_ge(placed, 1)
                        sweep(act, expert)
                        total = act.value_load(bounds_i[0:1, 8:9], min_val=8, max_val=ST)
                        leave(total - 1)

                    @block.tensor
                    def _(pe):
                        pe.wait_ge(gate_ok, 2)
                        for j in range(NT):
                            o = logit_ps[:, 16 * j:16 * j + 16]
                            for k in range(KD):
                                pe.matmul(o, FEAT[:, 8 + k, 0, j * P:(j + 1) * P], gate16[:, k, :, :].rearrange("p a e -> p (a e)"),
                                          start=(k == 0), stop=False)
                                mm = pe.matmul(o[:, 0:8], FEAT[:, 8 + k, 1, j * P:(j + 1) * P], gate16[:, k, 0, :], start=False, stop=(k == KD - 1))
                            mm.then_inc(logits_ok, 1)
                        pe.wait_ge(ramps, 4)
                        pe.wait_ge(sel_ok, 1)
                        pe.matmul(rank_ps[:, 0:8 * NT], before[:, :], sel.rearrange("p j e -> p (j e)"), start=True, stop=True)
                        pe.matmul(rank_ps[:, 8 * NT:16 * NT], ones32[:, :], sel.rearrange("p j e -> p (j e)"), start=True, stop=True).then_inc(ranked, 1)
                        for i in range(2 * NT):
                            pe.wait_ge(hot_ok, i + 1)
                            pe.matmul(node_ps[:, 0:ST + 1], hot_row[:, i % 2, :], hot_tile[:, i % 2, :], start=(i == 0), stop=(i == 2 * NT - 1)).then_inc(hot_used, 1)

                        def turn_rows(t):
                            pe.wait_ge(rows_in, 16 * t + 16)
                            for h, free in ((0, x_hi), (1, x_lo)):
                                pe.wait_ge(free, t + 1)
                                for k in range(KD):
                                    mm = pe.transpose(x_ps[:, h, k * P:(k + 1) * P], g_row[:, h * D + k * P:h * D + (k + 1) * P], ident[:, :])
                            mm.then_inc(x_turned, 1)

                        def chosen_rows(e):
                            return of_expert[:, e, :] if isinstance(e, int) else of_expert[:, bass.ds(e, 1), :]

                        def first_products(t, e, s):
                            w1s, w2s = W[s]
                            pe.wait_ge(gelu_ok, t + 1)
                            pe.wait_ge(x_hi, t + 2)
                            pe.wait_ge(x_lo, t + 2)
                            pe.matmul(h_ps[:, :], chosen_rows(e), b1_rows[:, :], start=True, stop=False)
                            for k in range(KD):
                                for a, b in ((0, 0), (0, 1), (1, 0)):
                                    mm = pe.matmul(h_ps[:, :], xT[:, a, k, :], w1s[:, k, b, :], start=False, stop=(k == KD - 1 and a == 1))
                            mm.then_inc(h_ok, 1)

                        def second_products(t, e, s):
                            w1s, w2s = W[s]
                            for ok in (hT_hi, hT_lo):
                                pe.wait_ge(ok, t + 2)
                            for free in (y_left, y_right):
                                pe.wait_ge(free, t + 1)
                            for h in range(2):
                                pe.matmul(y_ps[:, h, :], chosen_rows(e), b2_rows[:, h * HALF:(h + 1) * HALF], start=True, stop=False)
                            for k in range(4):
                                for a, b in ((0, 0), (0, 1), (1, 0)):
                                    for h in range(2):
                                        mm = pe.matmul(y_ps[:, h, :], hT[:, a, k, :], w2s[:, k, b, h * HALF:(h + 1) * HALF],
                                                       start=False, stop=(k == 3 and a == 1))
                            mm.then_inc(y_ok, 1)

                        def turn_hidden_rows(t):
                            pe.wait_ge(h_lo, t + 2)
                            for h, free in ((0, hT_hi), (1, hT_lo)):
                                pe.wait_ge(free, t + 1)
                                for k in range(4):
                                    mm = pe.transpose(t_ps[:, h, k * P:(k + 1) * P], hid[:, h, k * P:(k + 1) * P], ident[:, :])
                            mm.then_inc(h_turned, 1)

                        def expert(e, s, first, end):
                            pe.wait_ge(w_lo, 8 * e + 4 + 4)
                            first_products(first, e, s)
                            turn_rows(first + 1)
                            if not (isinstance(e, int) and e == 0):
                                second_products(first - 1, e - 1, 1 - s)
                            pe.wait_ge(w_lo, 8 * e + 8 + 4)
                            turn_hidden_rows(first)
                            with pe.If(first + 1 < end):
                                with pe.Fori(first + 1, end) as t:
                                    first_products(t, e, s)
                                    turn_rows(t + 1)
                                    second_products(t - 1, e, s)
                                    turn_hidden_rows(t)

                        turn_rows(0)
                        pe.wait_ge(placed, 1)
                        sweep(pe, expert)
                        total = pe.value_load(bounds_i[0:1, 8:9], min_val=8, max_val=ST)
                        second_products(total - 1, 7, 1)

                    @block.vector
                    def _(dve):
                        dve.sem_inc(w_lo, 4)
                        for free in (x_turned, gelu_ok, h_lo, h_turned, x_hi, x_lo, hT_hi, hT_lo, y_left, y_right):
                            dve.sem_inc(free, 1)
                        dve.sem_inc(stored, 16)

                        def split(e, s, some):
                            for i in some:
                                dve.wait_ge(w_hi, 8 * e + i + 1)
                                hi_, src = place(i, 0, s)
                                lo_, src = place(i, 1, s)
                                dve.scalar_tensor_tensor(lo_, src, WS, hi_, ALU.mult, ALU.subtract).then_inc(w_lo, 1)

                        def turned(t):
                            dve.wait_ge(x_turned, t + 2)
                            dve.tensor_copy(xT[:, 1, :, :].rearrange("p k n -> p (k n)"), x_ps[:, 1, :]).then_inc(x_lo, 1)

                        def hidden(t):
                            dve.wait_ge(h_hi, t + 1)
                            dve.scalar_tensor_tensor(hid[:, 1, :], h32, AS, hid[:, 0, :], ALU.mult, ALU.subtract).then_inc(h_lo, 1)

                        def leave(t):
                            dve.wait_ge(y_ok, t + 1)
                            dve.wait_ge(stored, 16 * t + 16)
                            dve.tensor_copy(y32[:, HALF:D], y_ps[:, 1, :]).then_inc(y_right, 1)

                        def hidden_turned(t):
                            dve.wait_ge(h_turned, t + 2)
                            dve.tensor_copy(hT[:, 1, :, :].rearrange("p k n -> p (k n)"), t_ps[:, 1, 0:HALF]).then_inc(hT_lo, 1)

                        def expert(e, s, first, end):
                            ahead = not (isinstance(e, int) and e == 7)
                            hidden(first)
                            turned(first + 1)
                            if ahead:
                                split(e + 1, 1 - s, range(4))
                            if not (isinstance(e, int) and e == 0):
                                leave(first - 1)
                            hidden_turned(first)
                            if ahead:
                                split(e + 1, 1 - s, range(4, 8))
                            with dve.If(first + 1 < end):
                                with dve.Fori(first + 1, end) as t:
                                    hidden(t)
                                    turned(t + 1)
                                    leave(t - 1)
                                    hidden_turned(t)

                        dve.memset(b1_rows[:, :], 0.0).then_inc(rows_zero, 1)
                        dve.memset(b2_rows[:, :], 0.0).then_inc(rows_zero, 1)
                        dve.wait_ge(gate_ok, 1)
                        dve.scalar_tensor_tensor(gate16[:, :, 1, :], gate32[:, :, :], WS, gate16[:, :, 0, :], ALU.mult, ALU.subtract).then_inc(gate_ok, 1)
                        dve.wait_ge(logits_ok, NT)
                        dve.tensor_scalar(both[:, :, :, :].rearrange("p j a e -> p (j a e)"), logit_ps[:, 0:16 * NT], 1 / (AS * WS), None, ALU.mult).then_inc(logit_chain, 1)
                        dve.wait_ge(logit_chain, 1)
                        dve.tensor_tensor(logit[:, :, :], both[:, :, 0, :], both[:, :, 1, :], ALU.add).then_inc(logit_chain, 1)
                        dve.wait_ge(logit_chain, 2)
                        for j in range(NT):
                            dve.max(best[:, j, :], logit[:, j, :]).then_inc(logit_chain, 1)
                        dve.wait_ge(logit_chain, NT + 2)
                        dve.tensor_scalar(neg[:, :], best[:, :, 0], -1.0, None, ALU.mult).then_inc(neg_ok, 1)
                        for j in range(NT):
                            dve.max_index(where[:, j, :], best[:, j, :], logit[:, j, :]).then_inc(where_ok, 1)
                        dve.wait_ge(where_ok, NT)
                        dve.tensor_copy(where_f[:, :, :], where[:, :, :]).then_inc(where_ok, 1)
                        dve.wait_ge(where_ok, NT + 1)
                        dve.wait_ge(which_ok, 1)
                        dve.wait_ge(exp_ok, NT)
                        for i in range(2):
                            dve.tensor_tensor(both[:, :, i, :], which[:, :].unsqueeze(1).to_broadcast([P, NT, 8]),
                                              where_f[:, :, i:i + 1].to_broadcast([P, NT, 8]), ALU.is_equal).then_inc(best_ok, 1)
                        dve.reciprocal(exp_sum[:, :], exp_sum[:, :]).then_inc(best_ok, 1)
                        dve.wait_ge(best_ok, 3)
                        dve.tensor_tensor(logit[:, :, :], both[:, :, 0, :], both[:, :, 1, :], ALU.add).then_inc(best_ok, 1)
                        dve.tensor_tensor(exps[:, :, :], exps[:, :, :], exp_sum[:, :].unsqueeze(2).to_broadcast([P, NT, 8]), ALU.mult).then_inc(best_ok, 1)
                        dve.wait_ge(best_ok, 5)
                        dve.tensor_tensor(chosen[:, :, :], exps[:, :, :], logit[:, :, :], ALU.mult).then_inc(probs_ok, 1)
                        dve.wait_ge(ramps, 4)
                        dve.tensor_scalar(live[:, :], node[:, :], float(NODES), None, ALU.is_lt).then_inc(chain, 1)
                        dve.wait_ge(chain, 1)
                        dve.tensor_tensor(node[:, :], node[:, :], live[:, :], ALU.mult).then_inc(chain, 1)
                        dve.tensor_tensor(sel[:, :, :], logit[:, :, :], live[:, :].unsqueeze(2).to_broadcast([P, NT, 8]), ALU.mult).then_inc(sel_ok, 1)
                        dve.wait_ge(ranked, 1)
                        dve.tensor_copy(per_tile.rearrange("p j e -> p (j e)"), rank_ps[:, 8 * NT:16 * NT]).then_inc(chain, 1)
                        dve.wait_ge(chain, 3)
                        dve.tensor_reduce(tiles[:, :], per_tile.rearrange("p j e -> p e j"), AX_X, ALU.add).then_inc(chain, 1)
                        dve.wait_ge(chain, 4)
                        dve.tensor_scalar(tiles[:, :], tiles[:, :], 1.0 / P, 0.498, ALU.mult, ALU.add).then_inc(chain, 1)
                        dve.wait_ge(chain, 5)
                        dve.tensor_scalar(tiles[:, :], tiles[:, :], MAGIC, None, ALU.add).then_inc(chain, 1)
                        dve.wait_ge(chain, 6)
                        dve.tensor_scalar(tiles[:, :], tiles[:, :], MAGIC, 1.0, ALU.subtract, ALU.max).then_inc(chain, 1)
                        dve.memset(start[:, :], 0.0).then_inc(chain, 1)
                        for e in range(8):
                            dve.wait_ge(chain, 8 + e)
                            dve.tensor_tensor(start[:, e + 1:e + 2], start[:, e:e + 1], tiles[:, e:e + 1], ALU.add).then_inc(chain, 1)
                        dve.wait_ge(chain, 16)
                        dve.tensor_copy(bounds_i[:, :], start[:, :]).then_inc(chain, 1)
                        dve.tensor_scalar(offset[:, 0, :], start[:, 0:8], float(P), None, ALU.mult).then_inc(chain, 1)
                        for j in range(1, NT):
                            dve.wait_ge(chain, 17 + j)
                            dve.tensor_tensor(offset[:, j, :], offset[:, j - 1, :], per_tile[:, j - 1, :], ALU.add).then_inc(chain, 1)
                        dve.wait_ge(chain, 17 + NT)
                        dve.tensor_tensor(offset.rearrange("p j e -> p (j e)"), offset.rearrange("p j e -> p (j e)"), rank_ps[:, 0:8 * NT], ALU.add).then_inc(chain, 1)
                        dve.wait_ge(chain, 18 + NT)
                        for i in range(2):
                            dve.tensor_tensor(pair[:, i, :, :], both[:, :, i, :], offset[:, :, :], ALU.mult).then_inc(chain, 1)
                        dve.wait_ge(chain, 20 + NT)
                        dve.tensor_reduce(slot[:, :, :], pair[:, :, :, :], AX_X, ALU.add).then_inc(chain, 1)
                        dve.wait_ge(chain, 21 + NT)
                        for i in range(2):
                            dve.tensor_tensor(pair[:, i, :, :], both[:, :, i, :], chosen[:, :, :], ALU.mult).then_inc(chain, 1)
                        dve.wait_ge(chain, 23 + NT)
                        dve.tensor_reduce(weight[:, :, :], pair[:, :, :, :], AX_X, ALU.add).then_inc(chain, 1)
                        dve.wait_ge(chain, 24 + NT)
                        dve.tensor_scalar(weight[:, :, :], weight[:, :, :], 1 / (AS * WS), None, ALU.mult).then_inc(chain, 1)
                        dve.tensor_scalar(slot_tile[:, :, :], slot[:, :, :], 1.0 / P, -0.498, ALU.mult, ALU.add).then_inc(chain, 1)
                        dve.wait_ge(chain, 26 + NT)
                        dve.tensor_scalar(slot_tile[:, :, :], slot_tile[:, :, :], MAGIC, None, ALU.add).then_inc(chain, 1)
                        dve.wait_ge(chain, 27 + NT)
                        dve.tensor_scalar(slot_tile[:, :, :], slot_tile[:, :, :], MAGIC, None, ALU.subtract).then_inc(chain, 1)
                        dve.wait_ge(chain, 28 + NT)
                        dve.scalar_tensor_tensor(slot_row[:, :, :], slot_tile[:, :, :], -float(P), slot[:, :, :], ALU.mult, ALU.add).then_inc(chain, 1)
                        dve.wait_ge(chain, 29 + NT)
                        for i in range(2):
                            dve.tensor_tensor(slot[:, i, :], slot[:, i, :], live[:, :], ALU.mult).then_inc(chain, 1)
                        dve.wait_ge(chain, 31 + NT)
                        dve.tensor_copy(slot_i[:, :, :], slot[:, :, :]).then_inc(chain, 1)
                        for i in range(2 * NT):
                            c_, j = i // NT, i % NT
                            if i >= 2:
                                dve.wait_ge(hot_used, i - 1)
                            dve.tensor_scalar(hot_row[:, i % 2, :], ramp[:, :], slot_row[:, c_, j:j + 1], None, ALU.is_equal)
                            dve.tensor_scalar(hot_tile[:, i % 2, :], ramp[:, 0:ST + 1], slot_tile[:, c_, j:j + 1], node[:, j:j + 1], ALU.is_equal, ALU.mult).then_inc(hot_ok, 1)
                        dve.wait_ge(hot_used, 2 * NT)
                        dve.tensor_copy(node_i[:, :], node_ps[:, 0:ST + 1]).then_inc(placed, 1)
                        split(0, 0, range(4))
                        for n, (part, src) in enumerate(((b1_rows, b1_32), (b2_rows, b2_32))):
                            dve.wait_ge(b_hi, n + 1)
                            dve.scalar_tensor_tensor(part[32:40, :], src[:, :], AS * WS, part[0:8, :], ALU.mult, ALU.subtract).then_inc(b_lo, 1)
                        turned(0)
                        split(0, 0, range(4, 8))
                        dve.wait_ge(placed, 1)
                        sweep(dve, expert)
                        total = dve.value_load(bounds_i[0:1, 8:9], min_val=8, max_val=ST)
                        leave(total - 1)

        def ternary_ffn():
            with ExitStack() as c:
                n32 = BIG[:, 20480:24576].bitcast(F32).rearrange("p (s d) -> p s d", s=2)
                wt = B1.rearrange("p j n -> p (j n)")[:, 0:12288].rearrange("p (m n) -> p m n", m=3)
                gk = sb("gk", [P, 2, HALF], F32, c)
                gq = sb("gq", [P, 2, HALF], F16, c)
                gT = sb("gT", [P, 2, 4, P], F16, c)
                k_gate, k_up, vmax, vscale, k_down = (sb(f"ffn_{n}", [P, NT], F32, c) for n in "k_gate k_up vmax vscale k_down".split())
                q_ps = c.enter_context(nc.psum_tensor("q_ps", [P, 2, 2 * HALF], F16))
                gate_ps = c.enter_context(nc.psum_tensor("gate_ps", [P, HALF], F32))
                up_ps = c.enter_context(nc.psum_tensor("up_ps", [P, HALF], F32))
                t_ps = c.enter_context(nc.psum_tensor("tq_ps", [P, 2, 2 * HALF], F16))
                down_ps = c.enter_context(nc.psum_tensor("down_ps", [P, 2, HALF], F32))
                stats, moments, root, n32_ok, whole_chain, rounded, whole_ok, q_turned, q_out, k_ok = (
                    sem(f"ffn_{n}") for n in "stats moments root n32_ok whole_chain rounded whole_ok q_turned q_out k_ok".split())
                up_ok, gate_free, v_ok, v_chain, v_whole, v_turned, v_out, down_ok, x_ok, x_out = (
                    sem(f"ffn_{n}") for n in "up_ok gate_free v_ok v_chain v_whole v_turned v_out down_ok x_ok x_out".split())
                with nc.Block() as block:
                    @block.sync
                    def _(sp):
                        for j in range(NT):
                            r = P if j < NT - 1 else LAST
                            sp.wait_ge(x_ok, j + 1)
                            sp.dma_start(out[j * P:j * P + r, :], X[0:r, j, :]).then_inc(x_out, 16)
                        sp.wait_ge(x_out, 16 * NT)

                    @block.gpsimd
                    def _(pool):
                        root_of(pool, EARLY, 0, moments, root, 1.0)
                        root_of(pool, EARLY + 1, 1, moments, root, 1.0)
                        for j in range(NT):
                            if j >= EARLY:
                                pool.wait_ge(rounded, j - EARLY + 1)
                            pool.tensor_scalar(k_gate[:, j:j + 1], qmax[:, j:j + 1], wmean[:, 0:1], 0.0, ALU.mult, ALU.add).then_inc(k_ok, 1)
                            pool.tensor_scalar(k_up[:, j:j + 1], qmax[:, j:j + 1], wmean[:, 1:2], 0.0, ALU.mult, ALU.add).then_inc(k_ok, 1)
                            if EARLY <= j < NT - 2:
                                root_of(pool, j + 2, j + 2 - EARLY, moments, root, 1.0)

                    @block.scalar
                    def _(act):
                        def norm(j):
                            n = j - EARLY
                            act.wait_ge(root, 5 * n + 5)
                            if n >= 2:
                                act.wait_ge(whole_ok, n - 1)
                            act.activation(n32[:, j % 2, :], X[:, j, :], ACT.Identity, bias=shift[:, j:j + 1],
                                           scale=rstd[:, j:j + 1]).then_inc(n32_ok, 1)

                        for j in range(NT + 3):
                            if EARLY <= j + 1 < NT:
                                norm(j + 1)
                            if 0 <= j - 2 < NT:
                                i = j - 2
                                act.wait_ge(up_ok, i + 1)
                                act.wait_ge(k_ok, 2 * i + 2)
                                if i >= 2:
                                    act.wait_ge(v_whole, i - 1)
                                act.activation(gk[:, i % 2, :], gate_ps[:, :], ACT.Silu, scale=k_gate[:, i:i + 1]).then_inc(gate_free, 1)
                            if j >= 3:
                                i = j - 3
                                act.wait_ge(v_turned, i + 1)
                                act.activation(gT[:, i % 2, :, :], t_ps[:, i % 2, 0:HALF].rearrange("p (k n) -> p k n", k=4), ACT.Copy).then_inc(v_out, 1)
                            if j < NT:
                                act.wait_ge(q_turned, j + 1)
                                act.activation(FEAT[:, 0:8, 0, j * P:(j + 1) * P], q_ps[:, j % 2, :].rearrange("p (k n) -> p k n", k=8), ACT.Copy).then_inc(q_out, 1)

                    @block.tensor
                    def _(pe):
                        for j in range(NT + 3):
                            if 0 <= j - 2 < NT:
                                i = j - 2
                                pe.wait_ge(q_out, i + 1)
                                if i:
                                    pe.wait_ge(gate_free, i)
                                    pe.wait_ge(v_ok, i)
                                for m, o in ((0, gate_ps), (1, up_ps)):
                                    for k in range(KD):
                                        mm = pe.matmul(o[:, :], FEAT[:, k, 0, i * P:(i + 1) * P], wt[:, m, k * HALF:(k + 1) * HALF],
                                                       start=(k == 0), stop=(k == KD - 1))
                                mm.then_inc(up_ok, 1)
                            if j >= 3:
                                i = j - 3
                                pe.wait_ge(v_whole, i + 1)
                                for k in range(4):
                                    mm = pe.transpose(t_ps[:, i % 2, k * P:(k + 1) * P], gq[:, i % 2, k * P:(k + 1) * P], ident[:, :])
                                mm.then_inc(v_turned, 1)
                                pe.wait_ge(v_out, i + 1)
                                if i:
                                    pe.wait_ge(x_ok, i)
                                for k in range(4):
                                    for h in range(2):
                                        mm = pe.matmul(down_ps[:, h, :], gT[:, i % 2, k, :], wt[:, 2, k * D + h * HALF:k * D + (h + 1) * HALF],
                                                       start=(k == 0), stop=(k == 3))
                                mm.then_inc(down_ok, 1)
                            if j < NT:
                                if j >= EARLY:
                                    pe.wait_ge(whole_ok, j - EARLY + 1)
                                if j >= 2:
                                    pe.wait_ge(q_out, j - 1)
                                for k in range(KD):
                                    mm = pe.transpose(q_ps[:, j % 2, k * P:(k + 1) * P], (N[:, j, 0, :] if j >= EARLY else whole_early[:, j, :])[:, k * P:(k + 1) * P], ident[:, :])
                                mm.then_inc(q_turned, 1)

                    @block.vector
                    def _(dve):
                        def moment(j):
                            moments_of(dve, j, j - EARLY, stats, moments)

                        moment(EARLY)
                        moment(EARLY + 1)
                        for j in range(NT + 3):
                            if EARLY <= j < NT:
                                v = n32[:, j % 2, :]
                                dve.wait_ge(n32_ok, j - EARLY + 1)
                                scale_to_whole(dve, v, qmax[:, j:j + 1], qscale[:, j:j + 1], whole_chain, 3 * (j - EARLY), rounded)
                                dve.wait_ge(rounded, j - EARLY + 1)
                                dve.tensor_scalar(N[:, j, 0, :], v, MAGIC, 127.0, ALU.subtract, ALU.min).then_inc(whole_ok, 1)
                            if EARLY <= j < NT - 2:
                                moment(j + 2)
                            if 0 <= j - 2 < NT:
                                i = j - 2
                                v = gk[:, i % 2, :]
                                dve.wait_ge(gate_free, i + 1)
                                dve.wait_ge(k_ok, 2 * i + 2)
                                dve.scalar_tensor_tensor(v, up_ps[:, :], k_up[:, i:i + 1], v, ALU.mult, ALU.mult).then_inc(v_ok, 1)
                                dve.wait_ge(v_ok, i + 1)
                                scale_to_whole(dve, v, vmax[:, i:i + 1], vscale[:, i:i + 1], v_chain, 5 * i, v_chain)
                                dve.tensor_scalar(k_down[:, i:i + 1], vmax[:, i:i + 1], wmean[:, 2:3], None, ALU.mult).then_inc(v_chain, 1)
                                dve.wait_ge(v_chain, 5 * i + 5)
                                dve.tensor_scalar(gq[:, i % 2, :], v, MAGIC, 127.0, ALU.subtract, ALU.min).then_inc(v_whole, 1)
                            if j >= 3:
                                i = j - 3
                                dve.wait_ge(down_ok, i + 1)
                                dve.scalar_tensor_tensor(X[:, i, :], down_ps.rearrange("p h n -> p (h n)"), k_down[:, i:i + 1], X[:, i, :],
                                                         ALU.mult, ALU.add).then_inc(x_ok, 1)

        def scale_to_whole(dve, v, vmax, vscale, chain, n, done):
            dve.tensor_reduce(vmax, v, AX_X, ALU.max, apply_absolute_value=True).then_inc(chain, 1)
            dve.wait_ge(chain, n + 1)
            dve.tensor_scalar(vmax, vmax, 1e-5, 1 / 127.0, ALU.max, ALU.mult).then_inc(chain, 1)
            dve.wait_ge(chain, n + 2)
            dve.reciprocal(vscale, vmax).then_inc(chain, 1)
            dve.wait_ge(chain, n + 3)
            dve.tensor_scalar(v, v, vscale, MAGIC, ALU.mult, ALU.add).then_inc(done, 1)

        experts()
        end_phase()
        degree_row = sb("degree_row", [P, NP], F32)
        merge_and_normalise()
        end_phase()
        sage("s0", [s0, n0], c0, True)
        end_phase()
        sage("s1", [s1, n1], c1, False)
        end_phase()
        ternary_ffn()
        end_phase()


def kernel(**inputs):
    import numpy as np
    import concourse.bacc as bacc
    from concourse.bass_utils import run_bass_kernel_spmd as run

    nc = bacc.Bacc("TRN2", target_bir_lowering=False, num_devices=1)

    def chunks(e):
        padded = np.full(CHP * P, NOWHERE, e.dtype)
        padded[:EDGES] = e
        return padded.reshape(CHP, P).T

    laid = {
        "x": inputs["x"], "src": chunks(np.asarray(inputs["src"])), "dst": chunks(np.asarray(inputs["dst"])),
        "l0_w": np.asarray(inputs["L0_gnn_W"]).T, "l0_b": inputs["L0_gnn_b"],
        "gate": np.asarray(inputs["L0_ffn_gate_w"]).T,
        "w1": np.asarray(inputs["L0_ffn_w1"]).transpose(1, 2, 0).reshape(8 * D, HALF),
        "b1": inputs["L0_ffn_b1"],
        "w2": np.asarray(inputs["L0_ffn_w2"]).transpose(1, 2, 0).reshape(8 * HALF, D),
        "b2": inputs["L0_ffn_b2"],
        "s0": inputs["L1_gnn_W_self0"], "n0": inputs["L1_gnn_W_neigh0"], "c0": inputs["L1_gnn_b0"],
        "s1": inputs["L1_gnn_W_self1"], "n1": inputs["L1_gnn_W_neigh1"], "c1": inputs["L1_gnn_b1"],
        "wg": np.asarray(inputs["L1_ffn_w_gate"]).T, "wu": np.asarray(inputs["L1_ffn_w_up"]).T,
        "wd": np.asarray(inputs["L1_ffn_w_down"]).T,
    }
    laid = {k: np.ascontiguousarray(v) for k, v in laid.items()}
    aps = {k: nc.dram_tensor(k, v.shape, mybir.dt.from_np(v.dtype), kind="ExternalInput").ap() for k, v in laid.items()}
    out = nc.dram_tensor("out", (NODES, D), F32, kind="ExternalOutput").ap()
    gnn_ffn_kernel(nc, **aps, out=out)
    r = run(nc, [laid], core_ids=[0])
    return r.results[0]["out"]
```
